# Optimizing a Trainium2 kernel written in Bass

```python
import numpy as np
import jax
import jax.numpy as jnp

def _softmax(x, axis=-1):
    return jax.nn.softmax(x, axis=axis)

def _gelu(x):
    return jax.nn.gelu(x, approximate=True)

def _silu(x):
    return jax.nn.silu(x)

def _sigmoid(x):
    return jax.nn.sigmoid(x)

def _layernorm(x, axis=-1, eps=1e-05):
    m = jnp.mean(x, axis=axis, keepdims=True)
    v = jnp.var(x, axis=axis, keepdims=True)
    return (x - m) / jnp.sqrt(v + eps)

def _scatter_add(tgt, idx, src, axis=0):
    return tgt.at[idx].add(src)

def _segment_sum(src, seg, n):
    return jax.ops.segment_sum(src, seg, n)
kernel_name = 'mk_seq_preln_d2_jaxref_r8_4c46e1'

def setup_inputs(seed: int=0):
    np.random.seed(seed)
    _w = jnp.asarray

    def _L0_attn_setup():
        import jax, jax.numpy as jnp
        import numpy as np
        B, T, D = (4, 256, 128)
        H, Kd = (4, 32)
        Vd = 64
        KEY_DIM, VAL_DIM = (H * Kd, H * Vd)
        CONV = 4
        EPS = 1e-06
        LN_EPS = 1e-05

        def _layernorm(x, g, b):
            m = jnp.mean(x, -1, keepdims=True)
            v = jnp.mean((x - m) ** 2, -1, keepdims=True)
            return (x - m) * jax.lax.rsqrt(v + LN_EPS) * g + b

        def _rmsnorm(x, w):
            return x * jax.lax.rsqrt(jnp.mean(x * x, -1, keepdims=True) + EPS) * w

        def _l2norm(x):
            return x * jax.lax.rsqrt(jnp.sum(x * x, -1, keepdims=True) + EPS)

        def _causal_conv_silu(x, w):
            t = x.shape[1]
            xp = jnp.pad(x, ((0, 0), (CONV - 1, 0), (0, 0)))
            y = xp[:, 0:t, :] * w[:, 0]
            for i in range(1, CONV):
                y = y + xp[:, i:i + t, :] * w[:, i]
            return jax.nn.silu(y)

        def _gated_delta_rule(q, k, v, g, beta):
            qT = jnp.moveaxis(q, 1, 0)
            kT = jnp.moveaxis(k, 1, 0)
            vT = jnp.moveaxis(v, 1, 0)
            gT = jnp.moveaxis(g, 1, 0)
            bT = jnp.moveaxis(beta, 1, 0)
            S0 = jnp.zeros((q.shape[0], H, Kd, Vd), q.dtype)

            def step(S, inp):
                q_t, k_t, v_t, g_t, b_t = inp
                S = S * jnp.exp(g_t)[..., None, None]
                kv = jnp.einsum('bhk,bhkv->bhv', k_t, S)
                delta = (v_t - kv) * b_t[..., None]
                S = S + k_t[..., :, None] * delta[..., None, :]
                o = jnp.einsum('bhk,bhkv->bhv', q_t, S)
                return (S, o)
            _, o = jax.lax.scan(step, S0, (qT, kT, vT, gT, bT))
            return jnp.moveaxis(o, 0, 1)

        def _forward(x, ln1_g, ln1_b, ln2_g, ln2_b, rms_in_w, Wq, Wk, Wv, conv_q_w, conv_k_w, conv_v_w, Wa, dt_bias, A_log, Wb, Wg, o_norm_w, Wo, W2, b2):
            b, t, _ = x.shape
            h = _layernorm(x, ln1_g, ln1_b)
            h = _rmsnorm(h, rms_in_w)
            q = _causal_conv_silu(h @ Wq, conv_q_w).reshape(b, t, H, Kd)
            k = _causal_conv_silu(h @ Wk, conv_k_w).reshape(b, t, H, Kd)
            v = _causal_conv_silu(h @ Wv, conv_v_w).reshape(b, t, H, Vd)
            q = _l2norm(q) * Kd ** (-0.5)
            k = _l2norm(k)
            g = -jnp.exp(A_log) * jax.nn.softplus(h @ Wa + dt_bias)
            beta = jax.nn.sigmoid(h @ Wb)
            o = _gated_delta_rule(q, k, v, g, beta)
            gate = (h @ Wg).reshape(b, t, H, Vd)
            o = _rmsnorm(o, o_norm_w) * jax.nn.silu(gate)
            enc = o.reshape(b, t, VAL_DIM) @ Wo
            x = x + enc
            h2 = _layernorm(x, ln2_g, ln2_b)
            x_out = jax.nn.gelu(h2 @ W2 + b2, approximate=False) + x
            return x_out
        key = jax.random.key(seed)
        ks = jax.random.split(key, 16)
        r = lambda k, shp, s=0.02: jax.random.normal(k, shp, dtype=jnp.float32) * s
        return {'x': jax.random.normal(ks[0], (B, T, D), dtype=jnp.float32), 'ln1_g': jnp.ones((D,), jnp.float32), 'ln1_b': jnp.zeros((D,), jnp.float32), 'ln2_g': jnp.ones((D,), jnp.float32), 'ln2_b': jnp.zeros((D,), jnp.float32), 'rms_in_w': jnp.ones((D,), jnp.float32), 'Wq': r(ks[1], (D, KEY_DIM)), 'Wk': r(ks[2], (D, KEY_DIM)), 'Wv': r(ks[3], (D, VAL_DIM)), 'conv_q_w': r(ks[4], (KEY_DIM, CONV), 0.3), 'conv_k_w': r(ks[5], (KEY_DIM, CONV), 0.3), 'conv_v_w': r(ks[6], (VAL_DIM, CONV), 0.3), 'Wa': r(ks[7], (D, H)), 'dt_bias': r(ks[8], (H,), 0.5), 'A_log': jnp.log(jax.random.uniform(ks[9], (H,), minval=1.0, maxval=16.0)), 'Wb': r(ks[10], (D, H)), 'Wg': r(ks[11], (D, VAL_DIM)), 'o_norm_w': jnp.ones((Vd,), jnp.float32), 'Wo': r(ks[12], (VAL_DIM, D)), 'W2': r(ks[13], (D, D)), 'b2': jnp.zeros((D,), jnp.float32)}
    _L0_attn_in = _L0_attn_setup()

    def _L0_ffn_setup():
        import jax, jax.numpy as jnp
        import numpy as np
        B, L, D = (4, 256, 128)
        E, K, S = (8, 2, 2)
        F = 176
        SCALE = 1.0
        INIT = 0.02

        def _swiglu(x, wg, wu, wd):
            return jax.nn.silu(x @ wg) * (x @ wu) @ wd
        key = jax.random.key(seed)
        ks = jax.random.split(key, 8)
        return {'hidden_states': jax.random.normal(ks[0], (B, L, D), jnp.float32), 'gate_w': jax.random.normal(ks[1], (D, E), jnp.float32) * INIT, 'exp_gate': jax.random.normal(ks[2], (E, D, F), jnp.float32) * INIT, 'exp_up': jax.random.normal(ks[3], (E, D, F), jnp.float32) * INIT, 'exp_down': jax.random.normal(ks[4], (E, F, D), jnp.float32) * INIT, 'sh_gate': jax.random.normal(ks[5], (S, D, F), jnp.float32) * INIT, 'sh_up': jax.random.normal(ks[6], (S, D, F), jnp.float32) * INIT, 'sh_down': jax.random.normal(ks[7], (S, F, D), jnp.float32) * INIT}
    _L0_ffn_in = _L0_ffn_setup()

    def _L1_attn_setup():
        import jax, jax.numpy as jnp
        import numpy as np
        D_MODEL = 128
        N_HEADS = 16
        D_LATENT = 32
        HEAD_DIM = D_MODEL // N_HEADS

        def apply_rope(x):
            B, T, H, D = x.shape
            inv_freq = 1.0 / 10000.0 ** (jnp.arange(0, D, 2, dtype=jnp.float32) / D)
            t = jnp.arange(T, dtype=jnp.float32)
            freqs = t[:, None] * inv_freq[None, :]
            sin_f = jnp.sin(freqs)[None, :, None, :]
            cos_f = jnp.cos(freqs)[None, :, None, :]
            x1, x2 = jnp.split(x, 2, axis=-1)
            return jnp.concatenate([x1 * cos_f - x2 * sin_f, x1 * sin_f + x2 * cos_f], axis=-1)
        key = jax.random.key(seed)
        ks = jax.random.split(key, 10)
        B, T = (4, 512)
        s = lambda fan_in: 1.0 / np.sqrt(fan_in)
        return {'x': jax.random.normal(ks[0], (B, T, D_MODEL), dtype=jnp.float32), 'Wq': jax.random.normal(ks[1], (D_MODEL, D_MODEL), dtype=jnp.float32) * s(D_MODEL), 'bq': jnp.zeros((D_MODEL,), jnp.float32), 'Wdown': jax.random.normal(ks[2], (D_MODEL, D_LATENT), dtype=jnp.float32) * s(D_MODEL), 'bdown': jnp.zeros((D_LATENT,), jnp.float32), 'Wup': jax.random.normal(ks[3], (D_LATENT, 2 * D_MODEL), dtype=jnp.float32) * s(D_LATENT), 'bup': jnp.zeros((2 * D_MODEL,), jnp.float32), 'Wout': jax.random.normal(ks[4], (D_MODEL, D_MODEL), dtype=jnp.float32) * s(D_MODEL), 'bout': jnp.zeros((D_MODEL,), jnp.float32)}
    _L1_attn_in = _L1_attn_setup()

    def _L1_ffn_setup():
        import jax, jax.numpy as jnp
        import numpy as np
        E = 8
        C = 160
        D = 128
        H = 512
        B, S = (4, 256)
        key = jax.random.key(seed)
        ks = jax.random.split(key, 12)
        sc = 0.02
        return {'input': jax.random.normal(ks[0], (B, S, D), jnp.float32), 'router_w': jax.random.normal(ks[1], (D, E), jnp.float32) * sc, 'router_b': jnp.zeros((E,), jnp.float32), 'w1': jax.random.normal(ks[2], (E, D, H), jnp.float32) * sc, 'b1': jnp.zeros((E, H), jnp.float32), 'w2': jax.random.normal(ks[3], (E, H, D), jnp.float32) * sc, 'b2': jnp.zeros((E, D), jnp.float32), 'ow1': jax.random.normal(ks[4], (D, H), jnp.float32) * sc, 'ob1': jnp.zeros((H,), jnp.float32), 'ow2': jax.random.normal(ks[5], (H, D), jnp.float32) * sc, 'ob2': jnp.zeros((D,), jnp.float32)}
    _L1_ffn_in = _L1_ffn_setup()
    _d = {'L0_attn_x': _L0_attn_in['x'], 'L0_attn_ln1_g': _L0_attn_in['ln1_g'], 'L0_attn_ln1_b': _L0_attn_in['ln1_b'], 'L0_attn_ln2_g': _L0_attn_in['ln2_g'], 'L0_attn_ln2_b': _L0_attn_in['ln2_b'], 'L0_attn_rms_in_w': _L0_attn_in['rms_in_w'], 'L0_attn_Wq': _L0_attn_in['Wq'], 'L0_attn_Wk': _L0_attn_in['Wk'], 'L0_attn_Wv': _L0_attn_in['Wv'], 'L0_attn_conv_q_w': _L0_attn_in['conv_q_w'], 'L0_attn_conv_k_w': _L0_attn_in['conv_k_w'], 'L0_attn_conv_v_w': _L0_attn_in['conv_v_w'], 'L0_attn_Wa': _L0_attn_in['Wa'], 'L0_attn_dt_bias': _L0_attn_in['dt_bias'], 'L0_attn_A_log': _L0_attn_in['A_log'], 'L0_attn_Wb': _L0_attn_in['Wb'], 'L0_attn_Wg': _L0_attn_in['Wg'], 'L0_attn_o_norm_w': _L0_attn_in['o_norm_w'], 'L0_attn_Wo': _L0_attn_in['Wo'], 'L0_attn_W2': _L0_attn_in['W2'], 'L0_attn_b2': _L0_attn_in['b2'], 'L0_ffn_gate_w': _L0_ffn_in['gate_w'], 'L0_ffn_exp_gate': _L0_ffn_in['exp_gate'], 'L0_ffn_exp_up': _L0_ffn_in['exp_up'], 'L0_ffn_exp_down': _L0_ffn_in['exp_down'], 'L0_ffn_sh_gate': _L0_ffn_in['sh_gate'], 'L0_ffn_sh_up': _L0_ffn_in['sh_up'], 'L0_ffn_sh_down': _L0_ffn_in['sh_down'], 'L1_attn_Wq': _L1_attn_in['Wq'], 'L1_attn_bq': _L1_attn_in['bq'], 'L1_attn_Wdown': _L1_attn_in['Wdown'], 'L1_attn_bdown': _L1_attn_in['bdown'], 'L1_attn_Wup': _L1_attn_in['Wup'], 'L1_attn_bup': _L1_attn_in['bup'], 'L1_attn_Wout': _L1_attn_in['Wout'], 'L1_attn_bout': _L1_attn_in['bout'], 'L1_ffn_router_w': _L1_ffn_in['router_w'], 'L1_ffn_router_b': _L1_ffn_in['router_b'], 'L1_ffn_w1': _L1_ffn_in['w1'], 'L1_ffn_b1': _L1_ffn_in['b1'], 'L1_ffn_w2': _L1_ffn_in['w2'], 'L1_ffn_b2': _L1_ffn_in['b2'], 'L1_ffn_ow1': _L1_ffn_in['ow1'], 'L1_ffn_ob1': _L1_ffn_in['ob1'], 'L1_ffn_ow2': _L1_ffn_in['ow2'], 'L1_ffn_ob2': _L1_ffn_in['ob2']}
    _x0 = _d['L0_attn_x']
    _d['L0_attn_x'] = jax.random.normal(jax.random.fold_in(jax.random.key(seed), 1), (4, 1024, 128), dtype=_x0.dtype)
    del _x0
    return _d

def reference(L0_attn_x, L0_attn_ln1_g, L0_attn_ln1_b, L0_attn_ln2_g, L0_attn_ln2_b, L0_attn_rms_in_w, L0_attn_Wq, L0_attn_Wk, L0_attn_Wv, L0_attn_conv_q_w, L0_attn_conv_k_w, L0_attn_conv_v_w, L0_attn_Wa, L0_attn_dt_bias, L0_attn_A_log, L0_attn_Wb, L0_attn_Wg, L0_attn_o_norm_w, L0_attn_Wo, L0_attn_W2, L0_attn_b2, L0_ffn_gate_w, L0_ffn_exp_gate, L0_ffn_exp_up, L0_ffn_exp_down, L0_ffn_sh_gate, L0_ffn_sh_up, L0_ffn_sh_down, L1_attn_Wq, L1_attn_bq, L1_attn_Wdown, L1_attn_bdown, L1_attn_Wup, L1_attn_bup, L1_attn_Wout, L1_attn_bout, L1_ffn_router_w, L1_ffn_router_b, L1_ffn_w1, L1_ffn_b1, L1_ffn_w2, L1_ffn_b2, L1_ffn_ow1, L1_ffn_ob1, L1_ffn_ow2, L1_ffn_ob2):

    def _L0_attn_ref(x, ln1_g, ln1_b, ln2_g, ln2_b, rms_in_w, Wq, Wk, Wv, conv_q_w, conv_k_w, conv_v_w, Wa, dt_bias, A_log, Wb, Wg, o_norm_w, Wo, W2, b2):
        import jax, jax.numpy as jnp
        import numpy as np
        B, T, D = (4, 256, 128)
        H, Kd = (4, 32)
        Vd = 64
        KEY_DIM, VAL_DIM = (H * Kd, H * Vd)
        CONV = 4
        EPS = 1e-06
        LN_EPS = 1e-05

        def _layernorm(x, g, b):
            m = jnp.mean(x, -1, keepdims=True)
            v = jnp.mean((x - m) ** 2, -1, keepdims=True)
            return (x - m) * jax.lax.rsqrt(v + LN_EPS) * g + b

        def _rmsnorm(x, w):
            return x * jax.lax.rsqrt(jnp.mean(x * x, -1, keepdims=True) + EPS) * w

        def _l2norm(x):
            return x * jax.lax.rsqrt(jnp.sum(x * x, -1, keepdims=True) + EPS)

        def _causal_conv_silu(x, w):
            t = x.shape[1]
            xp = jnp.pad(x, ((0, 0), (CONV - 1, 0), (0, 0)))
            y = xp[:, 0:t, :] * w[:, 0]
            for i in range(1, CONV):
                y = y + xp[:, i:i + t, :] * w[:, i]
            return jax.nn.silu(y)

        def _gated_delta_rule(q, k, v, g, beta):
            qT = jnp.moveaxis(q, 1, 0)
            kT = jnp.moveaxis(k, 1, 0)
            vT = jnp.moveaxis(v, 1, 0)
            gT = jnp.moveaxis(g, 1, 0)
            bT = jnp.moveaxis(beta, 1, 0)
            S0 = jnp.zeros((q.shape[0], H, Kd, Vd), q.dtype)

            def step(S, inp):
                q_t, k_t, v_t, g_t, b_t = inp
                S = S * jnp.exp(g_t)[..., None, None]
                kv = jnp.einsum('bhk,bhkv->bhv', k_t, S)
                delta = (v_t - kv) * b_t[..., None]
                S = S + k_t[..., :, None] * delta[..., None, :]
                o = jnp.einsum('bhk,bhkv->bhv', q_t, S)
                return (S, o)
            _, o = jax.lax.scan(step, S0, (qT, kT, vT, gT, bT))
            return jnp.moveaxis(o, 0, 1)

        def _forward(x, ln1_g, ln1_b, ln2_g, ln2_b, rms_in_w, Wq, Wk, Wv, conv_q_w, conv_k_w, conv_v_w, Wa, dt_bias, A_log, Wb, Wg, o_norm_w, Wo, W2, b2):
            b, t, _ = x.shape
            h = _layernorm(x, ln1_g, ln1_b)
            h = _rmsnorm(h, rms_in_w)
            q = _causal_conv_silu(h @ Wq, conv_q_w).reshape(b, t, H, Kd)
            k = _causal_conv_silu(h @ Wk, conv_k_w).reshape(b, t, H, Kd)
            v = _causal_conv_silu(h @ Wv, conv_v_w).reshape(b, t, H, Vd)
            q = _l2norm(q) * Kd ** (-0.5)
            k = _l2norm(k)
            g = -jnp.exp(A_log) * jax.nn.softplus(h @ Wa + dt_bias)
            beta = jax.nn.sigmoid(h @ Wb)
            o = _gated_delta_rule(q, k, v, g, beta)
            gate = (h @ Wg).reshape(b, t, H, Vd)
            o = _rmsnorm(o, o_norm_w) * jax.nn.silu(gate)
            enc = o.reshape(b, t, VAL_DIM) @ Wo
            x = x + enc
            h2 = _layernorm(x, ln2_g, ln2_b)
            x_out = jax.nn.gelu(h2 @ W2 + b2, approximate=False) + x
            return x_out
        return _forward(x, ln1_g, ln1_b, ln2_g, ln2_b, rms_in_w, Wq, Wk, Wv, conv_q_w, conv_k_w, conv_v_w, Wa, dt_bias, A_log, Wb, Wg, o_norm_w, Wo, W2, b2)

    def _L0_ffn_ref(hidden_states, gate_w, exp_gate, exp_up, exp_down, sh_gate, sh_up, sh_down):
        import jax, jax.numpy as jnp
        import numpy as np
        B, L, D = (4, 256, 128)
        E, K, S = (8, 2, 2)
        F = 176
        SCALE = 1.0
        INIT = 0.02

        def _swiglu(x, wg, wu, wd):
            return jax.nn.silu(x @ wg) * (x @ wu) @ wd
        Bx, Lx, Dx = hidden_states.shape
        x = hidden_states.reshape(-1, Dx)
        T = x.shape[0]
        shared = jnp.zeros_like(x)
        for i in range(sh_gate.shape[0]):
            shared = shared + _swiglu(x, sh_gate[i], sh_up[i], sh_down[i])
        logits = x @ gate_w
        probs = jax.nn.softmax(logits.astype(jnp.float32), axis=-1)
        w, sel = jax.lax.top_k(probs, K)
        w = w / jnp.sum(w, axis=-1, keepdims=True)
        w = w.astype(hidden_states.dtype)
        Wte = jnp.zeros((T, exp_gate.shape[0]), hidden_states.dtype)
        Wte = Wte.at[jnp.arange(T)[:, None], sel].add(w)
        routed = jnp.zeros_like(x)
        for e in range(exp_gate.shape[0]):
            routed = routed + Wte[:, e:e + 1] * _swiglu(x, exp_gate[e], exp_up[e], exp_down[e])
        out = shared + SCALE * routed
        return out.reshape(Bx, Lx, Dx)

    def _L1_attn_ref(x, Wq, bq, Wdown, bdown, Wup, bup, Wout, bout):
        import jax, jax.numpy as jnp
        import numpy as np
        D_MODEL = 128
        N_HEADS = 16
        D_LATENT = 32
        HEAD_DIM = D_MODEL // N_HEADS

        def apply_rope(x):
            B, T, H, D = x.shape
            inv_freq = 1.0 / 10000.0 ** (jnp.arange(0, D, 2, dtype=jnp.float32) / D)
            t = jnp.arange(T, dtype=jnp.float32)
            freqs = t[:, None] * inv_freq[None, :]
            sin_f = jnp.sin(freqs)[None, :, None, :]
            cos_f = jnp.cos(freqs)[None, :, None, :]
            x1, x2 = jnp.split(x, 2, axis=-1)
            return jnp.concatenate([x1 * cos_f - x2 * sin_f, x1 * sin_f + x2 * cos_f], axis=-1)
        B, T, D = x.shape
        H, Dh = (N_HEADS, HEAD_DIM)
        q = x @ Wq + bq
        kv_latent = x @ Wdown + bdown
        kv = kv_latent @ Wup + bup
        q = q.reshape(B, T, H, Dh)
        kv = kv.reshape(B, T, H, 2 * Dh)
        k, v = jnp.split(kv, 2, axis=-1)
        q = apply_rope(q)
        k = apply_rope(k)
        att = jnp.einsum('bthd,btgd->bthg', q, k) / jnp.sqrt(jnp.float32(Dh))
        att = jax.nn.softmax(att, axis=-1)
        out = jnp.einsum('bthg,btgd->bthd', att, v)
        out = out.reshape(B, T, D)
        return out @ Wout + bout

    def _L1_ffn_ref(input, router_w, router_b, w1, b1, w2, b2, ow1, ob1, ow2, ob2):
        import jax, jax.numpy as jnp
        import numpy as np
        E = 8
        C = 160
        D = 128
        H = 512
        B, S = (4, 256)
        Bq, Sq, Dq = input.shape
        N = Bq * Sq
        xf = input.reshape(N, Dq)
        probs = jax.nn.softmax(xf @ router_w + router_b, axis=-1)
        eid = jnp.argmax(probs, axis=-1)
        onehot = jax.nn.one_hot(eid, E, dtype=xf.dtype)
        rank = (jnp.cumsum(onehot, axis=0)[jnp.arange(N), eid] - 1.0).astype(jnp.int32)
        valid = rank < C
        pos = jnp.where(valid, rank, 0)
        vmask = valid.astype(xf.dtype)[:, None]
        buf = jnp.zeros((E, C, Dq), xf.dtype).at[eid, pos].add(xf * vmask)
        h = jax.nn.relu(jnp.einsum('ecd,edh->ech', buf, w1) + b1[:, None, :])
        y = jnp.einsum('ech,ehd->ecd', h, w2) + b2[:, None, :]
        y_tok = y[eid, pos] * vmask
        yov = jax.nn.relu(xf @ ow1 + ob1) @ ow2 + ob2
        out = y_tok + yov * (1.0 - vmask)
        return out.reshape(Bq, Sq, Dq)
    x = L0_attn_x
    x = x + _L0_attn_ref(_layernorm(x, axis=-1), L0_attn_ln1_g, L0_attn_ln1_b, L0_attn_ln2_g, L0_attn_ln2_b, L0_attn_rms_in_w, L0_attn_Wq, L0_attn_Wk, L0_attn_Wv, L0_attn_conv_q_w, L0_attn_conv_k_w, L0_attn_conv_v_w, L0_attn_Wa, L0_attn_dt_bias, L0_attn_A_log, L0_attn_Wb, L0_attn_Wg, L0_attn_o_norm_w, L0_attn_Wo, L0_attn_W2, L0_attn_b2)
    x = x + _L0_ffn_ref(_layernorm(x, axis=-1), L0_ffn_gate_w, L0_ffn_exp_gate, L0_ffn_exp_up, L0_ffn_exp_down, L0_ffn_sh_gate, L0_ffn_sh_up, L0_ffn_sh_down)
    x = x + _L1_attn_ref(_layernorm(x, axis=-1), L1_attn_Wq, L1_attn_bq, L1_attn_Wdown, L1_attn_bdown, L1_attn_Wup, L1_attn_bup, L1_attn_Wout, L1_attn_bout)
    x = x + _L1_ffn_ref(_layernorm(x, axis=-1), L1_ffn_router_w, L1_ffn_router_b, L1_ffn_w1, L1_ffn_b1, L1_ffn_w2, L1_ffn_b2, L1_ffn_ow1, L1_ffn_ob1, L1_ffn_ow2, L1_ffn_ob2)
    return x

_drawn_inputs = setup_inputs


def setup_inputs(seed=0):
    import zlib

    import numpy as np

    out = dict(_drawn_inputs(seed))
    spreads = {'L0_attn_ln1_g': (1.0, 0.6),
     'L0_attn_ln1_b': (0.0, 0.8),
     'L0_attn_ln2_g': (1.0, 0.6),
     'L0_attn_ln2_b': (0.0, 0.8),
     'L0_attn_rms_in_w': (1.0, 0.6),
     'L0_attn_o_norm_w': (1.0, 0.6),
     'L0_attn_b2': (0.0, 0.1),
     'L1_attn_bq': (0.0, 1.62),
     'L1_attn_bdown': (0.0, 1.186),
     'L1_attn_bup': (0.0, 1.032),
     'L1_attn_bout': (0.0, 0.509),
     'L1_ffn_router_b': (0.0, 0.1),
     'L1_ffn_b1': (0.0, 2.0),
     'L1_ffn_b2': (0.0, 1.1),
     'L1_ffn_ob1': (0.0, 1.998),
     'L1_ffn_ob2': (0.0, 0.77)}
    factors = {'L0_attn_Wq': 3.896,
     'L0_attn_Wk': 3.848,
     'L0_attn_Wv': 3.849,
     'L0_attn_conv_q_w': 3.866,
     'L0_attn_conv_k_w': 3.884,
     'L0_attn_conv_v_w': 3.77,
     'L0_attn_Wa': 8.0,
     'L0_attn_dt_bias': 8.0,
     'L0_attn_A_log': 8.0,
     'L0_attn_Wb': 8.0,
     'L0_attn_Wg': 3.861,
     'L0_attn_Wo': 3.855,
     'L0_ffn_gate_w': 8.0,
     'L0_ffn_exp_gate': 8.0,
     'L0_ffn_exp_up': 8.0,
     'L0_ffn_exp_down': 8.0,
     'L0_ffn_sh_gate': 7.992,
     'L0_ffn_sh_up': 8.0,
     'L0_ffn_sh_down': 8.0,
     'L1_ffn_w1': 12.483,
     'L1_ffn_ow1': 7.386}
    for name, (base, spread) in spreads.items():
        noise = np.random.default_rng([zlib.crc32(name.encode()), seed]).standard_normal(out[name].shape)
        drawn = base * np.exp(spread * noise) if base else spread * noise
        out[name] = jnp.asarray(drawn.astype(out[name].dtype))
    for name, factor in factors.items():
        out[name] = (out[name] * factor).astype(out[name].dtype)
    return out
```

```python
import numpy as np
import concourse.bass as bass
from concourse import mybir
from contextlib import ExitStack

F32 = mybir.dt.float32
I32 = mybir.dt.int32
U32 = mybir.dt.uint32
ALU = mybir.AluOpType
ACT = mybir.ActivationFunctionType
AX = mybir.AxisListType

B, T, D = 4, 1024, 128
P = 128
STEPS = T // P
TILES = B * STEPS
H, KD, VD, TAPS = 4, 32, 64, 4
KEYS, VALS = H * KD, H * VD
CHUNKS = (2 * KEYS + VALS) // P
GATES = VALS + 2 * H
LN_EPS, RMS_EPS = 1e-5, 1e-6
LOWEST_DECAY = -104.0
E, F, NETS = 8, 176, 10
CHUNKS_F = -(-NETS * F // P)
GROUPS = -(-CHUNKS_F // 4)
HEADS, HD, LATENT = 16, 8, 32
FF, CAP = 512, 160
LEVELS = (2, 4, 8, 16, 32, 64)


def spread(ap, axis, n):
    shape = list(ap.shape)
    return ap.unsqueeze(axis).to_broadcast(shape[:axis] + [n] + shape[axis:])


def named_signals(nc, ctx, layer=""):
    made = {}

    @ctx.callback
    def _():
        nc.clear_and_free_semaphores(list(made.values()))
        nc.all_engine_barrier()

    def signal(name):
        if name not in made:
            made[name] = nc.alloc_semaphore(layer + name)
        return made[name]

    return signal


def delta_rule_layer(nc, ctx0, x_all, const, w, x_loaded, LOADED, psum):
    with ExitStack() as ctx:
        def sb(name, shape, dt=F32):
            return ctx.enter_context(nc.sbuf_tensor(name, shape, dt))

        S = named_signals(nc, ctx)
        xc = sb("xc", [P, B, D])
        y0 = sb("y0", [P, B, D])
        z = sb("z", [P, B, D])
        z_scaled = sb("z_scaled", [P, B, D])
        z_affine = sb("z_affine", [P, B, D])
        h = sb("h", [P, B, D])
        h_t = sb("h_t", [P, B, P])
        stats = sb("stats", [P, B, 6])
        mean_var = sb("mean_var", [P, B, 2])
        var_eps = sb("var_eps", [P, B])
        rstd = sb("rstd", [P, B])
        sum_sq = sb("sum_sq", [P, B])
        conv_in = sb("conv_in", [P, CHUNKS, B, TAPS - 1 + P])
        conv_acc = sb("conv_acc", [P, CHUNKS, B, P])
        conv_act = sb("conv_act", [P, CHUNKS, B, P])
        gate = sb("gate", [P, B, VALS])
        ab = sb("ab", [P, B, 2 * H])
        sm = sb("sm", [P, 16, B, H])
        qk_sq = sb("qk_sq", [P, B, 2 * KEYS])
        qk_var = sb("qk_var", [P, B, 2 * H])
        qk_rn = sb("qk_rn", [P, B, 2 * H])
        qk = sb("qk", [P, B, 2 * H, KD])
        beta_v = sb("beta_v", [P, B, H, VD])
        g_wide = sb("g_wide", [P, B, H, KD])
        g_masked = sb("g_masked", [P, B, H, P])
        small_exp = sb("small_exp", [P, 2 * B * H + B])
        decay = sb("decay", [P, B, H, P])
        decay_strict = sb("decay_strict", [P, B, H, P])
        q_dec = sb("q_dec", [P, B, H, KD])
        k_dec = sb("k_dec", [P, B, H, KD])
        k_end = sb("k_end", [P, B, H, KD])
        k_t = sb("k_t", [P, B, P])
        q_t = sb("q_t", [P, B, P])
        qd_t = sb("qd_t", [P, B, P])
        kd_t = sb("kd_t", [P, B, P])
        a_mat = sb("a_mat", [P, H, B, P])
        inv = sb("inv", [P, H, B, P])
        inv_t = sb("inv_t", [P, H, B, P])
        prod = conv_acc
        att_t = sb("att_t", [P, H, B, P])
        att = g_masked[:, :, :, :].rearrange("p b h n -> p h b n")
        rhs = sb("rhs", [P, B, H, VD])
        delta = sb("delta", [P, B, H, VD])
        state = sb("state_bd", [P, B, H * VD])
        update = sb("update", [P, B, H * VD])
        o_sq = sb("o_sq", [P, B, H, VD])
        o_var = sb("o_var", [P, B, H])
        o_rn = sb("o_rn", [P, B, H])
        o_norm = sb("o_norm", [P, B, H * VD])
        o_gated = sb("o_gated", [P, B, H * VD])
        o_t = sb("o_t", [P, 2, B, P])
        x1 = sb("x1", [P, B, D])
        z2 = sb("z2", [P, B, D])
        z2_t = sb("z2_t", [P, B, P])
        pre_gelu = sb("pre_gelu", [P, B, D])
        post_gelu = sb("post_gelu", [P, B, D])
        x_plus = sb("x_plus", [P, B, D])
        bank = psum
        low = [bank[5], bank[6], bank[7], bank[0]]
        high = [bank[1], bank[2], bank[3], bank[4]]
        BETA, NEG_BETA, G, MAG, U, RELU, DEN, SER, SQ, Q0, Q1, EB, NBG, MAG2 = range(14)

        block = ctx.enter_context(nc.Block())

        def wait_apart(engine, semaphore, value):
            engine.wait_ge(semaphore, value)
            engine.sem_inc(S("waited_apart"), 1)

        def mean_and_variance(dve, src, tag, t):
            for j in range(B):
                last = nc.vector.bn_stats(stats[:, j, :], src[:, j, :])
            last.then_inc(S(tag + "_stats"), 1)
            wait_apart(dve, S(tag + "_stats"), t + 1)
            for j in range(B):
                last = nc.vector.bn_aggr(mean_var[:, j, :], stats[:, j, :])
            last.then_inc(S(tag + "_aggr"), 1)
            dve.wait_ge(S(tag + "_aggr"), t + 1)
            nc.vector.tensor_scalar(var_eps[:], mean_var[:, :, 1], LN_EPS, None, ALU.add).then_inc(S(tag + "_var"), 1)

        def normalise(dve, dst, src, tag, t):
            dve.wait_ge(S(tag + "_rstd"), t + 1)
            for j in range(B):
                last = nc.vector.tensor_scalar(dst[:, j, :], src[:, j, :], mean_var[:, j, 0:1], rstd[:, j:j + 1],
                                               ALU.subtract, ALU.mult)
            last.then_inc(S(tag), 1)

        def inverse_root(pool, dst, src, tag, out_tag, t):
            pool.wait_ge(S(tag), t + 1)
            n = src.free_size() if callable(src.free_size) else src.free_size
            nc.gpsimd.tensor_tensor(dst, src, const["minus_half"][:, 0:n], ALU.pow).then_inc(S(out_tag), 1)

        @block.sync
        def _(sp):
            sp.nop()

        @block.gpsimd
        def _(pool):
            nc.gpsimd.memset(conv_in[:, :, :, 0:TAPS - 1], 0.0).then_inc(S("halo"), 1)
            nc.gpsimd.memset(state[:], 0.0).then_inc(S("state"), 1)
            with pool.Fori(0, STEPS) as t:
                inverse_root(pool, rstd[:], var_eps[:], "ln0_var", "ln0_rstd", t)
                inverse_root(pool, rstd[:], var_eps[:], "ln1_var", "ln1_rstd", t)
                pool.wait_ge(S("ln1"), t + 1)
                nc.gpsimd.tensor_tensor(z_scaled[:], z[:], spread(const["ln1_g"][:], 1, B), ALU.mult).then_inc(S("z_scaled"), 1)
                pool.wait_ge(S("z_scaled"), t + 1)
                nc.gpsimd.tensor_tensor(z_affine[:], z_scaled[:], spread(const["ln1_b"][:], 1, B), ALU.add).then_inc(S("z_affine"), 1)
                inverse_root(pool, rstd[:], var_eps[:], "rms_var", "rms_rstd", t)
                wait_apart(pool, S("conv_done"), t + 1)
                nc.gpsimd.tensor_copy(conv_in[:, :, :, 0:TAPS - 1], conv_in[:, :, :, P:P + TAPS - 1]).then_inc(S("halo"), 1)
                inverse_root(pool, qk_rn[:].rearrange("p b n -> p (b n)"), qk_var[:].rearrange("p b n -> p (b n)"), "qk_var", "qk_rn", t)
                wait_apart(pool, S("g"), t + 1)
                nc.gpsimd.tensor_copy(g_wide[:], spread(sm[:, G], 3, KD)).then_inc(S("g_wide"), 1)
                for j in range(B):
                    nc.gpsimd.tensor_tensor(g_masked[:, j], spread(const["after"][:], 1, H),
                                            spread(sm[:, G, j, :], 2, P), ALU.mult).then_inc(S("g_masked"), 1)
                pool.wait_ge(S("neg_beta_decay"), t + 1)
                pool.wait_ge(S("qk"), B * (t + 1))
                eg = small_exp[:, 0:B * H].rearrange("p (b h) -> p b h", h=H)
                eg_end = small_exp[:, B * H:2 * B * H].rearrange("p (b h) -> p b h", h=H)
                for dst, src, scale, tag in ((q_dec, qk[:, :, 0:H, :], eg, "q_dec"),
                                             (k_dec, qk[:, :, H:2 * H, :], sm[:, NBG], "k_dec"),
                                             (k_end, qk[:, :, H:2 * H, :], eg_end, "k_end")):
                    nc.gpsimd.tensor_tensor(dst[:], src, spread(scale, 3, KD), ALU.mult).then_inc(S(tag), 1)
                for j in range(B):
                    wait_apart(pool, S("decay_raw"), B * t + j + 1)
                    nc.gpsimd.affine_select(out=decay[:, j], in_=decay[:, j], compare_op=ALU.is_ge, fill=0.0, base=0,
                                            pattern=[[0, H], [-1, P]], channel_multiplier=1).then_inc(S("decay"), 1)
                    wait_apart(pool, S("decay"), B * t + j + 1)
                    nc.gpsimd.affine_select(out=decay_strict[:, j], in_=decay[:, j], compare_op=ALU.is_ge, fill=0.0, base=-1,
                                            pattern=[[0, H], [-1, P]], channel_multiplier=1).then_inc(S("decay_strict"), 1)
                for hh in range(H):
                    nc.gpsimd.tensor_copy(inv[:, hh], spread(const["eye"][:], 1, B)).then_inc(S("inv_eye"), 1)
                inverse_root(pool, o_rn[:].rearrange("p b n -> p (b n)"), o_var[:].rearrange("p b n -> p (b n)"), "o_var", "o_rn", t)
                inverse_root(pool, rstd[:], var_eps[:], "ln2_var", "ln2_rstd", t)
                nc.gpsimd.tensor_tensor(x_plus[:], x1[:], xc[:], ALU.add).then_inc(S("x_plus"), 1)

        @block.scalar
        def _(act):
            with act.Fori(0, STEPS) as t:
                act.wait_ge(S("z_affine"), t + 1)
                for j in range(B):
                    last = nc.scalar.activation(z_scaled[:, j, :], z_affine[:, j, :], ACT.Square, accum_out=sum_sq[:, j:j + 1])
                last.then_inc(S("sum_sq"), 1)
                act.wait_ge(S("h_t_ps"), t + 1)
                nc.scalar.activation(h_t[:].rearrange("p b n -> p (b n)"), bank[0][:], ACT.Copy, scale=const["rms_in_w"][:]).then_inc(S("h_t"), 1)
                act.wait_ge(S("halo"), t + 1)
                for c in range(CHUNKS):
                    act.wait_ge(S("proj_ps"), CHUNKS * t + c + 1)
                    nc.scalar.activation(conv_in[:, c, :, TAPS - 1:], high[c][:].rearrange("p (b n) -> p b n", b=B), ACT.Copy).then_inc(S("conv_in"), 1)
                for j in range(B):
                    act.wait_ge(S("gates_ps"), B * t + j + 1)
                    nc.scalar.activation(gate[:, j, :], low[j][:, 0:VALS], ACT.Silu).then_inc(S("gate"), 1)
                for c in range(CHUNKS):
                    act.wait_ge(S("conv_acc"), (TAPS - 1) * CHUNKS + TAPS * CHUNKS * t + c + 1)
                    nc.scalar.activation(conv_act[:, c], conv_acc[:, c], ACT.Silu).then_inc(S("conv_act"), 1)
                for j in range(B):
                    act.wait_ge(S("conv_tok_ps"), B * t + j + 1)
                    nc.scalar.activation(qk_sq[:, j], high[j][:, 0:2 * KEYS], ACT.Square).then_inc(S("qk_sq"), 1)
                act.wait_ge(S("decay_in_mag"), t + 1)
                nc.scalar.activation(sm[:, U], sm[:, MAG], ACT.Exp, scale=-1.0).then_inc(S("u"), 1)
                nc.scalar.activation(sm[:, EB], ab[:, :, H:2 * H], ACT.Exp, scale=-1.0).then_inc(S("eb"), 1)
                act.wait_ge(S("small_ps"), t + 1)
                nc.scalar.activation(small_exp[:], bank[0][:, 0:2 * B * H + B], ACT.Exp).then_inc(S("small_exp"), 1)
                for j in range(B):
                    act.wait_ge(S("decay_ps"), B * t + j + 1)
                    nc.scalar.activation(decay[:, j], low[j % 3][:].rearrange("p (h n) -> p h n", h=H), ACT.Exp).then_inc(S("decay_raw"), 1)
                for n, dst in enumerate((k_t, q_t)):
                    act.wait_ge(S("feature_ps"), 4 * t + n + 1)
                    nc.scalar.activation(dst[:].rearrange("p b n -> p (b n)"), high[n][:], ACT.Copy).then_inc(S("feature_act"), 1)
                for hh in range(H):
                    act.wait_ge(S("att_t_ps"), H * t + hh + 1)
                    nc.scalar.activation(att_t[:, hh].rearrange("p b n -> p (b n)"), low[hh][:], ACT.Copy).then_inc(S("att_t"), 1)
                for hh in range(H):
                    act.wait_ge(S("inv_t0_ps"), H * t + hh + 1)
                    nc.scalar.activation(inv_t[:, hh].rearrange("p b n -> p (b n)"), high[hh][:], ACT.Copy).then_inc(S("inv_t0"), 1)
                NL = len(LEVELS)
                for l in range(NL):
                    for hh in range(H):
                        act.wait_ge(S("prod_ps"), H * NL * t + H * l + hh + 1)
                        nc.scalar.activation(prod[:, hh].rearrange("p b n -> p (b n)"), low[hh][:], ACT.Copy).then_inc(S("prod"), 1)
                    if l < NL - 1:
                        for hh in range(H // 2):
                            act.wait_ge(S("inv_ps"), H * (NL - 1) * t + H * l + hh + 1)
                            nc.scalar.activation(inv[:, hh].rearrange("p b n -> p (b n)"), low[hh][:], ACT.Copy).then_inc(S("inv_act"), 1)
                for n in range(2):
                    act.wait_ge(S("delta_ps"), 2 * t + n + 1)
                    nc.scalar.activation(delta[:, 2 * n:2 * n + 2].rearrange("p b h n -> p (b h n)"), low[2 + n][:], ACT.Copy).then_inc(S("delta"), 1)
                for n in range(2):
                    act.wait_ge(S("o_ps"), 2 * t + n + 1)
                    nc.scalar.activation(o_sq[:, 2 * n:2 * n + 2].rearrange("p b h n -> p (b h n)"), high[n][:], ACT.Square).then_inc(S("o_sq"), 1)
                for n in range(2):
                    act.wait_ge(S("o_t_ps"), 2 * t + n + 1)
                    nc.scalar.activation(o_t[:, n].rearrange("p b n -> p (b n)"), low[n][:], ACT.Copy, scale=const["o_norm_w"][:]).then_inc(S("o_t"), 1)
                act.wait_ge(S("z2_t_ps"), t + 1)
                nc.scalar.activation(z2_t[:].rearrange("p b n -> p (b n)"), bank[0][:], ACT.Identity, scale=const["ln2_g"][:], bias=const["ln2_b"][:]).then_inc(S("z2_t"), 1)
                act.wait_ge(S("pre_gelu"), t + 2)
                nc.scalar.activation(post_gelu[:], pre_gelu[:], ACT.Gelu).then_inc(S("post_gelu"), 1)

        @block.vector
        def _(dve):
            dve.sem_inc(S("pre_gelu"), 1)
            with dve.Fori(0, STEPS) as t:
                nc.vector.tensor_copy(xc[:], x_all[:, bass.ds(t * B, B), :]).then_inc(S("xc"), 1)
                dve.wait_ge(S("xc"), t + 1)
                mean_and_variance(dve, xc, "ln0", t)
                normalise(dve, y0, xc, "ln0", t)
                dve.wait_ge(S("ln0"), t + 1)
                mean_and_variance(dve, y0, "ln1", t)
                normalise(dve, z, y0, "ln1", t)
                dve.wait_ge(S("sum_sq"), t + 1)
                nc.vector.tensor_scalar(var_eps[:], sum_sq[:], 1.0 / D, RMS_EPS, ALU.mult, ALU.add).then_inc(S("rms_var"), 1)
                dve.wait_ge(S("rms_rstd"), t + 1)
                for j in range(B):
                    last = nc.vector.tensor_scalar(h[:, j, :], z_affine[:, j, :], rstd[:, j:j + 1], None, ALU.mult)
                last.then_inc(S("h"), 1)
                for i in range(TAPS):
                    for c in range(CHUNKS):
                        tap = const["conv_w"][:, c, i:i + 1]
                        src = conv_in[:, c, :, i:i + P]
                        if i == 0:
                            dve.wait_ge(S("conv_in"), CHUNKS * t + c + 1)
                            ins = nc.vector.tensor_scalar(conv_acc[:, c], src, tap, None, ALU.mult)
                        else:
                            dve.wait_ge(S("conv_acc"), TAPS * CHUNKS * t + CHUNKS * (i - 1) + c + 1)
                            ins = nc.vector.scalar_tensor_tensor(conv_acc[:, c], src, tap, conv_acc[:, c], ALU.mult, ALU.add)
                        ins.then_inc(S("conv_acc"), 1)
                dve.wait_ge(S("conv_acc"), TAPS * CHUNKS * (t + 1))
                for j in range(B):
                    dve.wait_ge(S("gate"), B * t + j + 1)
                    ins = nc.vector.tensor_tensor(ab[:, j, :], low[j][:, VALS:GATES], const["dt_bias"][:], ALU.add)
                    ins.then_inc(S("ab"), 1)
                dve.wait_ge(S("ab"), B * (t + 1))
                nc.vector.scalar_tensor_tensor(sm[:, MAG], ab[:, :, 0:H], -1.0, ab[:, :, 0:H], ALU.mult, ALU.max).then_inc(S("decay_in_mag"), 1)
                nc.vector.tensor_scalar(sm[:, RELU], ab[:, :, 0:H], 0.0, None, ALU.max).then_inc(S("conv_done"), 1)
                step = [0]
                SMALL = 14

                def chain(ins):
                    step[0] += 1
                    ins.then_inc(S("small_step"), 1)
                    dve.wait_ge(S("small_step"), SMALL * t + step[0])

                dve.wait_ge(S("eb"), t + 1)
                chain(nc.vector.tensor_scalar(sm[:, EB], sm[:, EB], 1.0, None, ALU.add))
                chain(nc.vector.reciprocal(sm[:, BETA], sm[:, EB]))
                chain(nc.vector.tensor_scalar(sm[:, DEN], sm[:, U], 2.0, None, ALU.add))
                chain(nc.vector.reciprocal(sm[:, DEN], sm[:, DEN]))
                chain(nc.vector.tensor_tensor(sm[:, SER], sm[:, U], sm[:, DEN], ALU.mult))
                chain(nc.vector.tensor_tensor(sm[:, SQ], sm[:, SER], sm[:, SER], ALU.mult))
                chain(nc.vector.tensor_scalar(sm[:, Q0], sm[:, SQ], 1.0 / 15, None, ALU.mult))
                for n in (13, 11, 9, 7, 5, 3):
                    chain(nc.vector.scalar_tensor_tensor(sm[:, Q0], sm[:, Q0], 1.0 / n, sm[:, SQ], ALU.add, ALU.mult))
                chain(nc.vector.scalar_tensor_tensor(sm[:, Q0], sm[:, Q0], 1.0, sm[:, SER], ALU.add, ALU.mult))
                assert step[0] == SMALL
                nc.vector.scalar_tensor_tensor(sm[:, Q1], sm[:, Q0], 2.0, sm[:, RELU], ALU.mult, ALU.add).then_inc(S("softplus"), 1)
                dve.wait_ge(S("softplus"), t + 1)
                nc.vector.tensor_tensor(sm[:, Q0], sm[:, Q1], spread(const["neg_exp_a"][:], 1, B), ALU.mult).then_inc(S("g_raw"), 1)
                dve.wait_ge(S("g_raw"), t + 1)
                nc.vector.tensor_scalar(sm[:, G], sm[:, Q0], LOWEST_DECAY, None, ALU.max).then_inc(S("g"), 1)
                nc.vector.tensor_scalar(sm[:, NEG_BETA], sm[:, BETA], -1.0, None, ALU.mult).then_inc(S("neg_beta"), 1)
                dve.wait_ge(S("qk_sq"), B * (t + 1))
                nc.vector.tensor_reduce(qk_var[:], qk_sq[:].rearrange("p b (n k) -> p b n k", k=KD), AX.X, ALU.add).then_inc(S("qk_sum"), 1)
                dve.wait_ge(S("qk_sum"), t + 1)
                nc.vector.scalar_tensor_tensor(qk_var[:], qk_var[:], RMS_EPS, spread(const["q_scale"][:], 1, B), ALU.add, ALU.mult).then_inc(S("qk_var"), 1)
                for j in range(B):
                    nc.vector.tensor_tensor(beta_v[:, j], high[j][:, 2 * KEYS:].rearrange("p (h v) -> p h v", h=H),
                                            spread(sm[:, BETA, j, :], 2, VD), ALU.mult).then_inc(S("beta_v"), 1)
                dve.wait_ge(S("qk_rn"), t + 1)
                for j in range(B):
                    nc.vector.tensor_tensor(qk[:, j], high[j][:, 0:2 * KEYS].rearrange("p (n k) -> p n k", k=KD),
                                            spread(qk_rn[:, j, :], 2, KD), ALU.mult).then_inc(S("qk"), 1)
                dve.wait_ge(S("small_exp"), t + 1)
                dve.wait_ge(S("neg_beta"), t + 1)
                nc.vector.tensor_tensor(sm[:, NBG], sm[:, NEG_BETA], small_exp[:, 0:B * H].rearrange("p (b h) -> p b h", h=H), ALU.mult).then_inc(S("neg_beta_decay"), 1)
                for n, dst in enumerate((qd_t, kd_t)):
                    dve.wait_ge(S("feature_ps"), 4 * t + n + 3)
                    nc.vector.tensor_copy(dst[:].rearrange("p b n -> p (b n)"), high[2 + n][:]).then_inc(S("feature_dve"), 1)
                dve.wait_ge(S("decay_strict"), B * (t + 1))
                for hh in range(H):
                    dve.wait_ge(S("kk_ps"), H * t + hh + 1)
                    for j in range(B):
                        ins = nc.vector.scalar_tensor_tensor(a_mat[:, hh, j, :], low[hh][:, j * P:(j + 1) * P], sm[:, NEG_BETA, j, hh:hh + 1],
                                                             decay_strict[:, j, hh, :], ALU.mult, ALU.mult)
                    ins.then_inc(S("a_mat"), 1)
                for hh in range(H):
                    dve.wait_ge(S("qk_ps"), H * t + hh + 1)
                    nc.vector.tensor_tensor(att[:, hh], high[hh][:].rearrange("p (b n) -> p b n", b=B), decay[:, :, hh, :], ALU.mult).then_inc(S("att"), 1)
                for hh in range(H):
                    dve.wait_ge(S("a_mat"), H * t + hh + 1)
                    wait_apart(dve, S("inv_eye"), H * t + hh + 1)
                    nc.vector.copy_predicated(inv[:, hh], spread(const["merge_low"][:], 1, B), a_mat[:, hh]).then_inc(S("inv0"), 1)
                NL = len(LEVELS)
                for l in range(NL):
                    for hh in range(H):
                        wait_apart(dve, S("merged_ps"), H * NL * t + H * l + hh + 1)
                        nc.vector.copy_predicated(inv_t[:, hh], spread(const["merge"][:, l, :], 1, B),
                                                  high[hh][:].rearrange("p (b n) -> p b n", b=B)).then_inc(S("inv_t"), 1)
                    if l < NL - 1:
                        for hh in range(H // 2, H):
                            dve.wait_ge(S("inv_ps"), H * (NL - 1) * t + H * l + hh + 1)
                            nc.vector.tensor_copy(inv[:, hh].rearrange("p b n -> p (b n)"), low[hh][:]).then_inc(S("inv_dve"), 1)
                for n in range(2):
                    dve.wait_ge(S("k_state_ps"), 2 * t + n + 1)
                    nc.vector.tensor_tensor(rhs[:, 2 * n:2 * n + 2].rearrange("p b h n -> p (b h n)"), low[n][:],
                                            beta_v[:, 2 * n:2 * n + 2].rearrange("p b h n -> p (b h n)"), ALU.add).then_inc(S("rhs"), 1)
                for n in range(2):
                    dve.wait_ge(S("update_ps"), 2 * t + n + 1)
                    nc.vector.tensor_tensor(update[:, 2 * n:2 * n + 2], high[2 + n][:].rearrange("p (b n) -> p b n", b=2),
                                            spread(const["own_head"][:], 1, 2), ALU.mult).then_inc(S("update"), 1)
                dve.wait_ge(S("update"), 2 * (t + 1))
                for j in range(B):
                    ins = nc.vector.scalar_tensor_tensor(state[:, j], state[:, j], small_exp[:, 2 * B * H + j:2 * B * H + j + 1], update[:, j], ALU.mult, ALU.add)
                ins.then_inc(S("state"), 1)
                dve.wait_ge(S("o_sq"), 2 * (t + 1))
                nc.vector.tensor_reduce(o_var[:], o_sq[:], AX.X, ALU.add).then_inc(S("o_sum"), 1)
                dve.wait_ge(S("o_sum"), t + 1)
                nc.vector.tensor_scalar(o_var[:], o_var[:], 1.0 / VD, RMS_EPS, ALU.mult, ALU.add).then_inc(S("o_var"), 1)
                dve.wait_ge(S("o_rn"), t + 1)
                for n in range(2):
                    nc.vector.tensor_tensor(o_norm[:, 2 * n:2 * n + 2].rearrange("p b (h v) -> p (b h) v", h=H), high[n][:].rearrange("p (b v) -> p b v", v=VD),
                                            spread(o_rn[:, 2 * n:2 * n + 2].rearrange("p b h -> p (b h)"), 2, VD), ALU.mult).then_inc(S("o_norm"), 1)
                dve.wait_ge(S("o_norm"), 2 * (t + 1))
                nc.vector.tensor_tensor(o_gated[:], o_norm[:], gate[:], ALU.mult).then_inc(S("o_gated"), 1)
                dve.wait_ge(S("x1_ps"), t + 1)
                nc.vector.tensor_tensor(x1[:].rearrange("p b n -> p (b n)"), low[2][:], y0[:].rearrange("p b n -> p (b n)"), ALU.add).then_inc(S("x1"), 1)
                dve.wait_ge(S("x1"), t + 1)
                mean_and_variance(dve, x1, "ln2", t)
                normalise(dve, z2, x1, "ln2", t)
                dve.wait_ge(S("w2_ps"), t + 1)
                nc.vector.tensor_tensor(pre_gelu[:], low[0][:].rearrange("p (b n) -> p b n", b=B), spread(const["b2"][:], 1, B), ALU.add).then_inc(S("pre_gelu"), 1)
                dve.wait_ge(S("post_gelu"), t + 1)
                dve.wait_ge(S("x_plus"), t + 1)
                nc.vector.tensor_tensor(x_all[:, bass.ds(t * B, B), :], post_gelu[:], x_plus[:], ALU.add).then_inc(S("x_after_delta"), 1)

        @block.tensor
        def _(pe):
            mm, tr = nc.tensor.matmul, nc.tensor.transpose
            eye = const["eye"]
            with pe.Fori(0, STEPS) as t:
                pe.wait_ge(S("h"), t + 1)
                for j in range(B):
                    last = tr(bank[0][:, j * P:(j + 1) * P], h[:, j, :], eye[:])
                last.then_inc(S("h_t_ps"), 1)
                pe.wait_ge(S("h_t"), t + 1)
                h_all = h_t[:].rearrange("p b n -> p (b n)")
                for c in range(CHUNKS):
                    mm(high[c][:], w["w_qkv"][:, c, :], h_all, start=True, stop=True).then_inc(S("proj_ps"), 1)
                pe.wait_ge(S("pre_gelu"), t + 1)
                for j in range(B):
                    mm(low[j][:, 0:GATES], h_t[:, j, :], w["w_gates"][:], start=True, stop=True).then_inc(S("gates_ps"), 1)
                pe.wait_ge(S("conv_act"), CHUNKS * (t + 1))
                for j in range(B):
                    for c in range(CHUNKS):
                        last = tr(high[j][:, c * P:(c + 1) * P], conv_act[:, c, j, :], eye[:])
                    last.then_inc(S("conv_tok_ps"), 1)
                pe.wait_ge(S("g"), t + 1)
                pe.wait_ge(S("gate"), B * (t + 1))
                g_all = sm[:, G].rearrange("p b h -> p (b h)")
                n = B * H
                mm(bank[0][:, 0:n], const["up_to"][:], g_all, start=True, stop=True)
                mm(bank[0][:, n:2 * n], const["after"][:], g_all, start=True, stop=True)
                pe.wait_ge(S("g_wide"), t + 1)
                for j in range(B):
                    last = mm(bank[0][:, 2 * n + j:2 * n + j + 1], g_wide[:, j].rearrange("p h k -> p (h k)"), const["ones"][:, 0:1], start=True, stop=True)
                last.then_inc(S("small_ps"), 1)
                for j in range(B):
                    pe.wait_ge(S("g_masked"), B * t + j + 1)
                    if j == 3:
                        pe.wait_ge(S("decay_raw"), B * t + 1)
                    mm(low[j % 3][:], const["up_to"][:], g_masked[:, j].rearrange("p h n -> p (h n)"), start=True, stop=True).then_inc(S("decay_ps"), 1)
                pe.wait_ge(S("qk"), B * (t + 1))
                pe.wait_ge(S("beta_v"), B * (t + 1))
                for n, (src, tag) in enumerate(((qk[:, :, H:2 * H], "qk"), (qk[:, :, 0:H], "qk"), (q_dec, "q_dec"), (k_dec, "k_dec"))):
                    if n >= 2:
                        pe.wait_ge(S(tag), t + 1)
                    for j in range(B):
                        last = tr(high[n][:, j * P:(j + 1) * P], src[:, j].rearrange("p h k -> p (h k)"), eye[:])
                    last.then_inc(S("feature_ps"), 1)
                pe.wait_ge(S("feature_act"), 2 * (t + 1))
                pe.wait_ge(S("decay_raw"), B * (t + 1))
                pe.wait_ge(S("small_exp"), t + 1)
                for hh in range(H):
                    rows = slice(hh * KD, (hh + 1) * KD)
                    for j in range(B):
                        last = mm(low[hh][:, j * P:(j + 1) * P], k_t[rows, j, :], k_t[rows, j, :], start=True, stop=True, tile_position=(hh * KD, 0))
                    last.then_inc(S("kk_ps"), 1)
                pe.wait_ge(S("feature_dve"), 2 * (t + 1))
                for hh in range(H):
                    rows = slice(hh * KD, (hh + 1) * KD)
                    for j in range(B):
                        last = mm(high[hh][:, j * P:(j + 1) * P], q_t[rows, j, :], k_t[rows, j, :], start=True, stop=True, tile_position=(hh * KD, 0))
                    last.then_inc(S("qk_ps"), 1)
                for hh in range(H):
                    pe.wait_ge(S("att"), H * t + hh + 1)
                    for j in range(B):
                        last = tr(low[hh][:, j * P:(j + 1) * P], att[:, hh, j, :], eye[:])
                    last.then_inc(S("att_t_ps"), 1)
                for hh in range(H):
                    pe.wait_ge(S("inv0"), H * t + hh + 1)
                    for j in range(B):
                        last = tr(high[hh][:, j * P:(j + 1) * P], inv[:, hh, j, :], eye[:])
                    last.then_inc(S("inv_t0_ps"), 1)
                NL = len(LEVELS)
                for l in range(NL):
                    for hh in range(H):
                        if l == 0:
                            pe.wait_ge(S("inv_t0"), H * t + hh + 1)
                            pe.wait_ge(S("att_t"), H * t + hh + 1)
                        elif hh < H // 2:
                            pe.wait_ge(S("inv_act"), (H // 2) * ((NL - 1) * t + l - 1) + hh + 1)
                        else:
                            pe.wait_ge(S("inv_dve"), (H // 2) * ((NL - 1) * t + l - 1) + hh - H // 2 + 1)
                        for j in range(B):
                            last = mm(low[hh][:, j * P:(j + 1) * P], a_mat[:, hh, j, :], inv_t[:, hh, j, :], start=True, stop=True)
                        last.then_inc(S("prod_ps"), 1)
                    for hh in range(H):
                        pe.wait_ge(S("prod"), H * NL * t + H * l + hh + 1)
                        for j in range(B):
                            last = mm(high[hh][:, j * P:(j + 1) * P], inv[:, hh, j, :], prod[:, hh, j, :], start=True, stop=True)
                        last.then_inc(S("merged_ps"), 1)
                    if l < NL - 1:
                        for hh in range(H):
                            pe.wait_ge(S("inv_t"), H * NL * t + H * l + hh + 1)
                            for j in range(B):
                                last = tr(low[hh][:, j * P:(j + 1) * P], inv_t[:, hh, j, :], eye[:])
                            last.then_inc(S("inv_ps"), 1)
                pe.wait_ge(S("state"), t + 1)
                for n in range(2):
                    for jj in range(2):
                        j = 2 * n + jj
                        last = mm(low[n][:, jj * VALS:(jj + 1) * VALS], kd_t[:, j, :], state[:, j], start=True, stop=True)
                    last.then_inc(S("k_state_ps"), 1)
                for n in range(2):
                    pe.wait_ge(S("rhs"), 2 * t + n + 1)
                    if n == 0:
                        pe.wait_ge(S("inv_t"), H * NL * (t + 1))
                    for jj in range(2):
                        for hh in range(H):
                            j = 2 * n + jj
                            c = (jj * H + hh) * VD
                            last = mm(low[2 + n][:, c:c + VD], inv_t[:, hh, j, :], rhs[:, j, hh, :], start=True, stop=True)
                    last.then_inc(S("delta_ps"), 1)
                for n in range(2):
                    pe.wait_ge(S("delta"), 2 * t + n + 1)
                    for jj in range(2):
                        j = 2 * n + jj
                        c = jj * VALS
                        mm(high[n][:, c:c + VALS], qd_t[:, j, :], state[:, j], start=True, stop=False)
                        for hh in range(H):
                            last = mm(high[n][:, c + hh * VD:c + (hh + 1) * VD], att_t[:, hh, j, :], delta[:, j, hh, :], start=False, stop=hh == H - 1)
                    last.then_inc(S("o_ps"), 1)
                pe.wait_ge(S("k_end"), t + 1)
                for n in range(2):
                    for jj in range(2):
                        j = 2 * n + jj
                        last = mm(high[2 + n][:, jj * VALS:(jj + 1) * VALS], k_end[:, j].rearrange("p h k -> p (h k)"),
                                  delta[:, j].rearrange("p h v -> p (h v)"), start=True, stop=True)
                    last.then_inc(S("update_ps"), 1)
                pe.wait_ge(S("o_gated"), t + 1)
                for n in range(2):
                    for j in range(B):
                        last = tr(low[n][:, j * P:(j + 1) * P], o_gated[:, j, n * P:(n + 1) * P], eye[:])
                    last.then_inc(S("o_t_ps"), 1)
                pe.wait_ge(S("o_t"), 2 * (t + 1))
                for j in range(B):
                    for n in range(2):
                        last = mm(low[2][:, j * P:(j + 1) * P], o_t[:, n, j, :], w["w_o"][:, n, :], start=n == 0, stop=n == 1)
                last.then_inc(S("x1_ps"), 1)
                pe.wait_ge(S("ln2"), t + 1)
                for j in range(B):
                    last = tr(bank[0][:, j * P:(j + 1) * P], z2[:, j, :], eye[:])
                last.then_inc(S("z2_t_ps"), 1)
                pe.wait_ge(S("z2_t"), t + 1)
                for j in range(B):
                    last = mm(low[0][:, j * P:(j + 1) * P], z2_t[:, j, :], w["w_2"][:], start=True, stop=True)
                last.then_inc(S("w2_ps"), 1)


def inverse_root(nc, pool, S, const, dst, src, n, ready, done, t):
    pool.wait_ge(S(ready), t + 1)
    nc.gpsimd.tensor_tensor(dst, src, const["minus_half"][:, 0:n], ALU.pow).then_inc(S(done), 1)


def token_layers(nc, x_all, y_all, over_all, onehot_all, expert_all, const, w, psum):
    with ExitStack() as ctx:
        def sb(name, shape, dt=F32):
            return ctx.enter_context(nc.sbuf_tensor(name, shape, dt))

        S = named_signals(nc, ctx, "tokens_")
        bank = psum
        xc = sb("m_xc", [P, B, D])
        y = sb("m_y", [P, B, D])
        y_t = sb("m_y_t", [P, B, P])
        stats = sb("m_stats", [P, B, 6])
        mean_var = sb("m_mean_var", [P, B, 2])
        var_eps = sb("m_var_eps", [P, B])
        rstd = sb("m_rstd", [P, B])
        logits = sb("m_logits", [P, B, E])
        top = sb("m_top", [P, B, E])
        top_at = sb("m_top_at", [P, B, E], U32)
        top_at_f = sb("m_top_at_f", [P, B, E])
        pick = sb("m_pick", [P, 3, B, E])
        shifted = sb("m_shifted", [P, B, E])
        exp_l = sb("m_exp_l", [P, B, E])
        kept = sb("m_kept", [P, B, E])
        kept_sum = sb("m_kept_sum", [P, B])
        kept_inv = sb("m_kept_inv", [P, B])
        weight = sb("m_weight", [P, B, E])
        act_gate = sb("m_act_gate", [P, 4, F])
        hidden = sb("m_hidden", [P, 2, NETS * F])
        hidden_t = sb("m_hidden_t", [P, 2, 4, P])
        x2 = sb("m_x2", [P, B, D])
        z = sb("m_z", [P, B, D])
        z_t = sb("m_z_t", [P, B, P])
        latent = sb("m_latent", [LATENT, B * P])
        qk = sb("m_qk", [P, B, 2, 2, D // 2])
        v = sb("m_v", [P, B, HD, HEADS])
        by_cos = sb("m_by_cos", [P, B * 2, 2, D // 2])
        by_sin = sb("m_by_sin", [P, B * 2, 2, D // 2])
        turned = sb("m_turned", [P, B * 2, HEADS, HD])
        prod = sb("m_prod", [P, 2, HEADS, HEADS, HD])
        score = sb("m_score", [P, B, HEADS, HEADS])
        score_max = sb("m_score_max", [P, B, HEADS])
        probs = sb("m_probs", [P, B, HEADS, HEADS])
        prob_sum = sb("m_prob_sum", [P, B, HEADS])
        prob_inv = sb("m_prob_inv", [P, B, HEADS])
        mixed = sb("m_mixed", [P, B, HEADS, HD])
        att_out = sb("m_att_out", [P, B, D])
        att_out_t = sb("m_att_out_t", [P, B, P])
        x2_bias = sb("m_x2_bias", [P, B, D])
        x3 = sb("m_x3", [P, B, D])
        y3_t = sb("m_y3_t", [P, B, P])
        over_h = sb("m_over_h", [P, 4, B * P])
        r_logits = sb("m_r_logits", [P, B, E])
        r_top = sb("m_r_top", [P, B, E])
        r_at = sb("m_r_at", [P, B, E], U32)

        block = ctx.enter_context(nc.Block())
        flat = lambda ap: ap.rearrange("p b n -> p (b n)")
        tiles = lambda t: bass.ds(t * B, B)

        def wait_apart(engine, semaphore, value):
            engine.wait_ge(semaphore, value)
            engine.sem_inc(S("waited_apart"), 1)

        def layernorm(dve, dst, src, tag, t):
            for j in range(B):
                last = nc.vector.bn_stats(stats[:, j, :], src[:, j, :])
            last.then_inc(S(tag + "_stats"), 1)
            wait_apart(dve, S(tag + "_stats"), t + 1)
            for j in range(B):
                last = nc.vector.bn_aggr(mean_var[:, j, :], stats[:, j, :])
            last.then_inc(S(tag + "_aggr"), 1)
            dve.wait_ge(S(tag + "_aggr"), t + 1)
            nc.vector.tensor_scalar(var_eps[:], mean_var[:, :, 1], LN_EPS, None, ALU.add).then_inc(S(tag + "_var"), 1)
            dve.wait_ge(S(tag + "_rstd"), t + 1)
            for j in range(B):
                last = nc.vector.tensor_scalar(dst(j), src[:, j, :], mean_var[:, j, 0:1], rstd[:, j:j + 1],
                                               ALU.subtract, ALU.mult)
            last.then_inc(S(tag), 1)

        @block.gpsimd
        def _(pool):
            with pool.Fori(0, STEPS) as t:
                inverse_root(nc, pool, S, const, rstd[:], var_eps[:], B, "ln3_var", "ln3_rstd", t)
                inverse_root(nc, pool, S, const, rstd[:], var_eps[:], B, "ln4_var", "ln4_rstd", t)
                pool.wait_ge(S("x2"), t + 1)
                nc.gpsimd.tensor_tensor(x2_bias[:], x2[:], spread(const["bout"][:], 1, B), ALU.add).then_inc(S("x2_bias"), 1)
                pool.wait_ge(S("qkv"), 3 * (t + 1))
                parts = qk[:].rearrange("p b q s n -> p (b q s) n")
                nc.gpsimd.tensor_tensor(by_cos[:].rearrange("p b s n -> p (b s) n"), parts,
                                        const["cos"][:, bass.ds(t, 1), :].to_broadcast([P, B * 4, D // 2]), ALU.mult).then_inc(S("by_cos"), 1)
                nc.gpsimd.tensor_tensor(by_sin[:].rearrange("p b s n -> p (b s) n"), parts,
                                        const["sin"][:, bass.ds(t, 1), :].to_broadcast([P, B * 4, D // 2]), ALU.mult).then_inc(S("by_sin"), 1)
                pool.wait_ge(S("by_cos"), t + 1)
                pool.wait_ge(S("by_sin"), t + 1)
                quads = lambda ap: ap.rearrange("p b (h d) -> p b h d", h=HEADS)
                nc.gpsimd.tensor_tensor(turned[:, :, :, 0:HD // 2], quads(by_cos[:, :, 0, :]), quads(by_sin[:, :, 1, :]), ALU.subtract).then_inc(S("turned"), 1)
                nc.gpsimd.tensor_tensor(turned[:, :, :, HD // 2:], quads(by_sin[:, :, 0, :]), quads(by_cos[:, :, 1, :]), ALU.add).then_inc(S("turned"), 1)
                pool.wait_ge(S("turned"), 2 * (t + 1))
                for j in range(B):
                    pool.wait_ge(S("prod_free"), B * t + j + 1)
                    nc.gpsimd.tensor_tensor(prod[:, j % 2], spread(turned[:, 2 * j], 2, HEADS), spread(turned[:, 2 * j + 1], 1, HEADS), ALU.mult).then_inc(S("qk_prod"), 1)
                inverse_root(nc, pool, S, const, rstd[:], var_eps[:], B, "ln5_var", "ln5_rstd", t)
                wait_apart(pool, S("ln5"), t + 1)
                nc.gpsimd.tensor_copy(y_all[:, tiles(t), :], y[:]).then_inc(S("y_kept"), 1)

        @block.scalar
        def _(act):
            with act.Fori(0, STEPS) as t:
                act.wait_ge(S("y_t_ps"), t + 1)
                nc.scalar.activation(flat(y_t[:]), bank[0][:], ACT.Copy).then_inc(S("y_t"), 1)
                act.wait_ge(S("shifted"), t + 1)
                nc.scalar.activation(exp_l[:], shifted[:], ACT.Exp).then_inc(S("exp_l"), 1)
                for j in range(B + 1):
                    for e in range(NETS if j < B else 0):
                        n = j * NETS + e
                        act.wait_ge(S("gate_up_ps"), B * NETS * t + n + 1)
                        nc.scalar.activation(act_gate[:, n % 4], bank[1 + n % 4][:, 0:F], ACT.Silu).then_inc(S("act_gate"), 1)
                    for g in range(1, GROUPS if j else 0, 2):
                        act.wait_ge(S("hidden_t_ps"), GROUPS * (B * t + j - 1) + g + 1)
                        n_chunks = min(4, CHUNKS_F - 4 * g)
                        nc.scalar.activation(flat(hidden_t[:, g % 2, 0:n_chunks, :]), bank[5 + g % 2][:, 0:n_chunks * P], ACT.Copy).then_inc(S("hidden_t_act"), 1)
                act.wait_ge(S("z_t_ps"), t + 1)
                nc.scalar.activation(flat(z_t[:]), bank[0][:], ACT.Copy).then_inc(S("z_t"), 1)
                act.wait_ge(S("latent_ps"), t + 1)
                nc.scalar.activation(latent[:], bank[2][0:LATENT, :], ACT.Identity, bias=const["bdown"][:]).then_inc(S("latent"), 1)
                act.wait_ge(S("centred"), t + 1)
                nc.scalar.activation(probs[:], score[:], ACT.Exp, scale=float(HD) ** -0.5).then_inc(S("probs"), 1)
                act.wait_ge(S("att_out_t_ps"), t + 1)
                nc.scalar.activation(flat(att_out_t[:]), bank[5][:], ACT.Copy).then_inc(S("att_out_t"), 1)
                act.wait_ge(S("y3_t_ps"), t + 1)
                nc.scalar.activation(flat(y3_t[:]), bank[0][:], ACT.Copy).then_inc(S("y3_t"), 1)
                for c in range(4):
                    act.wait_ge(S("over_h_ps"), 4 * t + c + 1)
                    nc.scalar.activation(over_h[:, c, :], bank[1 + c][:], ACT.Relu, bias=const["ob1"][:, c:c + 1]).then_inc(S("over_h"), 1)

        @block.vector
        def _(dve):
            dve.sem_inc(S("hidden"), 4)
            dve.sem_inc(S("prod_free"), 2)
            with dve.Fori(0, STEPS) as t:
                nc.vector.tensor_copy(xc[:], x_all[:, tiles(t), :]).then_inc(S("m_xc"), 1)
                dve.wait_ge(S("m_xc"), t + 1)
                layernorm(dve, lambda j: y[:, j, :], xc, "ln3", t)
                dve.wait_ge(S("logits_ps"), t + 1)
                nc.vector.tensor_copy(logits[:].rearrange("p b e -> p (b e)"), bank[7][:, 0:B * E]).then_inc(S("logits"), 1)
                wait_apart(dve, S("logits"), t + 1)
                for j in range(B):
                    last = nc.vector.max(top[:, j, :], logits[:, j, :])
                last.then_inc(S("top"), 1)
                wait_apart(dve, S("top"), t + 1)
                nc.vector.tensor_tensor(shifted[:], logits[:], spread(top[:, :, 0], 2, E), ALU.subtract).then_inc(S("shifted"), 1)
                for j in range(B):
                    last = nc.vector.max_index(top_at[:, j, :], top[:, j, :], logits[:, j, :])
                last.then_inc(S("top_at"), 1)
                dve.wait_ge(S("top_at"), t + 1)
                nc.vector.tensor_copy(top_at_f[:], top_at[:]).then_inc(S("top_at_f"), 1)
                dve.wait_ge(S("top_at_f"), t + 1)
                for k in range(2):
                    last = nc.vector.tensor_tensor(pick[:, k], spread(const["expert_ids"][:], 1, B), spread(top_at_f[:, :, k], 2, E), ALU.is_equal)
                last.then_inc(S("pick"), 1)
                dve.wait_ge(S("pick"), t + 1)
                nc.vector.tensor_tensor(pick[:, 2], pick[:, 0], pick[:, 1], ALU.add).then_inc(S("picked"), 1)
                dve.wait_ge(S("picked"), t + 1)
                dve.wait_ge(S("exp_l"), t + 1)
                nc.vector.tensor_tensor(kept[:], pick[:, 2], exp_l[:], ALU.mult).then_inc(S("kept"), 1)
                dve.wait_ge(S("kept"), t + 1)
                nc.vector.tensor_reduce(kept_sum[:], kept[:], AX.X, ALU.add).then_inc(S("kept_sum"), 1)
                dve.wait_ge(S("kept_sum"), t + 1)
                nc.vector.reciprocal(kept_inv[:], kept_sum[:]).then_inc(S("kept_inv"), 1)
                dve.wait_ge(S("kept_inv"), t + 1)
                nc.vector.tensor_tensor(weight[:], kept[:], spread(kept_inv[:], 2, E), ALU.mult).then_inc(S("weight"), 1)
                dve.wait_ge(S("weight"), t + 1)
                for j in range(B + 1):
                    for e in range(NETS if j < B else 0):
                        n = j * NETS + e
                        dve.wait_ge(S("act_gate"), B * NETS * t + n + 1)
                        out = hidden[:, j % 2, e * F:(e + 1) * F]
                        up = bank[1 + n % 4][:, F:2 * F]
                        if e < E:
                            ins = nc.vector.scalar_tensor_tensor(out, up, weight[:, j, e:e + 1], act_gate[:, n % 4], ALU.mult, ALU.mult)
                        else:
                            ins = nc.vector.tensor_tensor(out, up, act_gate[:, n % 4], ALU.mult)
                        ins.then_inc(S("hidden"), 1)
                    for g in range(0, GROUPS if j else 0, 2):
                        dve.wait_ge(S("hidden_t_ps"), GROUPS * (B * t + j - 1) + g + 1)
                        n_chunks = min(4, CHUNKS_F - 4 * g)
                        nc.vector.tensor_copy(flat(hidden_t[:, g % 2, 0:n_chunks, :]), bank[5 + g % 2][:, 0:n_chunks * P]).then_inc(S("hidden_t_dve"), 1)
                dve.wait_ge(S("mixture_ps"), B * (t + 1))
                nc.vector.tensor_tensor(flat(x2[:]), bank[7][:], flat(xc[:]), ALU.add).then_inc(S("x2"), 1)
                dve.wait_ge(S("x2"), t + 1)
                layernorm(dve, lambda j: z[:, j, :], x2, "ln4", t)
                dve.wait_ge(S("q_ps"), t + 1)
                nc.vector.tensor_tensor(qk[:, :, 0].rearrange("p b s n -> p b (s n)"), bank[1][:].rearrange("p (b n) -> p b n", b=B),
                                        spread(const["bq"][:], 1, B), ALU.add).then_inc(S("qkv"), 1)
                for n in range(2):
                    dve.wait_ge(S("kv_ps"), 2 * t + n + 1)
                    src = bank[3 + n][:].rearrange("p (b n) -> p b n", b=2)
                    nc.vector.tensor_tensor(qk[:, 2 * n:2 * n + 2, 1].rearrange("p b s n -> p b (s n)"), src[:, :, 0:D], spread(const["bup"][:, 0:D], 1, 2), ALU.add)
                    nc.vector.tensor_tensor(v[:, 2 * n:2 * n + 2].rearrange("p b d h -> p b (d h)"), src[:, :, D:2 * D], spread(const["bup"][:, D:2 * D], 1, 2), ALU.add).then_inc(S("qkv"), 1)
                for j in range(B):
                    dve.wait_ge(S("qk_prod"), B * t + j + 1)
                    nc.vector.tensor_reduce(score[:, j], prod[:, j % 2], AX.X, ALU.add).then_inc(S("prod_free" if j < 2 else "score"), 1)
                dve.wait_ge(S("score"), 2 * (t + 1))
                nc.vector.tensor_reduce(score_max[:], score[:], AX.X, ALU.max).then_inc(S("score_max"), 1)
                dve.wait_ge(S("score_max"), t + 1)
                merged = lambda ap: ap.rearrange("p b h g -> p (b h) g")
                nc.vector.tensor_tensor(merged(score[:]), merged(score[:]), spread(score_max[:].rearrange("p b h -> p (b h)"), 2, HEADS), ALU.subtract).then_inc(S("centred"), 1)
                dve.wait_ge(S("probs"), t + 1)
                nc.vector.tensor_reduce(prob_sum[:], probs[:], AX.X, ALU.add).then_inc(S("prob_sum"), 1)
                dve.wait_ge(S("prob_sum"), t + 1)
                nc.vector.reciprocal(prob_inv[:], prob_sum[:]).then_inc(S("prob_inv"), 1)
                for j in range(B):
                    if j >= 2:
                        dve.wait_ge(S("mixed"), B * t + j - 1)
                    nc.vector.tensor_tensor(prod[:, j % 2].rearrange("p h g d -> p h (g d)").rearrange("p h (d g) -> p h d g", d=HD),
                                            spread(probs[:, j], 2, HD), spread(v[:, j], 1, HEADS), ALU.mult).then_inc(S("pv_prod"), 1)
                    dve.wait_ge(S("pv_prod"), B * t + j + 1)
                    nc.vector.tensor_reduce(mixed[:, j], prod[:, j % 2].rearrange("p h g d -> p h (g d)").rearrange("p h (d g) -> p h d g", d=HD),
                                            AX.X, ALU.add).then_inc(S("mixed"), 1)
                dve.wait_ge(S("mixed"), B * (t + 1))
                nc.vector.tensor_tensor(att_out[:].rearrange("p b (h d) -> p (b h) d", h=HEADS), mixed[:].rearrange("p b h d -> p (b h) d"),
                                        spread(prob_inv[:].rearrange("p b h -> p (b h)"), 2, HD), ALU.mult).then_inc(S("att_out"), 1)
                dve.sem_inc(S("prod_free"), 2)
                dve.wait_ge(S("x2_bias"), t + 1)
                dve.wait_ge(S("wout_ps"), t + 1)
                nc.vector.tensor_tensor(flat(x3[:]), bank[6][:], flat(x2_bias[:]), ALU.add).then_inc(S("x3"), 1)
                wait_apart(dve, S("x3"), t + 1)
                nc.vector.tensor_copy(x_all[:, tiles(t), :], x3[:]).then_inc(S("x3_kept"), 1)
                layernorm(dve, lambda j: y[:, j, :], x3, "ln5", t)
                dve.wait_ge(S("r_logits_ps"), t + 1)
                nc.vector.tensor_tensor(r_logits[:], bank[7][:, 0:B * E].rearrange("p (b e) -> p b e", b=B), spread(const["router_b"][:], 1, B), ALU.add).then_inc(S("r_logits"), 1)
                wait_apart(dve, S("r_logits"), t + 1)
                for j in range(B):
                    last = nc.vector.max(r_top[:, j, :], r_logits[:, j, :])
                last.then_inc(S("r_top"), 1)
                wait_apart(dve, S("r_top"), t + 1)
                for j in range(B):
                    last = nc.vector.max_index(r_at[:, j, :], r_top[:, j, :], r_logits[:, j, :])
                last.then_inc(S("r_at"), 1)
                wait_apart(dve, S("r_at"), t + 1)
                nc.vector.tensor_copy(expert_all[:, tiles(t)], r_at[:, :, 0]).then_inc(S("expert"), 1)
                dve.wait_ge(S("expert"), t + 1)
                nc.vector.tensor_tensor(onehot_all[:, tiles(t), :], spread(const["expert_ids"][:], 1, B), spread(expert_all[:, tiles(t)], 2, E), ALU.is_equal).then_inc(S("onehot"), 1)
                dve.wait_ge(S("over_ps"), t + 1)
                nc.vector.tensor_tensor(over_all[:, tiles(t), :], bank[5][:].rearrange("p (b n) -> p b n", b=B), spread(const["ob2"][:], 1, B), ALU.add).then_inc(S("over"), 1)

        @block.tensor
        def _(pe):
            mm, tr = nc.tensor.matmul, nc.tensor.transpose
            eye = const["eye"]
            with pe.Fori(0, STEPS) as t:
                pe.wait_ge(S("ln3"), t + 1)
                for j in range(B):
                    last = tr(bank[0][:, j * P:(j + 1) * P], y[:, j, :], eye[:])
                last.then_inc(S("y_t_ps"), 1)
                pe.wait_ge(S("y_t"), t + 1)
                for j in range(B):
                    last = mm(bank[7][:, j * E:(j + 1) * E], y_t[:, j, :], w["gate_w"][:], start=True, stop=True)
                last.then_inc(S("logits_ps"), 1)
                pe.wait_ge(S("logits"), t + 1)
                for j in range(B + 1):
                    for e in range(NETS):
                        n = j * NETS + e
                        if j < B:
                            pe.wait_ge(S("hidden"), B * NETS * t + n + 1)
                            mm(bank[1 + n % 4][:, 0:2 * F], y_t[:, j, :], w["gate_up"][:, e, :], start=True, stop=True).then_inc(S("gate_up_ps"), 1)
                    if j == 0:
                        continue
                    i = j - 1
                    pe.wait_ge(S("hidden"), B * NETS * t + NETS * j + 4)

                    def down(g):
                        tag = "hidden_t_act" if g % 2 else "hidden_t_dve"
                        pe.wait_ge(S(tag), (GROUPS // 2) * (B * t + i) + g // 2 + 1)
                        for c in range(4 * g, min(4 * g + 4, CHUNKS_F)):
                            rows = min(P, NETS * F - c * P)
                            last = mm(bank[7][:, i * P:(i + 1) * P], hidden_t[0:rows, g % 2, c % 4, :], w["down"][0:rows, c, :], start=c == 0, stop=c == CHUNKS_F - 1)
                        return last

                    for g in range(GROUPS):
                        for c in range(4 * g, min(4 * g + 4, CHUNKS_F)):
                            cols = min(P, NETS * F - c * P)
                            last = tr(bank[5 + g % 2][0:cols, c % 4 * P:(c % 4 + 1) * P], hidden[:, i % 2, c * P:c * P + cols], eye[:])
                        last.then_inc(S("hidden_t_ps"), 1)
                        if g > 0:
                            down(g - 1)
                    down(GROUPS - 1).then_inc(S("mixture_ps"), 1)
                pe.wait_ge(S("ln4"), t + 1)
                for j in range(B):
                    last = tr(bank[0][:, j * P:(j + 1) * P], z[:, j, :], eye[:])
                last.then_inc(S("z_t_ps"), 1)
                pe.wait_ge(S("z_t"), t + 1)
                mm(bank[2][0:LATENT, :], w["wdown"][:], flat(z_t[:]), start=True, stop=True).then_inc(S("latent_ps"), 1)
                for j in range(B):
                    last = mm(bank[1][:, j * P:(j + 1) * P], z_t[:, j, :], w["wq"][:], start=True, stop=True)
                last.then_inc(S("q_ps"), 1)
                pe.wait_ge(S("latent"), t + 1)
                for n in range(2):
                    for jj in range(2):
                        j = 2 * n + jj
                        last = mm(bank[3 + n][:, jj * 2 * D:(jj + 1) * 2 * D], latent[:, j * P:(j + 1) * P], w["wup"][:], start=True, stop=True)
                    last.then_inc(S("kv_ps"), 1)
                pe.wait_ge(S("att_out"), t + 1)
                for j in range(B):
                    last = tr(bank[5][:, j * P:(j + 1) * P], att_out[:, j, :], eye[:])
                last.then_inc(S("att_out_t_ps"), 1)
                pe.wait_ge(S("att_out_t"), t + 1)
                for j in range(B):
                    last = mm(bank[6][:, j * P:(j + 1) * P], att_out_t[:, j, :], w["wout"][:], start=True, stop=True)
                last.then_inc(S("wout_ps"), 1)
                pe.wait_ge(S("ln5"), t + 1)
                for j in range(B):
                    last = tr(bank[0][:, j * P:(j + 1) * P], y[:, j, :], eye[:])
                last.then_inc(S("y3_t_ps"), 1)
                pe.wait_ge(S("y3_t"), t + 1)
                for j in range(B):
                    last = mm(bank[7][:, j * E:(j + 1) * E], y3_t[:, j, :], w["router_w"][:], start=True, stop=True)
                last.then_inc(S("r_logits_ps"), 1)
                for c in range(4):
                    mm(bank[1 + c][:], w["ow1"][:, c * P:(c + 1) * P], flat(y3_t[:]), start=True, stop=True).then_inc(S("over_h_ps"), 1)
                pe.wait_ge(S("over_h"), 4 * (t + 1))
                for j in range(B):
                    for c in range(4):
                        last = mm(bank[5][:, j * P:(j + 1) * P], over_h[:, c, j * P:(j + 1) * P], w["ow2"][:, c, :], start=c == 0, stop=c == 3)
                last.then_inc(S("over_ps"), 1)


def capacity_layer(nc, x_all, y_all, over_all, onehot_all, expert_all, const, w, psum, slots_in, slots_out, out_dram):
    with ExitStack() as ctx:
        def sb(name, shape, dt=F32):
            return ctx.enter_context(nc.sbuf_tensor(name, shape, dt))

        S = named_signals(nc, ctx, "capacity_")
        bank = psum
        n_slots = E * CAP
        blocks = n_slots // P
        zeros = sb("c_zeros", [P, n_slots // P, D])
        totals = sb("c_totals", [P, E, B, STEPS])
        running = sb("c_running", [P, E, B * STEPS])
        before = sb("c_before", [P, E, B, STEPS])
        place = sb("c_place", [P, STEPS, B, E])
        own = sb("c_own", [P, TILES, E])
        rank = sb("c_rank", [P, TILES])
        late = sb("c_late", [P, TILES])
        slot_f = sb("c_slot_f", [P, 2, TILES])
        slot = sb("c_slot", [P, TILES], U32)
        rows = sb("c_rows", [P, blocks, D])
        rows_t = sb("c_rows_t", [P, n_slots])
        hidden = sb("c_hidden", [P, 2, 4, CAP])
        y_t = sb("c_y_t", [P, n_slots])
        y_rows = sb("c_y_rows", [P, blocks, D])
        taken = sb("c_taken", [P, TILES, D])
        late_sum = sb("c_late_sum", [P, TILES, D])
        result = y_all
        block = ctx.enter_context(nc.Block())

        @block.sync
        def _(sp):
            sp.wait_ge(S("zeros"), 1)
            sp.dma_start(slots_in.rearrange("(c p) d -> p c d", p=P), zeros[:]).then_inc(S("slots_zeroed"), 16)
            sp.wait_ge(S("scattered"), 16 * TILES)
            sp.dma_start(rows[:], slots_in.rearrange("(c p) d -> p c d", p=P)).then_inc(S("rows"), 16)
            sp.wait_ge(S("y_rows"), 3)
            sp.dma_start(slots_out.rearrange("(c p) d -> p c d", p=P), y_rows[:]).then_inc(S("slots_done"), 16)
            for t in range(STEPS):
                sp.wait_ge(S("result"), t + 1)
                sp.dma_start(out_dram[t], result[:, t * B:(t + 1) * B, :]).then_inc(S("stored"), 16)
            sp.wait_ge(S("stored"), 16 * STEPS)

        @block.gpsimd
        def _(pool):
            nc.gpsimd.memset(zeros[:], 0.0).then_inc(S("zeros"), 1)
            nc.gpsimd.memset(taken[:], 0.0).then_inc(S("taken_zeroed"), 1)
            pool.wait_ge(S("slots_zeroed"), 16)
            pool.wait_ge(S("slot"), 1)
            for n in range(TILES):
                pool.indirect_dma_start(out=slots_in, out_offset=bass.IndirectOffsetOnAxis(slot[:, n:n + 1], 0), in_=y_all[:, n, :], in_offset=None,
                                        bounds_check=n_slots - 1, oob_is_err=False).then_inc(S("scattered"), 16)
            pool.wait_ge(S("slots_done"), 16)
            pool.wait_ge(S("taken_zeroed"), 1)
            for n in range(TILES):
                pool.indirect_dma_start(out=taken[:, n, :], out_offset=None, in_=slots_out, in_offset=bass.IndirectOffsetOnAxis(slot[:, n:n + 1], 0),
                                        bounds_check=n_slots - 1, oob_is_err=False).then_inc(S("taken"), 16)

        @block.vector
        def _(dve):
            counts = lambda ap: ap.rearrange("p (t b e) -> p t b e", t=STEPS, b=B)
            in_order = lambda ap: ap.rearrange("p e b t -> p t b e")
            dve.wait_ge(S("count_ps"), 2)
            for b in range(B):
                last = nc.vector.tensor_copy(totals[:, :, b, :].rearrange("p e t -> p t e"), counts(bank[1][:, 0:TILES * E])[:, :, b, :])
            last.then_inc(S("totals"), 1)
            dve.wait_ge(S("totals"), 1)
            for e in range(E):
                flat_e = totals[:, e].rearrange("p b t -> p (b t)")
                last = nc.vector.tensor_tensor_scan(running[:, e, :], const["ones"][:, 0:TILES], flat_e, 0.0, ALU.mult, ALU.add)
            last.then_inc(S("running"), 1)
            dve.wait_ge(S("running"), 1)
            nc.vector.tensor_tensor(before[:].rearrange("p e b t -> p (e b t)"), running[:].rearrange("p e n -> p (e n)"),
                                    totals[:].rearrange("p e b t -> p (e b t)"), ALU.subtract).then_inc(S("before"), 1)
            dve.wait_ge(S("before"), 1)
            nc.vector.tensor_tensor(place[:], counts(bank[0][:, 0:TILES * E]), in_order(before[:]), ALU.add).then_inc(S("place"), 1)
            dve.wait_ge(S("place"), 1)
            nc.vector.tensor_tensor(own[:], place[:].rearrange("p t b e -> p (t b) e"), onehot_all[:], ALU.mult).then_inc(S("own"), 1)
            dve.wait_ge(S("own"), 1)
            nc.vector.tensor_reduce(rank[:], own[:], AX.X, ALU.add).then_inc(S("rank"), 1)
            dve.wait_ge(S("rank"), 1)
            nc.vector.tensor_scalar(late[:], rank[:], float(CAP), None, ALU.is_gt).then_inc(S("late"), 1)
            nc.vector.scalar_tensor_tensor(slot_f[:, 0], expert_all[:], float(CAP), rank[:], ALU.mult, ALU.add).then_inc(S("slot_raw"), 1)
            dve.wait_ge(S("late"), 1)
            dve.wait_ge(S("slot_raw"), 1)
            nc.vector.scalar_tensor_tensor(slot_f[:, 1], late[:], float(4 * E * T), slot_f[:, 0], ALU.mult, ALU.add).then_inc(S("slot_f"), 1)
            dve.wait_ge(S("slot_f"), 1)
            nc.vector.tensor_scalar(slot[:], slot_f[:, 1], -1.0, None, ALU.add).then_inc(S("slot"), 1)
            for n in range(TILES):
                last = nc.vector.scalar_tensor_tensor(late_sum[:, n, :], over_all[:, n, :], late[:, n:n + 1], x_all[:, n, :], ALU.mult, ALU.add)
            last.then_inc(S("late_sum"), 1)
            for n in range(3):
                cols = min(4, blocks - 4 * n) * P
                dve.wait_ge(S("rows_t_ps"), n + 1)
                nc.vector.tensor_copy(rows_t[:, 512 * n:512 * n + cols], bank[5 + n][:, 0:cols]).then_inc(S("rows_t"), 1)
            for n in range(3):
                k = min(4, blocks - 4 * n)
                dve.wait_ge(S("y_rows_ps"), n + 1)
                nc.vector.tensor_copy(y_rows[:, 4 * n:4 * n + k, :].rearrange("p c d -> p (c d)"), bank[1 + n][:, 0:k * P]).then_inc(S("y_rows"), 1)
            dve.wait_ge(S("late_sum"), 1)
            dve.wait_ge(S("taken"), 16 * TILES)
            for t in range(STEPS):
                nc.vector.tensor_tensor(result[:, t * B:(t + 1) * B, :], late_sum[:, t * B:(t + 1) * B, :], taken[:, t * B:(t + 1) * B, :], ALU.add).then_inc(S("result"), 1)

        @block.scalar
        def _(act):
            for e in range(E):
                for c in range(4):
                    act.wait_ge(S("c_hidden_ps"), 4 * e + c + 1)
                    if e >= 2:
                        act.wait_ge(S("c_y_ps"), e - 1)
                    nc.scalar.activation(hidden[:, e % 2, c, :], bank[1 + c][:, 0:CAP], ACT.Relu, bias=const["b1"][:, e, c:c + 1]).then_inc(S("c_hidden"), 1)
                act.wait_ge(S("c_y_ps"), e + 1)
                nc.scalar.activation(y_t[:, e * CAP:(e + 1) * CAP], bank[5 + e % 2][:, 0:CAP], ACT.Identity, bias=const["e_b2"][:, e:e + 1]).then_inc(S("c_y"), 1)

        @block.tensor
        def _(pe):
            mm, tr = nc.tensor.matmul, nc.tensor.transpose
            eye = const["eye"]
            seen = onehot_all[:].rearrange("p n e -> p (n e)")
            mm(bank[0][:, 0:TILES * E], const["up_to"][:], seen, start=True, stop=True).then_inc(S("count_ps"), 1)
            mm(bank[1][:, 0:TILES * E], const["ones"][:], seen, start=True, stop=True).then_inc(S("count_ps"), 1)
            pe.wait_ge(S("rows"), 16)
            for c in range(blocks):
                last = tr(bank[5 + c // 4][:, c % 4 * P:(c % 4 + 1) * P], rows[:, c, :], eye[:])
                if c % 4 == 3 or c == blocks - 1:
                    last.then_inc(S("rows_t_ps"), 1)
            pe.wait_ge(S("rows_t"), 3)
            pe.wait_ge(S("place"), 1)
            for e in range(E):
                for c in range(4):
                    if e >= 1:
                        pe.wait_ge(S("c_hidden"), 4 * (e - 1) + c + 1)
                    mm(bank[1 + c][:, 0:CAP], w["w1"][:, e, c * P:(c + 1) * P], rows_t[:, e * CAP:(e + 1) * CAP], start=True, stop=True).then_inc(S("c_hidden_ps"), 1)
                if e >= 2:
                    pe.wait_ge(S("c_y"), e - 1)
                for c in range(4):
                    pe.wait_ge(S("c_hidden"), 4 * e + c + 1)
                    last = mm(bank[5 + e % 2][:, 0:CAP], w["w2"][:, e, c, :], hidden[:, e % 2, c, :], start=c == 0, stop=c == 3)
                last.then_inc(S("c_y_ps"), 1)
            pe.wait_ge(S("c_y"), E)
            for c in range(blocks):
                last = tr(bank[1 + c // 4][:, c % 4 * P:(c % 4 + 1) * P], y_t[:, c * P:(c + 1) * P], eye[:])
                if c % 4 == 3 or c == blocks - 1:
                    last.then_inc(S("y_rows_ps"), 1)


def build(nc, a, out):
    with ExitStack() as ctx:
        def sb(name, shape, dt=F32):
            return ctx.enter_context(nc.sbuf_tensor(name, shape, dt))

        signal = named_signals(nc, ctx)
        psum = [ctx.enter_context(nc.psum_tensor(f"bank{i}", [P, 512], F32)) for i in range(8)]
        x_all = sb("x_all", [P, TILES, D])
        loads = []
        const, w = {}, {}

        def load(where, name, shape, src, dt=F32):
            where[name] = sb(name + "_sb", shape, dt)
            loads.append((where[name][:], src))

        def row(ap, n):
            return ap.partition_broadcast(P)

        for name in ("eye", "after", "up_to", "own_head", "q_scale", "ones", "minus_half"):
            load(const, name, list(a[name].shape), a[name])
        load(const, "merge_low", [P, P], a["merge_low"], I32)
        load(const, "merge", [P, len(LEVELS), P], a["merge"], I32)
        for name, src in (("ln1_g", "L0_attn_ln1_g"), ("ln1_b", "L0_attn_ln1_b"), ("b2", "L0_attn_b2")):
            load(const, name, [P, D], row(a[src], D))
        for name, src in (("rms_in_w", "L0_attn_rms_in_w"), ("ln2_g", "L0_attn_ln2_g"), ("ln2_b", "L0_attn_ln2_b"), ("o_norm_w", "o_norm_w2")):
            load(const, name, [P, 1], a[src].rearrange("(p a) -> p a", a=1))
        load(const, "dt_bias", [P, 2 * H], row(a["dt_bias8"], 2 * H))
        load(const, "a_log", [P, H], row(a["L0_attn_A_log"], H))
        load(const, "conv_w", [P, CHUNKS, TAPS], a["conv_w"].rearrange("(c p) i -> p c i", p=P))
        load(w, "w_qkv", [P, CHUNKS, P], a["w_qkv"].rearrange("d (c n) -> d c n", n=P))
        load(w, "w_gates", [P, GATES], a["w_gates"])
        load(w, "w_o", [P, 2, D], a["L0_attn_Wo"].rearrange("(c p) n -> p c n", p=P))
        load(w, "w_2", [P, D], a["L0_attn_W2"])
        const["neg_exp_a"] = sb("neg_exp_a", [P, H])
        exp_a = sb("exp_a", [P, H])
        x_loaded = signal("x_loaded")
        x_dram = a["L0_attn_x"].rearrange("b (t p) d -> t p b d", p=P)
        out_dram = out.rearrange("b (t p) d -> t p b d", p=P)
        with nc.Block() as block:
            @block.sync
            def _(sp):
                for n, (dst, src) in enumerate(loads):
                    sp.dma_start(dst, src).then_inc(x_loaded, 16)
                for t in range(STEPS):
                    sp.dma_start(x_all[:, t * B:(t + 1) * B, :], x_dram[t]).then_inc(x_loaded, 16)
                sp.wait_ge(x_loaded, 16 * (len(loads) + STEPS))

            @block.scalar
            def _(act):
                act.wait_ge(x_loaded, 16 * (len(loads) + STEPS))
                nc.scalar.activation(exp_a[:], const["a_log"][:], ACT.Exp).then_inc(signal("exp_a"), 1)

            @block.vector
            def _(dve):
                dve.wait_ge(signal("exp_a"), 1)
                nc.vector.tensor_scalar(const["neg_exp_a"][:], exp_a[:], -1.0, None, ALU.mult).then_inc(signal("neg_exp_a"), 1)
                dve.wait_ge(signal("neg_exp_a"), 1)

        delta_rule_layer(nc, ctx, x_all, const, w, x_loaded, 16 * (len(loads) + STEPS), psum)
        loads.clear()
        load(w, "gate_w", [P, E], a["L0_ffn_gate_w"])
        load(w, "gate_up", [P, NETS, 2 * F], a["gate_up"].rearrange("e d n -> d e n"))
        w["down"] = sb("down_sb", [P, CHUNKS_F, D])
        whole = (CHUNKS_F - 1) * P
        loads.append((w["down"][:, 0:CHUNKS_F - 1, :], a["down"][0:whole, :].rearrange("(c p) n -> p c n", p=P)))
        loads.append((w["down"][0:NETS * F - whole, CHUNKS_F - 1, :], a["down"][whole:, :]))
        load(w, "wq", [P, D], a["wq"])
        load(w, "wdown", [P, LATENT], a["L1_attn_Wdown"])
        load(w, "wup", [LATENT, 2 * D], a["wup"])
        load(w, "wout", [P, D], a["L1_attn_Wout"])
        load(w, "router_w", [P, E], a["L1_ffn_router_w"])
        load(w, "ow1", [P, FF], a["L1_ffn_ow1"])
        load(w, "ow2", [P, 4, D], a["L1_ffn_ow2"].rearrange("(c p) n -> p c n", p=P))
        for name, src, n in (("bq", "bq", D), ("bup", "bup", 2 * D), ("bout", "L1_attn_bout", D), ("router_b", "L1_ffn_router_b", E), ("ob2", "L1_ffn_ob2", D)):
            load(const, name, [P, n], row(a[src], n))
        load(const, "bdown", [LATENT, 1], a["L1_attn_bdown"].rearrange("(p a) -> p a", a=1))
        for name in ("cos", "sin", "expert_ids", "ob1", "b1", "e_b2"):
            load(const, name, list(a[name].shape), a[name])
        y_all = sb("y_all", [P, TILES, D])
        over_all = sb("over_all", [P, TILES, D])
        onehot_all = sb("onehot_all", [P, TILES, E])
        expert_all = sb("expert_all", [P, TILES])
        with nc.Block() as block:
            @block.sync
            def _(sp):
                for dst, src in loads:
                    sp.dma_start(dst, src).then_inc(signal("token_layers_loaded"), 16)
                sp.wait_ge(signal("token_layers_loaded"), 16 * len(loads))
        token_layers(nc, x_all, y_all, over_all, onehot_all, expert_all, const, w, psum)
        slots_in = nc.dram_tensor("slots_in", (E * CAP, D), F32, kind="Internal").ap()
        slots_out = nc.dram_tensor("slots_out", (E * CAP, D), F32, kind="Internal").ap()
        loads.clear()
        w["w1"] = sb("w1_sb", [P, E, FF])
        w["w2"] = sb("w2_sb", [P, E, 4, D])
        loads.append((w["w1"][:], a["L1_ffn_w1"].rearrange("e d n -> d e n")))
        for e in range(E):
            loads.append((w["w2"][:, e], a["L1_ffn_w2"][e].rearrange("(c p) n -> p c n", p=P)))
        with nc.Block() as block:
            @block.sync
            def _(sp):
                for dst, src in loads:
                    sp.dma_start(dst, src).then_inc(signal("experts_loaded"), 16)
                sp.wait_ge(signal("experts_loaded"), 16 * len(loads))
        capacity_layer(nc, x_all, y_all, over_all, onehot_all, expert_all, const, w, psum, slots_in, slots_out, out_dram)


def constants():
    i = np.arange(P)
    r, c = i[:, None], i[None, :]
    f = lambda m: np.ascontiguousarray(m.astype(np.float32))
    out = {
        "eye": f(r == c),
        "after": f(r > c),
        "up_to": f(r <= c),
        "own_head": f((i // KD)[:, None] == (np.arange(VALS) // VD)[None, :]),
        "q_scale": np.tile(np.repeat(np.float32([KD, 1]), H)[None], (P, 1)),
        "ones": np.ones((P, P), np.float32),
        "minus_half": np.full((P, 32), -0.5, np.float32),
    }

    inv_freq = (1.0 / 10000.0 ** (np.arange(0, HD, 2, dtype=np.float32) / np.float32(HD))).astype(np.float32)
    angle = np.arange(T, dtype=np.float32)[:, None] * inv_freq[None, :]
    for name, fn in (("cos", np.cos), ("sin", np.sin)):
        table = np.tile(fn(angle.astype(np.float64)).astype(np.float32), (1, HEADS))
        out[name] = np.ascontiguousarray(table.reshape(STEPS, P, D // 2).transpose(1, 0, 2))
    out["expert_ids"] = np.tile(np.arange(E, dtype=np.float32)[None], (P, 1))

    def merge(s):
        return ((r // (2 * s) == c // (2 * s)) & (r // s % 2 == 1) & (c // s % 2 == 0)).astype(np.int32)

    out["merge_low"] = merge(1)
    out["merge"] = np.ascontiguousarray(np.stack([merge(s).T for s in LEVELS], 1))
    return out


def kernel(**inputs):
    import concourse.bacc as bacc
    from concourse.bass_utils import run_bass_kernel_spmd

    arrays = {k: np.ascontiguousarray(v) for k, v in inputs.items()}
    arrays["w_qkv"] = np.concatenate([arrays.pop("L0_attn_Wq"), arrays.pop("L0_attn_Wk"), arrays.pop("L0_attn_Wv")], 1)
    arrays["w_gates"] = np.concatenate([arrays.pop("L0_attn_Wg"), arrays.pop("L0_attn_Wa"), arrays.pop("L0_attn_Wb")], 1)
    arrays["conv_w"] = np.concatenate([arrays.pop("L0_attn_conv_q_w"), arrays.pop("L0_attn_conv_k_w"), arrays.pop("L0_attn_conv_v_w")], 0)
    arrays["dt_bias8"] = np.concatenate([arrays.pop("L0_attn_dt_bias"), np.zeros(H, np.float32)])
    arrays["o_norm_w2"] = np.tile(arrays.pop("L0_attn_o_norm_w"), 2)
    pop = arrays.pop
    arrays["gate_up"] = np.concatenate([np.concatenate([pop("L0_ffn_exp_gate"), pop("L0_ffn_exp_up")], 2),
                                        np.concatenate([pop("L0_ffn_sh_gate"), pop("L0_ffn_sh_up")], 2)], 0)
    arrays["down"] = np.concatenate([pop("L0_ffn_exp_down").reshape(-1, D), pop("L0_ffn_sh_down").reshape(-1, D)], 0)
    halves = np.arange(D).reshape(HEADS, 2, HD // 2).transpose(1, 0, 2).ravel()
    of_kv = np.arange(2 * D).reshape(HEADS, 2, HD)
    k_order = of_kv[:, 0].ravel()[halves]
    v_order = of_kv[:, 1].T.ravel()
    kv_order = np.concatenate([k_order, v_order])
    arrays["wq"] = np.ascontiguousarray(pop("L1_attn_Wq")[:, halves])
    arrays["bq"] = pop("L1_attn_bq")[halves]
    arrays["wup"] = np.ascontiguousarray(pop("L1_attn_Wup")[:, kv_order])
    arrays["bup"] = pop("L1_attn_bup")[kv_order]
    arrays["ob1"] = np.ascontiguousarray(pop("L1_ffn_ob1").reshape(4, P).T)
    arrays["b1"] = np.ascontiguousarray(pop("L1_ffn_b1").reshape(E, 4, P).transpose(2, 0, 1))
    arrays["e_b2"] = np.ascontiguousarray(pop("L1_ffn_b2").T)
    arrays.update(constants())
    nc = bacc.Bacc("TRN2", target_bir_lowering=False, num_devices=1)
    aps = {k: nc.dram_tensor("in_" + k, v.shape, mybir.dt.from_np(v.dtype), kind="ExternalInput").ap() for k, v in arrays.items()}
    out = nc.dram_tensor("out_0", (B, T, D), F32, kind="ExternalOutput").ap()
    build(nc, aps, out)
    r = run_bass_kernel_spmd(nc, [{"in_" + k: v for k, v in arrays.items()}], core_ids=[0])
    return r.results[0]["out_0"]
```

```python
import numpy as np
import concourse.bass as bass
from concourse import mybir
from contextlib import ExitStack

F32 = mybir.dt.float32
I32 = mybir.dt.int32
U32 = mybir.dt.uint32
ALU = mybir.AluOpType
ACT = mybir.ActivationFunctionType
AX = mybir.AxisListType

B, T, D = 4, 1024, 128
P = 128
STEPS = T // P
TILES = B * STEPS
H, KD, VD, TAPS = 4, 32, 64, 4
KEYS, VALS = H * KD, H * VD
CHUNKS = (2 * KEYS + VALS) // P
GATES = VALS + 2 * H
LN_EPS, RMS_EPS = 1e-5, 1e-6
LOWEST_DECAY = -104.0
E, F, NETS = 8, 176, 10
CHUNKS_F = -(-NETS * F // P)
GROUPS = -(-CHUNKS_F // 4)
NETBANKS = 3
HEADS, HD, LATENT = 16, 8, 32
FF, CAP = 512, 160
LEVELS = (2, 4, 8, 16, 32, 64)


def spread(ap, axis, n):
    shape = list(ap.shape)
    return ap.unsqueeze(axis).to_broadcast(shape[:axis] + [n] + shape[axis:])


def named_signals(nc, ctx, layer=""):
    made = {}

    @ctx.callback
    def _():
        nc.clear_and_free_semaphores(list(made.values()))
        nc.all_engine_barrier()

    def signal(name):
        if name not in made:
            made[name] = nc.alloc_semaphore(layer + name)
        return made[name]

    return signal


def delta_rule_layer(nc, ctx0, x_all, const, w, x_loaded, LOADED, psum):
    with ExitStack() as ctx:
        def sb(name, shape, dt=F32):
            return ctx.enter_context(nc.sbuf_tensor(name, shape, dt))

        S = named_signals(nc, ctx)
        xc = sb("xc", [P, B, D])
        y0 = sb("y0", [P, B, D])
        z = sb("z", [P, B, D])
        z_scaled = sb("z_scaled", [P, B, D])
        z_affine = sb("z_affine", [P, B, D])
        h = sb("h", [P, B, D])
        h_t = sb("h_t", [P, B, P])
        stats = sb("stats", [P, B, 6])
        mean_var = sb("mean_var", [P, B, 2])
        var_eps = sb("var_eps", [P, B])
        rstd = sb("rstd", [P, B])
        sum_sq = sb("sum_sq", [P, B])
        conv_in = sb("conv_in", [P, CHUNKS, B, TAPS - 1 + P])
        conv_acc = sb("conv_acc", [P, CHUNKS, B, P])
        conv_act = sb("conv_act", [P, CHUNKS, B, P])
        gate = sb("gate", [P, B, VALS])
        ab = sb("ab", [P, B, 2 * H])
        sm = sb("sm", [P, 16, B, H])
        qk_sq = sb("qk_sq", [P, B, 2 * KEYS])
        qk_var = sb("qk_var", [P, B, 2 * H])
        qk_rn = sb("qk_rn", [P, B, 2 * H])
        qk = sb("qk", [P, B, 2 * H, KD])
        beta_v = sb("beta_v", [P, B, H, VD])
        g_wide = sb("g_wide", [P, B, H, KD])
        g_masked = sb("g_masked", [P, B, H, P])
        small_exp = sb("small_exp", [P, 2 * B * H + B])
        decay = sb("decay", [P, B, H, P])
        decay_strict = sb("decay_strict", [P, B, H, P])
        q_dec = sb("q_dec", [P, B, H, KD])
        k_dec = sb("k_dec", [P, B, H, KD])
        k_end = sb("k_end", [P, B, H, KD])
        k_t = sb("k_t", [P, B, P])
        q_t = sb("q_t", [P, B, P])
        qd_t = sb("qd_t", [P, B, P])
        kd_t = sb("kd_t", [P, B, P])
        a_mat = sb("a_mat", [P, H, B, P])
        inv = sb("inv", [P, H, B, P])
        inv_t = sb("inv_t", [P, H, B, P])
        prod = conv_acc
        att_t = sb("att_t", [P, H, B, P])
        att = g_masked[:, :, :, :].rearrange("p b h n -> p h b n")
        rhs = sb("rhs", [P, B, H, VD])
        delta = sb("delta", [P, B, H, VD])
        state = sb("state_bd", [P, B, H * VD])
        update = sb("update", [P, B, H * VD])
        o_sq = sb("o_sq", [P, B, H, VD])
        o_var = sb("o_var", [P, B, H])
        o_rn = sb("o_rn", [P, B, H])
        o_norm = sb("o_norm", [P, B, H * VD])
        o_gated = sb("o_gated", [P, B, H * VD])
        o_t = sb("o_t", [P, 2, B, P])
        x1 = sb("x1", [P, B, D])
        z2 = sb("z2", [P, B, D])
        z2_t = sb("z2_t", [P, B, P])
        pre_gelu = sb("pre_gelu", [P, B, D])
        post_gelu = sb("post_gelu", [P, B, D])
        x_plus = sb("x_plus", [P, B, D])
        bank = psum
        low = [bank[5], bank[6], bank[7], bank[0]]
        high = [bank[1], bank[2], bank[3], bank[4]]
        BETA, NEG_BETA, G, MAG, U, RELU, DEN, SER, SQ, Q0, Q1, EB, NBG, MAG2 = range(14)

        block = ctx.enter_context(nc.Block())

        def wait_apart(engine, semaphore, value):
            engine.wait_ge(semaphore, value)
            engine.sem_inc(S("waited_apart"), 1)

        def mean_and_variance(dve, src, tag, t):
            for j in range(B):
                last = nc.vector.bn_stats(stats[:, j, :], src[:, j, :])
            last.then_inc(S(tag + "_stats"), 1)
            wait_apart(dve, S(tag + "_stats"), t + 1)
            for j in range(B):
                last = nc.vector.bn_aggr(mean_var[:, j, :], stats[:, j, :])
            last.then_inc(S(tag + "_aggr"), 1)
            dve.wait_ge(S(tag + "_aggr"), t + 1)
            nc.vector.tensor_scalar(var_eps[:], mean_var[:, :, 1], LN_EPS, None, ALU.add).then_inc(S(tag + "_var"), 1)

        def normalise(dve, dst, src, tag, t):
            dve.wait_ge(S(tag + "_rstd"), t + 1)
            for j in range(B):
                last = nc.vector.tensor_scalar(dst[:, j, :], src[:, j, :], mean_var[:, j, 0:1], rstd[:, j:j + 1],
                                               ALU.subtract, ALU.mult)
            last.then_inc(S(tag), 1)

        def inverse_root(pool, dst, src, tag, out_tag, t):
            pool.wait_ge(S(tag), t + 1)
            n = src.free_size() if callable(src.free_size) else src.free_size
            nc.gpsimd.tensor_tensor(dst, src, const["minus_half"][:, 0:n], ALU.pow).then_inc(S(out_tag), 1)

        @block.sync
        def _(sp):
            sp.nop()

        @block.gpsimd
        def _(pool):
            nc.gpsimd.memset(conv_in[:, :, :, 0:TAPS - 1], 0.0).then_inc(S("halo"), 1)
            nc.gpsimd.memset(state[:], 0.0).then_inc(S("state"), 1)
            with pool.Fori(0, STEPS) as t:
                inverse_root(pool, rstd[:], var_eps[:], "ln0_var", "ln0_rstd", t)
                inverse_root(pool, rstd[:], var_eps[:], "ln1_var", "ln1_rstd", t)
                pool.wait_ge(S("ln1"), t + 1)
                nc.gpsimd.tensor_tensor(z_scaled[:], z[:], spread(const["ln1_g"][:], 1, B), ALU.mult).then_inc(S("z_scaled"), 1)
                pool.wait_ge(S("z_scaled"), t + 1)
                nc.gpsimd.tensor_tensor(z_affine[:], z_scaled[:], spread(const["ln1_b"][:], 1, B), ALU.add).then_inc(S("z_affine"), 1)
                inverse_root(pool, rstd[:], var_eps[:], "rms_var", "rms_rstd", t)
                wait_apart(pool, S("conv_done"), t + 1)
                nc.gpsimd.tensor_copy(conv_in[:, :, :, 0:TAPS - 1], conv_in[:, :, :, P:P + TAPS - 1]).then_inc(S("halo"), 1)
                inverse_root(pool, qk_rn[:].rearrange("p b n -> p (b n)"), qk_var[:].rearrange("p b n -> p (b n)"), "qk_var", "qk_rn", t)
                wait_apart(pool, S("g"), t + 1)
                nc.gpsimd.tensor_copy(g_wide[:], spread(sm[:, G], 3, KD)).then_inc(S("g_wide"), 1)
                for j in range(B):
                    nc.gpsimd.tensor_tensor(g_masked[:, j], spread(const["after"][:], 1, H),
                                            spread(sm[:, G, j, :], 2, P), ALU.mult).then_inc(S("g_masked"), 1)
                pool.wait_ge(S("neg_beta_decay"), t + 1)
                pool.wait_ge(S("qk"), B * (t + 1))
                eg = small_exp[:, 0:B * H].rearrange("p (b h) -> p b h", h=H)
                eg_end = small_exp[:, B * H:2 * B * H].rearrange("p (b h) -> p b h", h=H)
                for dst, src, scale, tag in ((q_dec, qk[:, :, 0:H, :], eg, "q_dec"),
                                             (k_dec, qk[:, :, H:2 * H, :], sm[:, NBG], "k_dec"),
                                             (k_end, qk[:, :, H:2 * H, :], eg_end, "k_end")):
                    nc.gpsimd.tensor_tensor(dst[:], src, spread(scale, 3, KD), ALU.mult).then_inc(S(tag), 1)
                for j in range(B):
                    wait_apart(pool, S("decay_raw"), B * t + j + 1)
                    nc.gpsimd.affine_select(out=decay[:, j], in_=decay[:, j], compare_op=ALU.is_ge, fill=0.0, base=0,
                                            pattern=[[0, H], [-1, P]], channel_multiplier=1).then_inc(S("decay"), 1)
                    wait_apart(pool, S("decay"), B * t + j + 1)
                    nc.gpsimd.affine_select(out=decay_strict[:, j], in_=decay[:, j], compare_op=ALU.is_ge, fill=0.0, base=-1,
                                            pattern=[[0, H], [-1, P]], channel_multiplier=1).then_inc(S("decay_strict"), 1)
                for hh in range(H):
                    nc.gpsimd.tensor_copy(inv[:, hh], spread(const["eye"][:], 1, B)).then_inc(S("inv_eye"), 1)
                inverse_root(pool, o_rn[:].rearrange("p b n -> p (b n)"), o_var[:].rearrange("p b n -> p (b n)"), "o_var", "o_rn", t)
                inverse_root(pool, rstd[:], var_eps[:], "ln2_var", "ln2_rstd", t)
                nc.gpsimd.tensor_tensor(x_plus[:], x1[:], xc[:], ALU.add).then_inc(S("x_plus"), 1)

        @block.scalar
        def _(act):
            with act.Fori(0, STEPS) as t:
                act.wait_ge(S("z_affine"), t + 1)
                for j in range(B):
                    last = nc.scalar.activation(z_scaled[:, j, :], z_affine[:, j, :], ACT.Square, accum_out=sum_sq[:, j:j + 1])
                last.then_inc(S("sum_sq"), 1)
                act.wait_ge(S("h_t_ps"), t + 1)
                nc.scalar.activation(h_t[:].rearrange("p b n -> p (b n)"), bank[0][:], ACT.Copy, scale=const["rms_in_w"][:]).then_inc(S("h_t"), 1)
                act.wait_ge(S("halo"), t + 1)
                for c in range(CHUNKS):
                    act.wait_ge(S("proj_ps"), CHUNKS * t + c + 1)
                    nc.scalar.activation(conv_in[:, c, :, TAPS - 1:], high[c][:].rearrange("p (b n) -> p b n", b=B), ACT.Copy).then_inc(S("conv_in"), 1)
                for j in range(B):
                    act.wait_ge(S("gates_ps"), B * t + j + 1)
                    nc.scalar.activation(gate[:, j, :], low[j][:, 0:VALS], ACT.Silu).then_inc(S("gate"), 1)
                for c in range(CHUNKS):
                    act.wait_ge(S("conv_acc"), (TAPS - 1) * CHUNKS + TAPS * CHUNKS * t + c + 1)
                    nc.scalar.activation(conv_act[:, c], conv_acc[:, c], ACT.Silu).then_inc(S("conv_act"), 1)
                for j in range(B):
                    act.wait_ge(S("conv_tok_ps"), B * t + j + 1)
                    nc.scalar.activation(qk_sq[:, j], high[j][:, 0:2 * KEYS], ACT.Square).then_inc(S("qk_sq"), 1)
                act.wait_ge(S("decay_in_mag"), t + 1)
                nc.scalar.activation(sm[:, U], sm[:, MAG], ACT.Exp, scale=-1.0).then_inc(S("u"), 1)
                nc.scalar.activation(sm[:, EB], ab[:, :, H:2 * H], ACT.Exp, scale=-1.0).then_inc(S("eb"), 1)
                act.wait_ge(S("small_ps"), t + 1)
                nc.scalar.activation(small_exp[:], bank[0][:, 0:2 * B * H + B], ACT.Exp).then_inc(S("small_exp"), 1)
                for j in range(B):
                    act.wait_ge(S("decay_ps"), B * t + j + 1)
                    nc.scalar.activation(decay[:, j], low[j % 3][:].rearrange("p (h n) -> p h n", h=H), ACT.Exp).then_inc(S("decay_raw"), 1)
                for n, dst in enumerate((k_t, q_t)):
                    act.wait_ge(S("feature_ps"), 4 * t + n + 1)
                    nc.scalar.activation(dst[:].rearrange("p b n -> p (b n)"), high[n][:], ACT.Copy).then_inc(S("feature_act"), 1)
                for hh in range(H):
                    act.wait_ge(S("att_t_ps"), H * t + hh + 1)
                    nc.scalar.activation(att_t[:, hh].rearrange("p b n -> p (b n)"), low[hh][:], ACT.Copy).then_inc(S("att_t"), 1)
                for hh in range(H):
                    act.wait_ge(S("inv_t0_ps"), H * t + hh + 1)
                    nc.scalar.activation(inv_t[:, hh].rearrange("p b n -> p (b n)"), high[hh][:], ACT.Copy).then_inc(S("inv_t0"), 1)
                NL = len(LEVELS)
                for l in range(NL):
                    for hh in range(H):
                        act.wait_ge(S("prod_ps"), H * NL * t + H * l + hh + 1)
                        nc.scalar.activation(prod[:, hh].rearrange("p b n -> p (b n)"), low[hh][:], ACT.Copy).then_inc(S("prod"), 1)
                    if l < NL - 1:
                        for hh in range(H // 2):
                            act.wait_ge(S("inv_ps"), H * (NL - 1) * t + H * l + hh + 1)
                            nc.scalar.activation(inv[:, hh].rearrange("p b n -> p (b n)"), low[hh][:], ACT.Copy).then_inc(S("inv_act"), 1)
                for n in range(2):
                    act.wait_ge(S("delta_ps"), 2 * t + n + 1)
                    nc.scalar.activation(delta[:, 2 * n:2 * n + 2].rearrange("p b h n -> p (b h n)"), low[2 + n][:], ACT.Copy).then_inc(S("delta"), 1)
                for n in range(2):
                    act.wait_ge(S("o_ps"), 2 * t + n + 1)
                    nc.scalar.activation(o_sq[:, 2 * n:2 * n + 2].rearrange("p b h n -> p (b h n)"), high[n][:], ACT.Square).then_inc(S("o_sq"), 1)
                for n in range(2):
                    act.wait_ge(S("o_t_ps"), 2 * t + n + 1)
                    nc.scalar.activation(o_t[:, n].rearrange("p b n -> p (b n)"), low[n][:], ACT.Copy, scale=const["o_norm_w"][:]).then_inc(S("o_t"), 1)
                act.wait_ge(S("z2_t_ps"), t + 1)
                nc.scalar.activation(z2_t[:].rearrange("p b n -> p (b n)"), bank[0][:], ACT.Identity, scale=const["ln2_g"][:], bias=const["ln2_b"][:]).then_inc(S("z2_t"), 1)
                act.wait_ge(S("pre_gelu"), t + 2)
                nc.scalar.activation(post_gelu[:], pre_gelu[:], ACT.Gelu).then_inc(S("post_gelu"), 1)

        @block.vector
        def _(dve):
            dve.sem_inc(S("pre_gelu"), 1)
            with dve.Fori(0, STEPS) as t:
                nc.vector.tensor_copy(xc[:], x_all[:, bass.ds(t * B, B), :]).then_inc(S("xc"), 1)
                dve.wait_ge(S("xc"), t + 1)
                mean_and_variance(dve, xc, "ln0", t)
                normalise(dve, y0, xc, "ln0", t)
                dve.wait_ge(S("ln0"), t + 1)
                mean_and_variance(dve, y0, "ln1", t)
                normalise(dve, z, y0, "ln1", t)
                dve.wait_ge(S("sum_sq"), t + 1)
                nc.vector.tensor_scalar(var_eps[:], sum_sq[:], 1.0 / D, RMS_EPS, ALU.mult, ALU.add).then_inc(S("rms_var"), 1)
                dve.wait_ge(S("rms_rstd"), t + 1)
                for j in range(B):
                    last = nc.vector.tensor_scalar(h[:, j, :], z_affine[:, j, :], rstd[:, j:j + 1], None, ALU.mult)
                last.then_inc(S("h"), 1)
                for i in range(TAPS):
                    for c in range(CHUNKS):
                        tap = const["conv_w"][:, c, i:i + 1]
                        src = conv_in[:, c, :, i:i + P]
                        if i == 0:
                            dve.wait_ge(S("conv_in"), CHUNKS * t + c + 1)
                            ins = nc.vector.tensor_scalar(conv_acc[:, c], src, tap, None, ALU.mult)
                        else:
                            dve.wait_ge(S("conv_acc"), TAPS * CHUNKS * t + CHUNKS * (i - 1) + c + 1)
                            ins = nc.vector.scalar_tensor_tensor(conv_acc[:, c], src, tap, conv_acc[:, c], ALU.mult, ALU.add)
                        ins.then_inc(S("conv_acc"), 1)
                dve.wait_ge(S("conv_acc"), TAPS * CHUNKS * (t + 1))
                for j in range(B):
                    dve.wait_ge(S("gate"), B * t + j + 1)
                    ins = nc.vector.tensor_tensor(ab[:, j, :], low[j][:, VALS:GATES], const["dt_bias"][:], ALU.add)
                    ins.then_inc(S("ab"), 1)
                dve.wait_ge(S("ab"), B * (t + 1))
                nc.vector.scalar_tensor_tensor(sm[:, MAG], ab[:, :, 0:H], -1.0, ab[:, :, 0:H], ALU.mult, ALU.max).then_inc(S("decay_in_mag"), 1)
                nc.vector.tensor_scalar(sm[:, RELU], ab[:, :, 0:H], 0.0, None, ALU.max).then_inc(S("conv_done"), 1)
                step = [0]
                SMALL = 14

                def chain(ins):
                    step[0] += 1
                    ins.then_inc(S("small_step"), 1)
                    dve.wait_ge(S("small_step"), SMALL * t + step[0])

                dve.wait_ge(S("eb"), t + 1)
                chain(nc.vector.tensor_scalar(sm[:, EB], sm[:, EB], 1.0, None, ALU.add))
                chain(nc.vector.reciprocal(sm[:, BETA], sm[:, EB]))
                chain(nc.vector.tensor_scalar(sm[:, DEN], sm[:, U], 2.0, None, ALU.add))
                chain(nc.vector.reciprocal(sm[:, DEN], sm[:, DEN]))
                chain(nc.vector.tensor_tensor(sm[:, SER], sm[:, U], sm[:, DEN], ALU.mult))
                chain(nc.vector.tensor_tensor(sm[:, SQ], sm[:, SER], sm[:, SER], ALU.mult))
                chain(nc.vector.tensor_scalar(sm[:, Q0], sm[:, SQ], 1.0 / 15, None, ALU.mult))
                for n in (13, 11, 9, 7, 5, 3):
                    chain(nc.vector.scalar_tensor_tensor(sm[:, Q0], sm[:, Q0], 1.0 / n, sm[:, SQ], ALU.add, ALU.mult))
                chain(nc.vector.scalar_tensor_tensor(sm[:, Q0], sm[:, Q0], 1.0, sm[:, SER], ALU.add, ALU.mult))
                assert step[0] == SMALL
                nc.vector.scalar_tensor_tensor(sm[:, Q1], sm[:, Q0], 2.0, sm[:, RELU], ALU.mult, ALU.add).then_inc(S("softplus"), 1)
                dve.wait_ge(S("softplus"), t + 1)
                nc.vector.tensor_tensor(sm[:, Q0], sm[:, Q1], spread(const["neg_exp_a"][:], 1, B), ALU.mult).then_inc(S("g_raw"), 1)
                dve.wait_ge(S("g_raw"), t + 1)
                nc.vector.tensor_scalar(sm[:, G], sm[:, Q0], LOWEST_DECAY, None, ALU.max).then_inc(S("g"), 1)
                nc.vector.tensor_scalar(sm[:, NEG_BETA], sm[:, BETA], -1.0, None, ALU.mult).then_inc(S("neg_beta"), 1)
                dve.wait_ge(S("qk_sq"), B * (t + 1))
                nc.vector.tensor_reduce(qk_var[:], qk_sq[:].rearrange("p b (n k) -> p b n k", k=KD), AX.X, ALU.add).then_inc(S("qk_sum"), 1)
                dve.wait_ge(S("qk_sum"), t + 1)
                nc.vector.scalar_tensor_tensor(qk_var[:], qk_var[:], RMS_EPS, spread(const["q_scale"][:], 1, B), ALU.add, ALU.mult).then_inc(S("qk_var"), 1)
                for j in range(B):
                    nc.vector.tensor_tensor(beta_v[:, j], high[j][:, 2 * KEYS:].rearrange("p (h v) -> p h v", h=H),
                                            spread(sm[:, BETA, j, :], 2, VD), ALU.mult).then_inc(S("beta_v"), 1)
                dve.wait_ge(S("qk_rn"), t + 1)
                for j in range(B):
                    nc.vector.tensor_tensor(qk[:, j], high[j][:, 0:2 * KEYS].rearrange("p (n k) -> p n k", k=KD),
                                            spread(qk_rn[:, j, :], 2, KD), ALU.mult).then_inc(S("qk"), 1)
                dve.wait_ge(S("small_exp"), t + 1)
                dve.wait_ge(S("neg_beta"), t + 1)
                nc.vector.tensor_tensor(sm[:, NBG], sm[:, NEG_BETA], small_exp[:, 0:B * H].rearrange("p (b h) -> p b h", h=H), ALU.mult).then_inc(S("neg_beta_decay"), 1)
                for n, dst in enumerate((qd_t, kd_t)):
                    dve.wait_ge(S("feature_ps"), 4 * t + n + 3)
                    nc.vector.tensor_copy(dst[:].rearrange("p b n -> p (b n)"), high[2 + n][:]).then_inc(S("feature_dve"), 1)
                dve.wait_ge(S("decay_strict"), B * (t + 1))
                for hh in range(H):
                    dve.wait_ge(S("kk_ps"), H * t + hh + 1)
                    for j in range(B):
                        ins = nc.vector.scalar_tensor_tensor(a_mat[:, hh, j, :], low[hh][:, j * P:(j + 1) * P], sm[:, NEG_BETA, j, hh:hh + 1],
                                                             decay_strict[:, j, hh, :], ALU.mult, ALU.mult)
                    ins.then_inc(S("a_mat"), 1)
                for hh in range(H):
                    dve.wait_ge(S("qk_ps"), H * t + hh + 1)
                    nc.vector.tensor_tensor(att[:, hh], high[hh][:].rearrange("p (b n) -> p b n", b=B), decay[:, :, hh, :], ALU.mult).then_inc(S("att"), 1)
                for hh in range(H):
                    dve.wait_ge(S("a_mat"), H * t + hh + 1)
                    wait_apart(dve, S("inv_eye"), H * t + hh + 1)
                    nc.vector.copy_predicated(inv[:, hh], spread(const["merge_low"][:], 1, B), a_mat[:, hh]).then_inc(S("inv0"), 1)
                NL = len(LEVELS)
                for l in range(NL):
                    for hh in range(H):
                        wait_apart(dve, S("merged_ps"), H * NL * t + H * l + hh + 1)
                        nc.vector.copy_predicated(inv_t[:, hh], spread(const["merge"][:, l, :], 1, B),
                                                  high[hh][:].rearrange("p (b n) -> p b n", b=B)).then_inc(S("inv_t"), 1)
                    if l < NL - 1:
                        for hh in range(H // 2, H):
                            dve.wait_ge(S("inv_ps"), H * (NL - 1) * t + H * l + hh + 1)
                            nc.vector.tensor_copy(inv[:, hh].rearrange("p b n -> p (b n)"), low[hh][:]).then_inc(S("inv_dve"), 1)
                for n in range(2):
                    dve.wait_ge(S("k_state_ps"), 2 * t + n + 1)
                    nc.vector.tensor_tensor(rhs[:, 2 * n:2 * n + 2].rearrange("p b h n -> p (b h n)"), low[n][:],
                                            beta_v[:, 2 * n:2 * n + 2].rearrange("p b h n -> p (b h n)"), ALU.add).then_inc(S("rhs"), 1)
                for n in range(2):
                    dve.wait_ge(S("update_ps"), 2 * t + n + 1)
                    nc.vector.tensor_tensor(update[:, 2 * n:2 * n + 2], high[2 + n][:].rearrange("p (b n) -> p b n", b=2),
                                            spread(const["own_head"][:], 1, 2), ALU.mult).then_inc(S("update"), 1)
                dve.wait_ge(S("update"), 2 * (t + 1))
                for j in range(B):
                    ins = nc.vector.scalar_tensor_tensor(state[:, j], state[:, j], small_exp[:, 2 * B * H + j:2 * B * H + j + 1], update[:, j], ALU.mult, ALU.add)
                ins.then_inc(S("state"), 1)
                dve.wait_ge(S("o_sq"), 2 * (t + 1))
                nc.vector.tensor_reduce(o_var[:], o_sq[:], AX.X, ALU.add).then_inc(S("o_sum"), 1)
                dve.wait_ge(S("o_sum"), t + 1)
                nc.vector.tensor_scalar(o_var[:], o_var[:], 1.0 / VD, RMS_EPS, ALU.mult, ALU.add).then_inc(S("o_var"), 1)
                dve.wait_ge(S("o_rn"), t + 1)
                for n in range(2):
                    nc.vector.tensor_tensor(o_norm[:, 2 * n:2 * n + 2].rearrange("p b (h v) -> p (b h) v", h=H), high[n][:].rearrange("p (b v) -> p b v", v=VD),
                                            spread(o_rn[:, 2 * n:2 * n + 2].rearrange("p b h -> p (b h)"), 2, VD), ALU.mult).then_inc(S("o_norm"), 1)
                dve.wait_ge(S("o_norm"), 2 * (t + 1))
                nc.vector.tensor_tensor(o_gated[:], o_norm[:], gate[:], ALU.mult).then_inc(S("o_gated"), 1)
                dve.wait_ge(S("x1_ps"), t + 1)
                nc.vector.tensor_tensor(x1[:].rearrange("p b n -> p (b n)"), low[2][:], y0[:].rearrange("p b n -> p (b n)"), ALU.add).then_inc(S("x1"), 1)
                dve.wait_ge(S("x1"), t + 1)
                mean_and_variance(dve, x1, "ln2", t)
                normalise(dve, z2, x1, "ln2", t)
                dve.wait_ge(S("w2_ps"), t + 1)
                nc.vector.tensor_tensor(pre_gelu[:], low[0][:].rearrange("p (b n) -> p b n", b=B), spread(const["b2"][:], 1, B), ALU.add).then_inc(S("pre_gelu"), 1)
                dve.wait_ge(S("post_gelu"), t + 1)
                dve.wait_ge(S("x_plus"), t + 1)
                nc.vector.tensor_tensor(x_all[:, bass.ds(t * B, B), :], post_gelu[:], x_plus[:], ALU.add).then_inc(S("x_after_delta"), 1)

        @block.tensor
        def _(pe):
            mm, tr = nc.tensor.matmul, nc.tensor.transpose
            eye = const["eye"]
            with pe.Fori(0, STEPS) as t:
                pe.wait_ge(S("h"), t + 1)
                for j in range(B):
                    last = tr(bank[0][:, j * P:(j + 1) * P], h[:, j, :], eye[:])
                last.then_inc(S("h_t_ps"), 1)
                pe.wait_ge(S("h_t"), t + 1)
                h_all = h_t[:].rearrange("p b n -> p (b n)")
                for c in range(CHUNKS):
                    mm(high[c][:], w["w_qkv"][:, c, :], h_all, start=True, stop=True).then_inc(S("proj_ps"), 1)
                pe.wait_ge(S("pre_gelu"), t + 1)
                for j in range(B):
                    mm(low[j][:, 0:GATES], h_t[:, j, :], w["w_gates"][:], start=True, stop=True).then_inc(S("gates_ps"), 1)
                pe.wait_ge(S("conv_act"), CHUNKS * (t + 1))
                for j in range(B):
                    for c in range(CHUNKS):
                        last = tr(high[j][:, c * P:(c + 1) * P], conv_act[:, c, j, :], eye[:])
                    last.then_inc(S("conv_tok_ps"), 1)
                pe.wait_ge(S("g"), t + 1)
                pe.wait_ge(S("gate"), B * (t + 1))
                g_all = sm[:, G].rearrange("p b h -> p (b h)")
                n = B * H
                mm(bank[0][:, 0:n], const["up_to"][:], g_all, start=True, stop=True)
                mm(bank[0][:, n:2 * n], const["after"][:], g_all, start=True, stop=True)
                pe.wait_ge(S("g_wide"), t + 1)
                for j in range(B):
                    last = mm(bank[0][:, 2 * n + j:2 * n + j + 1], g_wide[:, j].rearrange("p h k -> p (h k)"), const["ones"][:, 0:1], start=True, stop=True)
                last.then_inc(S("small_ps"), 1)
                for j in range(B):
                    pe.wait_ge(S("g_masked"), B * t + j + 1)
                    if j == 3:
                        pe.wait_ge(S("decay_raw"), B * t + 1)
                    mm(low[j % 3][:], const["up_to"][:], g_masked[:, j].rearrange("p h n -> p (h n)"), start=True, stop=True).then_inc(S("decay_ps"), 1)
                pe.wait_ge(S("qk"), B * (t + 1))
                pe.wait_ge(S("beta_v"), B * (t + 1))
                for n, (src, tag) in enumerate(((qk[:, :, H:2 * H], "qk"), (qk[:, :, 0:H], "qk"), (q_dec, "q_dec"), (k_dec, "k_dec"))):
                    if n >= 2:
                        pe.wait_ge(S(tag), t + 1)
                    for j in range(B):
                        last = tr(high[n][:, j * P:(j + 1) * P], src[:, j].rearrange("p h k -> p (h k)"), eye[:])
                    last.then_inc(S("feature_ps"), 1)
                pe.wait_ge(S("feature_act"), 2 * (t + 1))
                pe.wait_ge(S("decay_raw"), B * (t + 1))
                pe.wait_ge(S("small_exp"), t + 1)
                for hh in range(H):
                    rows = slice(hh * KD, (hh + 1) * KD)
                    for j in range(B):
                        last = mm(low[hh][:, j * P:(j + 1) * P], k_t[rows, j, :], k_t[rows, j, :], start=True, stop=True, tile_position=(hh * KD, 0))
                    last.then_inc(S("kk_ps"), 1)
                pe.wait_ge(S("feature_dve"), 2 * (t + 1))
                for hh in range(H):
                    rows = slice(hh * KD, (hh + 1) * KD)
                    for j in range(B):
                        last = mm(high[hh][:, j * P:(j + 1) * P], q_t[rows, j, :], k_t[rows, j, :], start=True, stop=True, tile_position=(hh * KD, 0))
                    last.then_inc(S("qk_ps"), 1)
                for hh in range(H):
                    pe.wait_ge(S("att"), H * t + hh + 1)
                    for j in range(B):
                        last = tr(low[hh][:, j * P:(j + 1) * P], att[:, hh, j, :], eye[:])
                    last.then_inc(S("att_t_ps"), 1)
                for hh in range(H):
                    pe.wait_ge(S("inv0"), H * t + hh + 1)
                    for j in range(B):
                        last = tr(high[hh][:, j * P:(j + 1) * P], inv[:, hh, j, :], eye[:])
                    last.then_inc(S("inv_t0_ps"), 1)
                NL = len(LEVELS)
                for l in range(NL):
                    for hh in range(H):
                        if l == 0:
                            pe.wait_ge(S("inv_t0"), H * t + hh + 1)
                            pe.wait_ge(S("att_t"), H * t + hh + 1)
                        elif hh < H // 2:
                            pe.wait_ge(S("inv_act"), (H // 2) * ((NL - 1) * t + l - 1) + hh + 1)
                        else:
                            pe.wait_ge(S("inv_dve"), (H // 2) * ((NL - 1) * t + l - 1) + hh - H // 2 + 1)
                        for j in range(B):
                            last = mm(low[hh][:, j * P:(j + 1) * P], a_mat[:, hh, j, :], inv_t[:, hh, j, :], start=True, stop=True)
                        last.then_inc(S("prod_ps"), 1)
                    for hh in range(H):
                        pe.wait_ge(S("prod"), H * NL * t + H * l + hh + 1)
                        for j in range(B):
                            last = mm(high[hh][:, j * P:(j + 1) * P], inv[:, hh, j, :], prod[:, hh, j, :], start=True, stop=True)
                        last.then_inc(S("merged_ps"), 1)
                    if l < NL - 1:
                        for hh in range(H):
                            pe.wait_ge(S("inv_t"), H * NL * t + H * l + hh + 1)
                            for j in range(B):
                                last = tr(low[hh][:, j * P:(j + 1) * P], inv_t[:, hh, j, :], eye[:])
                            last.then_inc(S("inv_ps"), 1)
                pe.wait_ge(S("state"), t + 1)
                for n in range(2):
                    for jj in range(2):
                        j = 2 * n + jj
                        last = mm(low[n][:, jj * VALS:(jj + 1) * VALS], kd_t[:, j, :], state[:, j], start=True, stop=True)
                    last.then_inc(S("k_state_ps"), 1)
                for n in range(2):
                    pe.wait_ge(S("rhs"), 2 * t + n + 1)
                    if n == 0:
                        pe.wait_ge(S("inv_t"), H * NL * (t + 1))
                    for jj in range(2):
                        for hh in range(H):
                            j = 2 * n + jj
                            c = (jj * H + hh) * VD
                            last = mm(low[2 + n][:, c:c + VD], inv_t[:, hh, j, :], rhs[:, j, hh, :], start=True, stop=True)
                    last.then_inc(S("delta_ps"), 1)
                for n in range(2):
                    pe.wait_ge(S("delta"), 2 * t + n + 1)
                    for jj in range(2):
                        j = 2 * n + jj
                        c = jj * VALS
                        mm(high[n][:, c:c + VALS], qd_t[:, j, :], state[:, j], start=True, stop=False)
                        for hh in range(H):
                            last = mm(high[n][:, c + hh * VD:c + (hh + 1) * VD], att_t[:, hh, j, :], delta[:, j, hh, :], start=False, stop=hh == H - 1)
                    last.then_inc(S("o_ps"), 1)
                pe.wait_ge(S("k_end"), t + 1)
                for n in range(2):
                    for jj in range(2):
                        j = 2 * n + jj
                        last = mm(high[2 + n][:, jj * VALS:(jj + 1) * VALS], k_end[:, j].rearrange("p h k -> p (h k)"),
                                  delta[:, j].rearrange("p h v -> p (h v)"), start=True, stop=True)
                    last.then_inc(S("update_ps"), 1)
                pe.wait_ge(S("o_gated"), t + 1)
                for n in range(2):
                    for j in range(B):
                        last = tr(low[n][:, j * P:(j + 1) * P], o_gated[:, j, n * P:(n + 1) * P], eye[:])
                    last.then_inc(S("o_t_ps"), 1)
                pe.wait_ge(S("o_t"), 2 * (t + 1))
                for j in range(B):
                    for n in range(2):
                        last = mm(low[2][:, j * P:(j + 1) * P], o_t[:, n, j, :], w["w_o"][:, n, :], start=n == 0, stop=n == 1)
                last.then_inc(S("x1_ps"), 1)
                pe.wait_ge(S("ln2"), t + 1)
                for j in range(B):
                    last = tr(bank[0][:, j * P:(j + 1) * P], z2[:, j, :], eye[:])
                last.then_inc(S("z2_t_ps"), 1)
                pe.wait_ge(S("z2_t"), t + 1)
                for j in range(B):
                    last = mm(low[0][:, j * P:(j + 1) * P], z2_t[:, j, :], w["w_2"][:], start=True, stop=True)
                last.then_inc(S("w2_ps"), 1)


def inverse_root(nc, pool, S, const, dst, src, n, ready, done, t):
    pool.wait_ge(S(ready), t + 1)
    nc.gpsimd.tensor_tensor(dst, src, const["minus_half"][:, 0:n], ALU.pow).then_inc(S(done), 1)


def token_layers(nc, x_all, y_all, over_all, onehot_all, expert_all, const, w, psum):
    with ExitStack() as ctx:
        def sb(name, shape, dt=F32):
            return ctx.enter_context(nc.sbuf_tensor(name, shape, dt))

        S = named_signals(nc, ctx, "tokens_")
        bank = psum
        y = sb("m_y", [P, B, D])
        y_t = sb("m_y_t", [P, B, P])
        stats = sb("m_stats", [P, B, 6])
        mean_var = sb("m_mean_var", [P, B, 2])
        var_eps = sb("m_var_eps", [P, B])
        rstd = sb("m_rstd", [P, B])
        logits = sb("m_logits", [P, B, E])
        top = sb("m_top", [P, B, E])
        top_at = sb("m_top_at", [P, B, E], U32)
        top_at_f = sb("m_top_at_f", [P, B, E])
        pick = sb("m_pick", [P, 3, B, E])
        shifted = sb("m_shifted", [P, B, E])
        exp_l = sb("m_exp_l", [P, B, E])
        kept = sb("m_kept", [P, B, E])
        kept_sum = sb("m_kept_sum", [P, B])
        kept_inv = sb("m_kept_inv", [P, B])
        weight = sb("m_weight", [P, B, E])
        act_gate = sb("m_act_gate", [P, NETBANKS, F])
        hidden = sb("m_hidden", [P, 2, NETS * F])
        hidden_t = sb("m_hidden_t", [P, 2, 4, P])
        z = sb("m_z", [P, B, D])
        z_t = sb("m_z_t", [P, B, P])
        latent = sb("m_latent", [LATENT, B * P])
        qk = sb("m_qk", [P, B, 2, 2, D // 2])
        v_new = sb("m_v_new", [P, B, HD, HEADS])
        v = sb("m_v", [P, B, HD, HEADS])
        by_cos = sb("m_by_cos", [P, B * 2, 2, D // 2])
        by_sin = sb("m_by_sin", [P, B * 2, 2, D // 2])
        turned = sb("m_turned", [P, B * 2, HEADS, HD])
        qk_prod = sb("m_qk_prod", [P, 2, HEADS, HEADS, HD])
        pv_prod = sb("m_pv_prod", [P, HEADS, HD, HEADS])
        score = sb("m_score", [P, B, HEADS, HEADS])
        score_max = sb("m_score_max", [P, B, HEADS])
        probs = sb("m_probs", [P, B, HEADS, HEADS])
        prob_sum = sb("m_prob_sum", [P, B, HEADS])
        prob_inv = sb("m_prob_inv", [P, B, HEADS])
        mixed = sb("m_mixed", [P, B, HEADS, HD])
        att_out = sb("m_att_out", [P, B, D])
        att_out_t = sb("m_att_out_t", [P, B, P])
        y3 = sb("m_y3", [P, B, D])
        y3_t = sb("m_y3_t", [P, B, P])
        over_h = sb("m_over_h", [P, 4, B * P])
        r_logits = sb("m_r_logits", [P, B, E])
        r_top = sb("m_r_top", [P, B, E])
        r_at = sb("m_r_at", [P, B, E], U32)

        block = ctx.enter_context(nc.Block())
        flat = lambda ap: ap.rearrange("p b n -> p (b n)")
        tiles = lambda t: bass.ds(t * B, B)
        tile_of = lambda t, j: x_all[:, bass.ds(t * B + j, 1), :].rearrange("p a d -> p (a d)")
        net_bank = lambda n: bank[1 + n % NETBANKS]

        def wait_apart(engine, semaphore, value):
            engine.wait_ge(semaphore, value)
            engine.sem_inc(S("waited_apart"), 1)

        def all_steps(engine, body):
            body(0, None, None, None)
            body(1, 0, None, None)
            body(2, 1, 0, None)
            with engine.Fori(2, STEPS - 1) as t:
                body(t + 1, t, t - 1, t - 2)
            body(None, STEPS - 1, STEPS - 2, STEPS - 3)
            body(None, None, STEPS - 1, STEPS - 2)
            body(None, None, None, STEPS - 1)

        def layernorm(dve, dst, src, tag, t):
            for j in range(B):
                last = nc.vector.bn_stats(stats[:, j, :], src(j))
            last.then_inc(S(tag + "_stats"), 1)
            wait_apart(dve, S(tag + "_stats"), t + 1)
            for j in range(B):
                last = nc.vector.bn_aggr(mean_var[:, j, :], stats[:, j, :])
            last.then_inc(S(tag + "_aggr"), 1)
            dve.wait_ge(S(tag + "_aggr"), t + 1)
            nc.vector.tensor_scalar(var_eps[:], mean_var[:, :, 1], LN_EPS, None, ALU.add).then_inc(S(tag + "_var"), 1)
            dve.wait_ge(S(tag + "_rstd"), t + 1)
            for j in range(B):
                last = nc.vector.tensor_scalar(dst[:, j, :], src(j), mean_var[:, j, 0:1], rstd[:, j:j + 1],
                                               ALU.subtract, ALU.mult)
            last.then_inc(S(tag), 1)

        @block.gpsimd
        def _(pool):
            def body(head, nets, scores, output):
                if scores is not None:
                    t = scores
                    inverse_root(nc, pool, S, const, rstd[:], var_eps[:], B, "ln4_var", "ln4_rstd", t)
                    pool.wait_ge(S("ln4"), t + 1)
                    nc.gpsimd.tensor_tensor(x_all[:, tiles(t), :], x_all[:, tiles(t), :], spread(const["bout"][:], 1, B), ALU.add).then_inc(S("x2_bias"), 1)
                if head is not None:
                    inverse_root(nc, pool, S, const, rstd[:], var_eps[:], B, "ln3_var", "ln3_rstd", head)
                if scores is not None:
                    pool.wait_ge(S("qkv"), 3 * (t + 1))
                    parts = qk[:].rearrange("p b q s n -> p (b q s) n")
                    nc.gpsimd.tensor_tensor(by_cos[:].rearrange("p b s n -> p (b s) n"), parts,
                                            const["cos"][:, bass.ds(t, 1), :].to_broadcast([P, B * 4, D // 2]), ALU.mult).then_inc(S("by_cos"), 1)
                    nc.gpsimd.tensor_tensor(by_sin[:].rearrange("p b s n -> p (b s) n"), parts,
                                            const["sin"][:, bass.ds(t, 1), :].to_broadcast([P, B * 4, D // 2]), ALU.mult).then_inc(S("by_sin"), 1)
                    pool.wait_ge(S("by_cos"), t + 1)
                    pool.wait_ge(S("by_sin"), t + 1)
                    quads = lambda ap: ap.rearrange("p b (h d) -> p b h d", h=HEADS)
                    nc.gpsimd.tensor_tensor(turned[:, :, :, 0:HD // 2], quads(by_cos[:, :, 0, :]), quads(by_sin[:, :, 1, :]), ALU.subtract).then_inc(S("turned"), 1)
                    nc.gpsimd.tensor_tensor(turned[:, :, :, HD // 2:], quads(by_sin[:, :, 0, :]), quads(by_cos[:, :, 1, :]), ALU.add).then_inc(S("turned"), 1)
                    pool.wait_ge(S("turned"), 2 * (t + 1))
                for j in range(B):
                    if scores is not None:
                        pool.wait_ge(S("score"), B * t + j + 1)
                        nc.gpsimd.tensor_tensor(qk_prod[:, j % 2], spread(turned[:, 2 * j], 2, HEADS), spread(turned[:, 2 * j + 1], 1, HEADS), ALU.mult).then_inc(S("qk_prod"), 1)
                    if j == 1 and output is not None:
                        inverse_root(nc, pool, S, const, rstd[:], var_eps[:], B, "ln5_var", "ln5_rstd", output)
                        wait_apart(pool, S("ln5"), output + 1)
                        nc.gpsimd.tensor_copy(y_all[:, tiles(output), :], y3[:]).then_inc(S("y_kept"), 1)
                if scores is not None:
                    if output is not None:
                        wait_apart(pool, S("mixed"), B * (output + 1))
                    nc.gpsimd.tensor_copy(v[:], v_new[:]).then_inc(S("v"), 1)

            all_steps(pool, body)

        @block.scalar
        def _(act):
            def turned_copy(dst, src, ready, done, t):
                act.wait_ge(S(ready), t + 1)
                nc.scalar.activation(flat(dst[:]), src[:], ACT.Copy).then_inc(S(done), 1)

            def body(head, nets, scores, output):
                for j in range(B + 1):
                    for e in range(NETS):
                        if j < B and nets is not None:
                            n = j * NETS + e
                            act.wait_ge(S("gate_up_ps"), B * NETS * nets + n + 1)
                            nc.scalar.activation(act_gate[:, n % NETBANKS], net_bank(n)[:, 0:F], ACT.Silu).then_inc(S("act_gate"), 1)
                        if scores is not None and (j, e) == (0, 3):
                            turned_copy(z_t, bank[0], "z_t_ps", "z_t", scores)
                        if scores is not None and (j, e) == (0, 7):
                            act.wait_ge(S("latent_ps"), scores + 1)
                            nc.scalar.activation(latent[:], bank[7][0:LATENT, :], ACT.Identity, bias=const["bdown"][:]).then_inc(S("latent"), 1)
                        if output is not None and (j, e) == (2, 2):
                            turned_copy(att_out_t, bank[7], "att_out_t_ps", "att_out_t", output)
                        if output is not None and (j, e) == (3, 3):
                            turned_copy(y3_t, bank[0], "y3_t_ps", "y3_t", output)
                    if j == B and head is not None:
                        turned_copy(y_t, bank[7], "y_t_ps", "y_t", head)
                    for g in range(GROUPS):
                        if j and nets is not None:
                            act.wait_ge(S("hidden_t_ps"), GROUPS * (B * nets + j - 1) + g + 1)
                            n_chunks = min(4, CHUNKS_F - 4 * g)
                            nc.scalar.activation(flat(hidden_t[:, g % 2, 0:n_chunks, :]), bank[4 + g % 2][:, 0:n_chunks * P], ACT.Copy).then_inc(S("hidden_t"), 1)
                        if j == B and output is not None:
                            act.wait_ge(S("over_h_ps"), 4 * output + g + 1)
                            nc.scalar.activation(over_h[:, g, :], bank[7 if g == 3 else 0][:], ACT.Relu, bias=const["ob1"][:, g:g + 1]).then_inc(S("over_h"), 1)
                if head is not None:
                    act.wait_ge(S("shifted"), head + 1)
                    nc.scalar.activation(exp_l[:], shifted[:], ACT.Exp).then_inc(S("exp_l"), 1)
                if scores is not None:
                    act.wait_ge(S("centred"), scores + 1)
                    nc.scalar.activation(probs[:], score[:], ACT.Exp, scale=float(HD) ** -0.5).then_inc(S("probs"), 1)

            all_steps(act, body)

        @block.vector
        def _(dve):
            def route(t):
                dve.wait_ge(S("logits_ps"), t + 1)
                nc.vector.tensor_copy(logits[:].rearrange("p b e -> p (b e)"), bank[7][:, 0:B * E]).then_inc(S("logits"), 1)
                wait_apart(dve, S("logits"), t + 1)
                for j in range(B):
                    last = nc.vector.max(top[:, j, :], logits[:, j, :])
                last.then_inc(S("top"), 1)
                wait_apart(dve, S("top"), t + 1)
                nc.vector.tensor_tensor(shifted[:], logits[:], spread(top[:, :, 0], 2, E), ALU.subtract).then_inc(S("shifted"), 1)
                for j in range(B):
                    last = nc.vector.max_index(top_at[:, j, :], top[:, j, :], logits[:, j, :])
                last.then_inc(S("top_at"), 1)
                dve.wait_ge(S("top_at"), t + 1)
                nc.vector.tensor_copy(top_at_f[:], top_at[:]).then_inc(S("top_at_f"), 1)
                dve.wait_ge(S("top_at_f"), t + 1)
                for k in range(2):
                    last = nc.vector.tensor_tensor(pick[:, k], spread(const["expert_ids"][:], 1, B), spread(top_at_f[:, :, k], 2, E), ALU.is_equal)
                last.then_inc(S("pick"), 1)
                dve.wait_ge(S("pick"), t + 1)
                nc.vector.tensor_tensor(pick[:, 2], pick[:, 0], pick[:, 1], ALU.add).then_inc(S("picked"), 1)
                dve.wait_ge(S("picked"), t + 1)
                dve.wait_ge(S("exp_l"), t + 1)
                nc.vector.tensor_tensor(kept[:], pick[:, 2], exp_l[:], ALU.mult).then_inc(S("kept"), 1)
                dve.wait_ge(S("kept"), t + 1)
                nc.vector.tensor_reduce(kept_sum[:], kept[:], AX.X, ALU.add).then_inc(S("kept_sum"), 1)
                dve.wait_ge(S("kept_sum"), t + 1)
                nc.vector.reciprocal(kept_inv[:], kept_sum[:]).then_inc(S("kept_inv"), 1)
                dve.wait_ge(S("kept_inv"), t + 1)
                nc.vector.tensor_tensor(weight[:], kept[:], spread(kept_inv[:], 2, E), ALU.mult).then_inc(S("weight"), 1)
                dve.wait_ge(S("weight"), t + 1)

            def values_times_probs(t, j):
                if j == 0:
                    dve.wait_ge(S("probs"), t + 1)
                    dve.wait_ge(S("v"), t + 1)
                    nc.vector.tensor_reduce(prob_sum[:], probs[:], AX.X, ALU.add).then_inc(S("prob_sum"), 1)
                else:
                    dve.wait_ge(S("mixed"), B * t + j)
                nc.vector.tensor_tensor(pv_prod[:], spread(probs[:, j], 2, HD), spread(v[:, j], 1, HEADS), ALU.mult).then_inc(S("pv_prod"), 1)

            def mix(t, j):
                dve.wait_ge(S("pv_prod"), B * t + j + 1)
                nc.vector.tensor_reduce(mixed[:, j], pv_prod[:], AX.X, ALU.add).then_inc(S("mixed"), 1)
                if j == B - 1:
                    dve.wait_ge(S("prob_sum"), t + 1)
                    nc.vector.reciprocal(prob_inv[:], prob_sum[:]).then_inc(S("prob_inv"), 1)
                    dve.wait_ge(S("prob_inv"), t + 1)
                    dve.wait_ge(S("mixed"), B * (t + 1))
                    nc.vector.tensor_tensor(att_out[:].rearrange("p b (h d) -> p (b h) d", h=HEADS), mixed[:].rearrange("p b h d -> p (b h) d"),
                                            spread(prob_inv[:].rearrange("p b h -> p (b h)"), 2, HD), ALU.mult).then_inc(S("att_out"), 1)

            def add_q_bias(t):
                dve.wait_ge(S("q_ps"), t + 1)
                nc.vector.tensor_tensor(qk[:, :, 0].rearrange("p b s n -> p b (s n)"), bank[0][:].rearrange("p (b n) -> p b n", b=B),
                                        spread(const["bq"][:], 1, B), ALU.add).then_inc(S("qkv"), 1)

            def add_kv_bias(t):
                for n in range(2):
                    dve.wait_ge(S("kv_ps"), 2 * t + n + 1)
                    src = bank[0 if n else 7][:].rearrange("p (b n) -> p b n", b=2)
                    nc.vector.tensor_tensor(qk[:, 2 * n:2 * n + 2, 1].rearrange("p b s n -> p b (s n)"), src[:, :, 0:D], spread(const["bup"][:, 0:D], 1, 2), ALU.add)
                    nc.vector.tensor_tensor(v_new[:, 2 * n:2 * n + 2].rearrange("p b d h -> p b (d h)"), src[:, :, D:2 * D], spread(const["bup"][:, D:2 * D], 1, 2), ALU.add).then_inc(S("qkv"), 1)

            def sum_score(t, j):
                dve.wait_ge(S("qk_prod"), B * t + j + 1)
                nc.vector.tensor_reduce(score[:, j], qk_prod[:, j % 2], AX.X, ALU.add).then_inc(S("score"), 1)

            def centre(t):
                dve.wait_ge(S("score"), B * (t + 1) + 2)
                nc.vector.tensor_reduce(score_max[:], score[:], AX.X, ALU.max).then_inc(S("score_max"), 1)
                dve.wait_ge(S("score_max"), t + 1)
                merged = lambda ap: ap.rearrange("p b h g -> p (b h) g")
                nc.vector.tensor_tensor(merged(score[:]), merged(score[:]), spread(score_max[:].rearrange("p b h -> p (b h)"), 2, HEADS), ALU.subtract).then_inc(S("centred"), 1)

            def third_norm(t):
                dve.wait_ge(S("x2_bias"), t + 1)
                dve.wait_ge(S("wout_ps"), t + 1)
                nc.vector.tensor_tensor(x_all[:, tiles(t), :], bank[0][:].rearrange("p (b n) -> p b n", b=B), x_all[:, tiles(t), :], ALU.add).then_inc(S("x3"), 1)
                wait_apart(dve, S("x3"), t + 1)
                layernorm(dve, y3, lambda j: tile_of(t, j), "ln5", t)

            def choose(t):
                dve.wait_ge(S("r_logits_ps"), t + 1)
                nc.vector.tensor_tensor(r_logits[:], bank[7][:, 0:B * E].rearrange("p (b e) -> p b e", b=B), spread(const["router_b"][:], 1, B), ALU.add).then_inc(S("r_logits"), 1)
                wait_apart(dve, S("r_logits"), t + 1)
                for j in range(B):
                    last = nc.vector.max(r_top[:, j, :], r_logits[:, j, :])
                last.then_inc(S("r_top"), 1)
                wait_apart(dve, S("r_top"), t + 1)
                for j in range(B):
                    last = nc.vector.max_index(r_at[:, j, :], r_top[:, j, :], r_logits[:, j, :])
                last.then_inc(S("r_at"), 1)
                wait_apart(dve, S("r_at"), t + 1)
                nc.vector.tensor_copy(expert_all[:, tiles(t)], r_at[:, :, 0]).then_inc(S("expert"), 1)
                dve.wait_ge(S("expert"), t + 1)
                nc.vector.tensor_tensor(onehot_all[:, tiles(t), :], spread(const["expert_ids"][:], 1, B), spread(expert_all[:, tiles(t)], 2, E), ALU.is_equal).then_inc(S("onehot"), 1)

            def body(head, nets, scores, output):
                if scores is not None:
                    wait_apart(dve, S("x2"), scores + 1)
                    layernorm(dve, z, lambda j: tile_of(scores, j), "ln4", scores)
                for j in range(B + 1):
                    for e in range(NETS):
                        if nets is not None and j < B:
                            n = j * NETS + e
                            dve.wait_ge(S("act_gate"), B * NETS * nets + n + 1)
                            out = hidden[:, j % 2, e * F:(e + 1) * F]
                            up = net_bank(n)[:, F:2 * F]
                            if e < E:
                                ins = nc.vector.scalar_tensor_tensor(out, up, weight[:, j, e:e + 1], act_gate[:, n % NETBANKS], ALU.mult, ALU.mult)
                            else:
                                ins = nc.vector.tensor_tensor(out, up, act_gate[:, n % NETBANKS], ALU.mult)
                            ins.then_inc(S("hidden"), 1)
                        if output is not None and j < 2 and e in (1, 6):
                            values_times_probs(output, 2 * j + e // 5)
                        if output is not None and j < 2 and e in (3, 9):
                            mix(output, 2 * j + e // 5)
                        if scores is not None and (j, e) == (0, 8):
                            add_q_bias(scores)
                        if scores is not None and (j, e) == (1, 4):
                            add_kv_bias(scores)
                        if output is not None and (j, e) == (2, 5):
                            third_norm(output)
                        if scores is not None and (j, e) in ((2, 8), (3, 2), (3, 6)):
                            sum_score(scores, {8: 0, 2: 1, 6: 2}[e])
                        if output is not None and (j, e) == (3, 8):
                            choose(output)
                        if head is not None and (j, e) == (2, 1):
                            layernorm(dve, y, lambda j: tile_of(head, j), "ln3", head)
                if head is not None:
                    route(head)
                if nets is not None:
                    dve.wait_ge(S("mixture_ps"), B * (nets + 1))
                    nc.vector.tensor_tensor(x_all[:, tiles(nets), :], bank[6][:].rearrange("p (b n) -> p b n", b=B), x_all[:, tiles(nets), :], ALU.add).then_inc(S("x2"), 1)
                if scores is not None:
                    sum_score(scores, 3)
                    centre(scores)
                if output is not None:
                    dve.wait_ge(S("over_ps"), output + 1)
                    nc.vector.tensor_tensor(over_all[:, tiles(output), :], bank[0][:].rearrange("p (b n) -> p b n", b=B), spread(const["ob2"][:], 1, B), ALU.add).then_inc(S("over"), 1)

            dve.sem_inc(S("hidden"), NETBANKS)
            dve.sem_inc(S("score"), 2)
            all_steps(dve, body)

        @block.tensor
        def _(pe):
            mm, tr = nc.tensor.matmul, nc.tensor.transpose
            eye = const["eye"]

            def turn(dst, src, ready, done, t):
                pe.wait_ge(S(ready), t + 1)
                for j in range(B):
                    last = tr(dst[:, j * P:(j + 1) * P], src[:, j, :], eye[:])
                last.then_inc(S(done), 1)

            def times(dst, src_t, weights, width, ready, done, t):
                pe.wait_ge(S(ready), t + 1)
                for j in range(B):
                    last = mm(dst[:, j * width:(j + 1) * width], src_t[:, j, :], weights[:], start=True, stop=True)
                last.then_inc(S(done), 1)

            def keys_and_values(t):
                pe.wait_ge(S("latent"), t + 1)
                for n in range(2):
                    if n:
                        pe.wait_ge(S("qkv"), 3 * t + 1)
                    for jj in range(2):
                        j = 2 * n + jj
                        last = mm(bank[0 if n else 7][:, jj * 2 * D:(jj + 1) * 2 * D], latent[:, j * P:(j + 1) * P], w["wup"][:], start=True, stop=True)
                    last.then_inc(S("kv_ps"), 1)

            def overflow_hidden(t, c):
                mm(bank[7 if c == 3 else 0][:], w["ow1"][:, c * P:(c + 1) * P], flat(y3_t[:]), start=True, stop=True).then_inc(S("over_h_ps"), 1)

            def down(nets, i, g):
                pe.wait_ge(S("hidden_t"), GROUPS * (B * nets + i) + g + 1)
                for c in range(4 * g, min(4 * g + 4, CHUNKS_F)):
                    rows = min(P, NETS * F - c * P)
                    last = mm(bank[6][:, i * P:(i + 1) * P], hidden_t[0:rows, g % 2, c % 4, :], w["down"][0:rows, c, :], start=c == 0, stop=c == CHUNKS_F - 1)
                return last

            def body(head, nets, scores, output):
                for j in range(B + 1):
                    for e in range(NETS):
                        if nets is not None and j < B:
                            n = j * NETS + e
                            pe.wait_ge(S("hidden"), B * NETS * nets + n + 1)
                            mm(net_bank(n)[:, 0:2 * F], y_t[:, j, :], w["gate_up"][:, e, :], start=True, stop=True).then_inc(S("gate_up_ps"), 1)
                        if scores is not None and (j, e) == (0, 3):
                            turn(bank[0], z, "ln4", "z_t_ps", scores)
                        if scores is not None and (j, e) == (0, 6):
                            pe.wait_ge(S("z_t"), scores + 1)
                            mm(bank[7][0:LATENT, :], w["wdown"][:], flat(z_t[:]), start=True, stop=True).then_inc(S("latent_ps"), 1)
                            times(bank[0], z_t, w["wq"], D, "z_t", "q_ps", scores)
                        if scores is not None and (j, e) == (1, 2):
                            keys_and_values(scores)
                        if output is not None and (j, e) == (2, 1):
                            if scores is not None:
                                pe.wait_ge(S("qkv"), 3 * (scores + 1))
                            turn(bank[7], att_out, "att_out", "att_out_t_ps", output)
                        if output is not None and (j, e) == (2, 4):
                            times(bank[0], att_out_t, w["wout"], D, "att_out_t", "wout_ps", output)
                        if output is not None and (j, e) == (3, 2):
                            turn(bank[0], y3, "ln5", "y3_t_ps", output)
                        if output is not None and (j, e) == (3, 6):
                            times(bank[7], y3_t, w["router_w"], E, "y3_t", "r_logits_ps", output)
                        if output is not None and (j, e) == (3, 9):
                            overflow_hidden(output, 0)
                    if j == B and head is not None:
                        if output is not None:
                            pe.wait_ge(S("r_logits"), output + 1)
                        turn(bank[7], y, "ln3", "y_t_ps", head)
                    for g in range(GROUPS + 1):
                        if nets is not None and j:
                            if g == 0:
                                pe.wait_ge(S("hidden"), B * NETS * nets + NETS * j + NETBANKS)
                            if g < GROUPS:
                                for c in range(4 * g, min(4 * g + 4, CHUNKS_F)):
                                    cols = min(P, NETS * F - c * P)
                                    last = tr(bank[4 + g % 2][0:cols, c % 4 * P:(c % 4 + 1) * P], hidden[:, (j - 1) % 2, c * P:c * P + cols], eye[:])
                                last.then_inc(S("hidden_t_ps"), 1)
                            if g > 0:
                                last = down(nets, j - 1, g - 1)
                                if g == GROUPS:
                                    last.then_inc(S("mixture_ps"), 1)
                        if j == B and g == 1 and head is not None:
                            times(bank[7], y_t, w["gate_w"], E, "y_t", "logits_ps", head)
                        if j == B and output is not None and 1 <= g <= 3:
                            pe.wait_ge(S("over_h"), 4 * output + g - (g == 3))
                            if g == 3:
                                if head is not None:
                                    pe.wait_ge(S("logits"), head + 1)
                                else:
                                    pe.wait_ge(S("r_logits"), output + 1)
                            overflow_hidden(output, g)
                if output is not None:
                    pe.wait_ge(S("over_h"), 4 * (output + 1))
                    for j in range(B):
                        for c in range(4):
                            last = mm(bank[0][:, j * P:(j + 1) * P], over_h[:, c, j * P:(j + 1) * P], w["ow2"][:, c, :], start=c == 0, stop=c == 3)
                    last.then_inc(S("over_ps"), 1)

            all_steps(pe, body)


def capacity_layer(nc, x_all, y_all, over_all, onehot_all, expert_all, const, w, psum, slots_in, slots_out, out_dram):
    with ExitStack() as ctx:
        def sb(name, shape, dt=F32):
            return ctx.enter_context(nc.sbuf_tensor(name, shape, dt))

        S = named_signals(nc, ctx, "capacity_")
        bank = psum
        n_slots = E * CAP
        blocks = n_slots // P
        zeros = sb("c_zeros", [P, n_slots // P, D])
        totals = sb("c_totals", [P, E, B, STEPS])
        running = sb("c_running", [P, E, B * STEPS])
        before = sb("c_before", [P, E, B, STEPS])
        place = sb("c_place", [P, STEPS, B, E])
        own = sb("c_own", [P, TILES, E])
        rank = sb("c_rank", [P, TILES])
        late = sb("c_late", [P, TILES])
        slot_f = sb("c_slot_f", [P, 2, TILES])
        slot = sb("c_slot", [P, TILES], U32)
        rows = sb("c_rows", [P, blocks, D])
        rows_t = sb("c_rows_t", [P, n_slots])
        hidden = sb("c_hidden", [P, 2, 4, CAP])
        y_t = sb("c_y_t", [P, n_slots])
        y_rows = sb("c_y_rows", [P, blocks, D])
        taken = sb("c_taken", [P, TILES, D])
        late_sum = sb("c_late_sum", [P, TILES, D])
        result = y_all
        block = ctx.enter_context(nc.Block())

        @block.sync
        def _(sp):
            sp.wait_ge(S("zeros"), 1)
            sp.dma_start(slots_in.rearrange("(c p) d -> p c d", p=P), zeros[:]).then_inc(S("slots_zeroed"), 16)
            sp.wait_ge(S("scattered"), 16 * TILES)
            sp.dma_start(rows[:], slots_in.rearrange("(c p) d -> p c d", p=P)).then_inc(S("rows"), 16)
            sp.wait_ge(S("y_rows"), 3)
            sp.dma_start(slots_out.rearrange("(c p) d -> p c d", p=P), y_rows[:]).then_inc(S("slots_done"), 16)
            for t in range(STEPS):
                sp.wait_ge(S("result"), t + 1)
                sp.dma_start(out_dram[t], result[:, t * B:(t + 1) * B, :]).then_inc(S("stored"), 16)
            sp.wait_ge(S("stored"), 16 * STEPS)

        @block.gpsimd
        def _(pool):
            nc.gpsimd.memset(zeros[:], 0.0).then_inc(S("zeros"), 1)
            nc.gpsimd.memset(taken[:], 0.0).then_inc(S("taken_zeroed"), 1)
            pool.wait_ge(S("slots_zeroed"), 16)
            pool.wait_ge(S("slot"), 1)
            for n in range(TILES):
                pool.indirect_dma_start(out=slots_in, out_offset=bass.IndirectOffsetOnAxis(slot[:, n:n + 1], 0), in_=y_all[:, n, :], in_offset=None,
                                        bounds_check=n_slots - 1, oob_is_err=False).then_inc(S("scattered"), 16)
            pool.wait_ge(S("slots_done"), 16)
            pool.wait_ge(S("taken_zeroed"), 1)
            for n in range(TILES):
                pool.indirect_dma_start(out=taken[:, n, :], out_offset=None, in_=slots_out, in_offset=bass.IndirectOffsetOnAxis(slot[:, n:n + 1], 0),
                                        bounds_check=n_slots - 1, oob_is_err=False).then_inc(S("taken"), 16)

        @block.vector
        def _(dve):
            counts = lambda ap: ap.rearrange("p (t b e) -> p t b e", t=STEPS, b=B)
            in_order = lambda ap: ap.rearrange("p e b t -> p t b e")
            dve.wait_ge(S("count_ps"), 2)
            for b in range(B):
                last = nc.vector.tensor_copy(totals[:, :, b, :].rearrange("p e t -> p t e"), counts(bank[1][:, 0:TILES * E])[:, :, b, :])
            last.then_inc(S("totals"), 1)
            dve.wait_ge(S("totals"), 1)
            for e in range(E):
                flat_e = totals[:, e].rearrange("p b t -> p (b t)")
                last = nc.vector.tensor_tensor_scan(running[:, e, :], const["ones"][:, 0:TILES], flat_e, 0.0, ALU.mult, ALU.add)
            last.then_inc(S("running"), 1)
            dve.wait_ge(S("running"), 1)
            nc.vector.tensor_tensor(before[:].rearrange("p e b t -> p (e b t)"), running[:].rearrange("p e n -> p (e n)"),
                                    totals[:].rearrange("p e b t -> p (e b t)"), ALU.subtract).then_inc(S("before"), 1)
            dve.wait_ge(S("before"), 1)
            nc.vector.tensor_tensor(place[:], counts(bank[0][:, 0:TILES * E]), in_order(before[:]), ALU.add).then_inc(S("place"), 1)
            dve.wait_ge(S("place"), 1)
            nc.vector.tensor_tensor(own[:], place[:].rearrange("p t b e -> p (t b) e"), onehot_all[:], ALU.mult).then_inc(S("own"), 1)
            dve.wait_ge(S("own"), 1)
            nc.vector.tensor_reduce(rank[:], own[:], AX.X, ALU.add).then_inc(S("rank"), 1)
            dve.wait_ge(S("rank"), 1)
            nc.vector.tensor_scalar(late[:], rank[:], float(CAP), None, ALU.is_gt).then_inc(S("late"), 1)
            nc.vector.scalar_tensor_tensor(slot_f[:, 0], expert_all[:], float(CAP), rank[:], ALU.mult, ALU.add).then_inc(S("slot_raw"), 1)
            dve.wait_ge(S("late"), 1)
            dve.wait_ge(S("slot_raw"), 1)
            nc.vector.scalar_tensor_tensor(slot_f[:, 1], late[:], float(4 * E * T), slot_f[:, 0], ALU.mult, ALU.add).then_inc(S("slot_f"), 1)
            dve.wait_ge(S("slot_f"), 1)
            nc.vector.tensor_scalar(slot[:], slot_f[:, 1], -1.0, None, ALU.add).then_inc(S("slot"), 1)
            for n in range(TILES):
                last = nc.vector.scalar_tensor_tensor(late_sum[:, n, :], over_all[:, n, :], late[:, n:n + 1], x_all[:, n, :], ALU.mult, ALU.add)
            last.then_inc(S("late_sum"), 1)
            for n in range(3):
                cols = min(4, blocks - 4 * n) * P
                dve.wait_ge(S("rows_t_ps"), n + 1)
                nc.vector.tensor_copy(rows_t[:, 512 * n:512 * n + cols], bank[5 + n][:, 0:cols]).then_inc(S("rows_t"), 1)
            for n in range(3):
                k = min(4, blocks - 4 * n)
                dve.wait_ge(S("y_rows_ps"), n + 1)
                nc.vector.tensor_copy(y_rows[:, 4 * n:4 * n + k, :].rearrange("p c d -> p (c d)"), bank[1 + n][:, 0:k * P]).then_inc(S("y_rows"), 1)
            dve.wait_ge(S("late_sum"), 1)
            dve.wait_ge(S("taken"), 16 * TILES)
            for t in range(STEPS):
                nc.vector.tensor_tensor(result[:, t * B:(t + 1) * B, :], late_sum[:, t * B:(t + 1) * B, :], taken[:, t * B:(t + 1) * B, :], ALU.add).then_inc(S("result"), 1)

        @block.scalar
        def _(act):
            for e in range(E):
                for c in range(4):
                    act.wait_ge(S("c_hidden_ps"), 4 * e + c + 1)
                    if e >= 2:
                        act.wait_ge(S("c_y_ps"), e - 1)
                    nc.scalar.activation(hidden[:, e % 2, c, :], bank[1 + c][:, 0:CAP], ACT.Relu, bias=const["b1"][:, e, c:c + 1]).then_inc(S("c_hidden"), 1)
                act.wait_ge(S("c_y_ps"), e + 1)
                nc.scalar.activation(y_t[:, e * CAP:(e + 1) * CAP], bank[5 + e % 2][:, 0:CAP], ACT.Identity, bias=const["e_b2"][:, e:e + 1]).then_inc(S("c_y"), 1)

        @block.tensor
        def _(pe):
            mm, tr = nc.tensor.matmul, nc.tensor.transpose
            eye = const["eye"]
            seen = onehot_all[:].rearrange("p n e -> p (n e)")
            mm(bank[0][:, 0:TILES * E], const["up_to"][:], seen, start=True, stop=True).then_inc(S("count_ps"), 1)
            mm(bank[1][:, 0:TILES * E], const["ones"][:], seen, start=True, stop=True).then_inc(S("count_ps"), 1)
            pe.wait_ge(S("rows"), 16)
            for c in range(blocks):
                last = tr(bank[5 + c // 4][:, c % 4 * P:(c % 4 + 1) * P], rows[:, c, :], eye[:])
                if c % 4 == 3 or c == blocks - 1:
                    last.then_inc(S("rows_t_ps"), 1)
            pe.wait_ge(S("rows_t"), 3)
            pe.wait_ge(S("place"), 1)
            for e in range(E):
                for c in range(4):
                    if e >= 1:
                        pe.wait_ge(S("c_hidden"), 4 * (e - 1) + c + 1)
                    mm(bank[1 + c][:, 0:CAP], w["w1"][:, e, c * P:(c + 1) * P], rows_t[:, e * CAP:(e + 1) * CAP], start=True, stop=True).then_inc(S("c_hidden_ps"), 1)
                if e >= 2:
                    pe.wait_ge(S("c_y"), e - 1)
                for c in range(4):
                    pe.wait_ge(S("c_hidden"), 4 * e + c + 1)
                    last = mm(bank[5 + e % 2][:, 0:CAP], w["w2"][:, e, c, :], hidden[:, e % 2, c, :], start=c == 0, stop=c == 3)
                last.then_inc(S("c_y_ps"), 1)
            pe.wait_ge(S("c_y"), E)
            for c in range(blocks):
                last = tr(bank[1 + c // 4][:, c % 4 * P:(c % 4 + 1) * P], y_t[:, c * P:(c + 1) * P], eye[:])
                if c % 4 == 3 or c == blocks - 1:
                    last.then_inc(S("y_rows_ps"), 1)


def build(nc, a, out):
    with ExitStack() as ctx:
        def sb(name, shape, dt=F32):
            return ctx.enter_context(nc.sbuf_tensor(name, shape, dt))

        signal = named_signals(nc, ctx)
        psum = [ctx.enter_context(nc.psum_tensor(f"bank{i}", [P, 512], F32)) for i in range(8)]
        x_all = sb("x_all", [P, TILES, D])
        loads = []
        const, w = {}, {}

        first_ctx = ctx.enter_context(ExitStack())

        def load(where, name, shape, src, dt=F32, within=ctx):
            where[name] = within.enter_context(nc.sbuf_tensor(name + "_sb", shape, dt))
            loads.append((where[name][:], src))

        def row(ap, n):
            return ap.partition_broadcast(P)

        for name in ("eye", "after", "up_to", "own_head", "q_scale", "ones", "minus_half"):
            load(const, name, list(a[name].shape), a[name])
        load(const, "merge_low", [P, P], a["merge_low"], I32)
        load(const, "merge", [P, len(LEVELS), P], a["merge"], I32)
        for name, src in (("ln1_g", "L0_attn_ln1_g"), ("ln1_b", "L0_attn_ln1_b"), ("b2", "L0_attn_b2")):
            load(const, name, [P, D], row(a[src], D))
        for name, src in (("rms_in_w", "L0_attn_rms_in_w"), ("ln2_g", "L0_attn_ln2_g"), ("ln2_b", "L0_attn_ln2_b"), ("o_norm_w", "o_norm_w2")):
            load(const, name, [P, 1], a[src].rearrange("(p a) -> p a", a=1))
        load(const, "dt_bias", [P, 2 * H], row(a["dt_bias8"], 2 * H))
        load(const, "a_log", [P, H], row(a["L0_attn_A_log"], H))
        load(const, "conv_w", [P, CHUNKS, TAPS], a["conv_w"].rearrange("(c p) i -> p c i", p=P))
        load(w, "w_qkv", [P, CHUNKS, P], a["w_qkv"].rearrange("d (c n) -> d c n", n=P))
        load(w, "w_gates", [P, GATES], a["w_gates"])
        load(w, "w_o", [P, 2, D], a["L0_attn_Wo"].rearrange("(c p) n -> p c n", p=P))
        load(w, "w_2", [P, D], a["L0_attn_W2"])
        const["neg_exp_a"] = sb("neg_exp_a", [P, H])
        exp_a = sb("exp_a", [P, H])
        x_loaded = signal("x_loaded")
        x_dram = a["L0_attn_x"].rearrange("b (t p) d -> t p b d", p=P)
        out_dram = out.rearrange("b (t p) d -> t p b d", p=P)
        with nc.Block() as block:
            @block.sync
            def _(sp):
                for n, (dst, src) in enumerate(loads):
                    sp.dma_start(dst, src).then_inc(x_loaded, 16)
                for t in range(STEPS):
                    sp.dma_start(x_all[:, t * B:(t + 1) * B, :], x_dram[t]).then_inc(x_loaded, 16)
                sp.wait_ge(x_loaded, 16 * (len(loads) + STEPS))

            @block.scalar
            def _(act):
                act.wait_ge(x_loaded, 16 * (len(loads) + STEPS))
                nc.scalar.activation(exp_a[:], const["a_log"][:], ACT.Exp).then_inc(signal("exp_a"), 1)

            @block.vector
            def _(dve):
                dve.wait_ge(signal("exp_a"), 1)
                nc.vector.tensor_scalar(const["neg_exp_a"][:], exp_a[:], -1.0, None, ALU.mult).then_inc(signal("neg_exp_a"), 1)
                dve.wait_ge(signal("neg_exp_a"), 1)

        delta_rule_layer(nc, ctx, x_all, const, w, x_loaded, 16 * (len(loads) + STEPS), psum)
        loads.clear()
        load(w, "gate_w", [P, E], a["L0_ffn_gate_w"])
        load(w, "gate_up", [P, NETS, 2 * F], a["gate_up"].rearrange("e d n -> d e n"))
        w["down"] = sb("down_sb", [P, CHUNKS_F, D])
        whole = (CHUNKS_F - 1) * P
        loads.append((w["down"][:, 0:CHUNKS_F - 1, :], a["down"][0:whole, :].rearrange("(c p) n -> p c n", p=P)))
        loads.append((w["down"][0:NETS * F - whole, CHUNKS_F - 1, :], a["down"][whole:, :]))
        load(w, "wq", [P, D], a["wq"])
        load(w, "wdown", [P, LATENT], a["L1_attn_Wdown"])
        load(w, "wup", [LATENT, 2 * D], a["wup"])
        load(w, "wout", [P, D], a["L1_attn_Wout"])
        load(w, "router_w", [P, E], a["L1_ffn_router_w"])
        load(w, "ow1", [P, FF], a["L1_ffn_ow1"])
        load(w, "ow2", [P, 4, D], a["L1_ffn_ow2"].rearrange("(c p) n -> p c n", p=P))
        for name, src, n in (("bq", "bq", D), ("bup", "bup", 2 * D), ("bout", "L1_attn_bout", D), ("router_b", "L1_ffn_router_b", E), ("ob2", "L1_ffn_ob2", D)):
            load(const, name, [P, n], row(a[src], n))
        load(const, "bdown", [LATENT, 1], a["L1_attn_bdown"].rearrange("(p a) -> p a", a=1))
        for name in ("cos", "sin", "expert_ids", "ob1", "b1", "e_b2"):
            load(const, name, list(a[name].shape), a[name])
        y_all = sb("y_all", [P, TILES, D])
        over_all = sb("over_all", [P, TILES, D])
        onehot_all = sb("onehot_all", [P, TILES, E])
        expert_all = sb("expert_all", [P, TILES])
        with nc.Block() as block:
            @block.sync
            def _(sp):
                for dst, src in loads:
                    sp.dma_start(dst, src).then_inc(signal("token_layers_loaded"), 16)
                sp.wait_ge(signal("token_layers_loaded"), 16 * len(loads))
        token_layers(nc, x_all, y_all, over_all, onehot_all, expert_all, const, w, psum)
        slots_in = nc.dram_tensor("slots_in", (E * CAP, D), F32, kind="Internal").ap()
        slots_out = nc.dram_tensor("slots_out", (E * CAP, D), F32, kind="Internal").ap()
        loads.clear()
        w["w1"] = sb("w1_sb", [P, E, FF])
        w["w2"] = sb("w2_sb", [P, E, 4, D])
        loads.append((w["w1"][:], a["L1_ffn_w1"].rearrange("e d n -> d e n")))
        for e in range(E):
            loads.append((w["w2"][:, e], a["L1_ffn_w2"][e].rearrange("(c p) n -> p c n", p=P)))
        with nc.Block() as block:
            @block.sync
            def _(sp):
                for dst, src in loads:
                    sp.dma_start(dst, src).then_inc(signal("experts_loaded"), 16)
                sp.wait_ge(signal("experts_loaded"), 16 * len(loads))
        capacity_layer(nc, x_all, y_all, over_all, onehot_all, expert_all, const, w, psum, slots_in, slots_out, out_dram)


def constants():
    i = np.arange(P)
    r, c = i[:, None], i[None, :]
    f = lambda m: np.ascontiguousarray(m.astype(np.float32))
    out = {
        "eye": f(r == c),
        "after": f(r > c),
        "up_to": f(r <= c),
        "own_head": f((i // KD)[:, None] == (np.arange(VALS) // VD)[None, :]),
        "q_scale": np.tile(np.repeat(np.float32([KD, 1]), H)[None], (P, 1)),
        "ones": np.ones((P, P), np.float32),
        "minus_half": np.full((P, 32), -0.5, np.float32),
    }

    inv_freq = (1.0 / 10000.0 ** (np.arange(0, HD, 2, dtype=np.float32) / np.float32(HD))).astype(np.float32)
    angle = np.arange(T, dtype=np.float32)[:, None] * inv_freq[None, :]
    for name, fn in (("cos", np.cos), ("sin", np.sin)):
        table = np.tile(fn(angle.astype(np.float64)).astype(np.float32), (1, HEADS))
        out[name] = np.ascontiguousarray(table.reshape(STEPS, P, D // 2).transpose(1, 0, 2))
    out["expert_ids"] = np.tile(np.arange(E, dtype=np.float32)[None], (P, 1))

    def merge(s):
        return ((r // (2 * s) == c // (2 * s)) & (r // s % 2 == 1) & (c // s % 2 == 0)).astype(np.int32)

    out["merge_low"] = merge(1)
    out["merge"] = np.ascontiguousarray(np.stack([merge(s).T for s in LEVELS], 1))
    return out


def kernel(**inputs):
    import concourse.bacc as bacc
    from concourse.bass_utils import run_bass_kernel_spmd

    arrays = {k: np.ascontiguousarray(v) for k, v in inputs.items()}
    arrays["w_qkv"] = np.concatenate([arrays.pop("L0_attn_Wq"), arrays.pop("L0_attn_Wk"), arrays.pop("L0_attn_Wv")], 1)
    arrays["w_gates"] = np.concatenate([arrays.pop("L0_attn_Wg"), arrays.pop("L0_attn_Wa"), arrays.pop("L0_attn_Wb")], 1)
    arrays["conv_w"] = np.concatenate([arrays.pop("L0_attn_conv_q_w"), arrays.pop("L0_attn_conv_k_w"), arrays.pop("L0_attn_conv_v_w")], 0)
    arrays["dt_bias8"] = np.concatenate([arrays.pop("L0_attn_dt_bias"), np.zeros(H, np.float32)])
    arrays["o_norm_w2"] = np.tile(arrays.pop("L0_attn_o_norm_w"), 2)
    pop = arrays.pop
    arrays["gate_up"] = np.concatenate([np.concatenate([pop("L0_ffn_exp_gate"), pop("L0_ffn_exp_up")], 2),
                                        np.concatenate([pop("L0_ffn_sh_gate"), pop("L0_ffn_sh_up")], 2)], 0)
    arrays["down"] = np.concatenate([pop("L0_ffn_exp_down").reshape(-1, D), pop("L0_ffn_sh_down").reshape(-1, D)], 0)
    halves = np.arange(D).reshape(HEADS, 2, HD // 2).transpose(1, 0, 2).ravel()
    of_kv = np.arange(2 * D).reshape(HEADS, 2, HD)
    k_order = of_kv[:, 0].ravel()[halves]
    v_order = of_kv[:, 1].T.ravel()
    kv_order = np.concatenate([k_order, v_order])
    arrays["wq"] = np.ascontiguousarray(pop("L1_attn_Wq")[:, halves])
    arrays["bq"] = pop("L1_attn_bq")[halves]
    arrays["wup"] = np.ascontiguousarray(pop("L1_attn_Wup")[:, kv_order])
    arrays["bup"] = pop("L1_attn_bup")[kv_order]
    arrays["ob1"] = np.ascontiguousarray(pop("L1_ffn_ob1").reshape(4, P).T)
    arrays["b1"] = np.ascontiguousarray(pop("L1_ffn_b1").reshape(E, 4, P).transpose(2, 0, 1))
    arrays["e_b2"] = np.ascontiguousarray(pop("L1_ffn_b2").T)
    arrays.update(constants())
    nc = bacc.Bacc("TRN2", target_bir_lowering=False, num_devices=1)
    aps = {k: nc.dram_tensor("in_" + k, v.shape, mybir.dt.from_np(v.dtype), kind="ExternalInput").ap() for k, v in arrays.items()}
    out = nc.dram_tensor("out_0", (B, T, D), F32, kind="ExternalOutput").ap()
    build(nc, aps, out)
    r = run_bass_kernel_spmd(nc, [{"in_" + k: v for k, v in arrays.items()}], core_ids=[0])
    return r.results[0]["out_0"]
```

```python
import numpy as np
import concourse.bass as bass
from concourse import mybir
from contextlib import ExitStack

F32 = mybir.dt.float32
I32 = mybir.dt.int32
U32 = mybir.dt.uint32
ALU = mybir.AluOpType
ACT = mybir.ActivationFunctionType
AX = mybir.AxisListType

B, T, D = 4, 1024, 128
P = 128
STEPS = T // P
TILES = B * STEPS
H, KD, VD, TAPS = 4, 32, 64, 4
KEYS, VALS = H * KD, H * VD
CHUNKS = (2 * KEYS + VALS) // P
GATES = VALS + 2 * H
LN_EPS, RMS_EPS = 1e-5, 1e-6
LOWEST_DECAY = -104.0
E, F, NETS = 8, 176, 10
CHUNKS_F = -(-NETS * F // P)
GROUPS = -(-CHUNKS_F // 4)
NETBANKS = 3
HEADS, HD, LATENT = 16, 8, 32
FF, CAP = 512, 160
Q = 32
LEVELS = (2, 4, 8, 16)


def spread(ap, axis, n):
    shape = list(ap.shape)
    return ap.unsqueeze(axis).to_broadcast(shape[:axis] + [n] + shape[axis:])


def named_signals(nc, ctx, layer=""):
    made = {}

    @ctx.callback
    def _():
        nc.clear_and_free_semaphores(list(made.values()))
        nc.all_engine_barrier()

    def signal(name):
        if name not in made:
            made[name] = nc.alloc_semaphore(layer + name)
        return made[name]

    return signal


def delta_rule_layer(nc, x_all, const, w, later_x_loaded, psum):
    with ExitStack() as ctx:
        def sb(name, shape, dt=F32):
            return ctx.enter_context(nc.sbuf_tensor(name, shape, dt))

        S = named_signals(nc, ctx)
        y0 = sb("y0", [P, B, D])
        y0_solved = sb("y0_solved", [P, B, D])
        y0_kept = sb("y0_kept", [P, B, D])
        z = sb("z", [P, B, D])
        z_affine = z
        h = sb("h", [P, B, D])
        z_scaled = h
        h_t = sb("h_t", [P, B, P])
        stats = sb("stats", [P, B, 6])
        mean_var = sb("mean_var", [P, B, 2])
        var_eps = sb("var_eps", [P, B])
        rstd = sb("rstd", [P, B])
        stats2 = sb("stats2", [P, B, 6])
        mean_var2 = sb("mean_var2", [P, B, 2])
        var_eps2 = sb("var_eps2", [P, B])
        rstd2 = sb("rstd2", [P, B])
        sum_sq = sb("sum_sq", [P, B])
        conv_in = sb("conv_in", [P, CHUNKS, B, TAPS - 1 + P])
        conv_acc = sb("conv_acc", [P, CHUNKS, B, P])
        tok = sb("tok", [P, B, 2 * KEYS + VALS])
        gate = sb("gate", [P, B, VALS])
        ab = sb("ab", [P, B, 2 * H])
        sm = sb("sm", [P, 16, B, H])
        qk_sq = sb("qk_sq", [P, B, 2 * KEYS])
        qk_var = sb("qk_var", [P, B, 2 * H])
        qk_rn = sb("qk_rn", [P, B, 2 * H])
        qk = sb("qk", [P, B, 2 * H, KD])
        beta_v = sb("beta_v", [P, B, H, VD])
        g_wide = sb("g_wide", [P, B, H, KD])
        g_masked = sb("g_masked", [P, B, H, P])
        small_exp = sb("small_exp", [P, 2 * B * H + B])
        decay = sb("decay", [P, B, H, P])
        q_dec = sb("q_dec", [P, B, H, KD])
        k_dec = sb("k_dec", [P, B, H, KD])
        k_end = sb("k_end", [P, B, H, KD])
        k_t = sb("k_t", [P, B, P])
        q_t = sb("q_t", [P, B, P])
        qd_t = sb("qd_t", [P, B, P])
        kd_t = sb("kd_t", [P, B, P])
        PAIRS = H * B
        HALF = PAIRS // 2
        a_mat = sb("a_mat", [P, PAIRS, P])
        a_diag = sb("a_diag", [P, PAIRS, P])
        inv = sb("inv", [P, PAIRS, P])
        inv_t = sb("inv_t", [P, PAIRS, P])
        inv_t_diag = sb("inv_t_diag", [P, PAIRS, Q])
        prod_diag = sb("prod_diag", [P, PAIRS, Q])
        prod = sb("prod", [P, PAIRS, 2 * Q])
        att_t = sb("att_t", [P, H, B, P])
        att = g_masked[:, :, :, :].rearrange("p b h n -> p h b n")
        rhs = sb("rhs", [P, B, H, VD])
        delta = sb("delta", [P, B, H, VD])
        state = sb("state_bd", [P, B, H * VD])
        update = sb("update", [P, B, H * VD])
        o_sq = sb("o_sq", [P, B, H, VD])
        o_var = sb("o_var", [P, B, H])
        o_rn = sb("o_rn", [P, B, H])
        o_norm = sb("o_norm", [P, B, H * VD])
        o_gated = o_sq[:].rearrange("p b h v -> p b (h v)")
        o_t = sb("o_t", [P, 2, B, P])
        x1 = sb("x1", [P, B, D])
        z2 = sb("z2", [P, B, D])
        z2_t = sb("z2_t", [P, B, P])
        pre_gelu = sb("pre_gelu", [P, B, D])
        x_plus = sb("x_plus", [P, B, D])
        post_gelu = z2

        bank = psum
        BETA, NEG_BETA, G, MAG, U, RELU, DEN, SER, SQ, Q0, Q1, EB, NBG = range(13)
        NL = len(LEVELS)
        quads = [slice(q * Q, (q + 1) * Q) for q in range(4)]
        halves = [slice(0, HALF), slice(HALF, PAIRS)]
        tile_of = lambda t, j: x_all[:, bass.ds(t * B + j, 1), :].rearrange("p a d -> p (a d)")

        block = ctx.enter_context(nc.Block())

        def wait_apart(engine, semaphore, value):
            engine.wait_ge(semaphore, value)
            engine.sem_inc(S("waited_apart"), 1)

        def all_steps(engine, body):
            body(0, None, None)
            body(1, 0, None)
            with engine.Fori(0, STEPS - 2) as t:
                body(t + 2, t + 1, t)
            body(None, STEPS - 1, STEPS - 2)
            body(None, None, STEPS - 1)

        def norm_stats(dve, src, tag, t, stats, mean_var, var_eps):
            for j in range(B):
                last = nc.vector.bn_stats(stats[:, j, :], src(j))
            last.then_inc(S(tag + "_stats"), 1)
            wait_apart(dve, S(tag + "_stats"), t + 1)
            for j in range(B):
                last = nc.vector.bn_aggr(mean_var[:, j, :], stats[:, j, :])
            last.then_inc(S(tag + "_aggr"), 1)
            dve.wait_ge(S(tag + "_aggr"), t + 1)
            nc.vector.tensor_scalar(var_eps[:], mean_var[:, :, 1], LN_EPS, None, ALU.add).then_inc(S(tag + "_var"), 1)

        def normalise(dve, dst, src, tag, t, mean_var, rstd):
            dve.wait_ge(S(tag + "_rstd"), t + 1)
            for j in range(B):
                last = nc.vector.tensor_scalar(dst[:, j, :], src(j), mean_var[:, j, 0:1], rstd[:, j:j + 1],
                                               ALU.subtract, ALU.mult)
            last.then_inc(S(tag), 1)

        def root(pool, dst, src, n, ready, done, t):
            inverse_root(nc, pool, S, const, dst, src, n, ready, done, t)

        @block.gpsimd
        def _(pool):
            nc.gpsimd.memset(conv_in[:, :, :, 0:TAPS - 1], 0.0).then_inc(S("halo"), 1)
            nc.gpsimd.memset(state[:], 0.0).then_inc(S("state"), 1)
            nc.gpsimd.memset(a_diag[:], 0.0).then_inc(S("zeroed"), 1)
            nc.gpsimd.memset(inv[:], 0.0).then_inc(S("zeroed"), 1)
            nc.gpsimd.memset(inv_t[:], 0.0).then_inc(S("zeroed"), 1)
            pool.wait_ge(S("zeroed"), 3)

            def clear_merged():
                for q in range(0, 4, 2):
                    nc.gpsimd.memset(inv[quads[q + 1], :, quads[q]], 0.0)
                    nc.gpsimd.memset(inv_t[quads[q], :, quads[q + 1]], 0.0)
                for q in range(2):
                    ins = nc.gpsimd.memset(inv_t[quads[q], :, 2 * Q:], 0.0)
                ins.then_inc(S("cleared"), 1)

            clear_merged()
            pool.wait_ge(S("cleared"), 1)

            def body(n, m, p):
                if n is not None:
                    root(pool, rstd[:], var_eps[:], B, "ln0_var", "ln0_rstd", n)
                if m is not None:
                    pool.wait_ge(S("neg_beta_decay"), m + 1)
                    eg = small_exp[:, 0:B * H].rearrange("p (b h) -> p b h", h=H)
                    eg_end = small_exp[:, B * H:2 * B * H].rearrange("p (b h) -> p b h", h=H)
                    for dst, src, scale, tag in ((q_dec, qk[:, :, 0:H, :], eg, "q_dec"),
                                                 (k_dec, qk[:, :, H:2 * H, :], sm[:, NBG], "k_dec"),
                                                 (k_end, qk[:, :, H:2 * H, :], eg_end, "k_end")):
                        nc.gpsimd.tensor_tensor(dst[:], src, spread(scale, 3, KD), ALU.mult).then_inc(S(tag), 1)
                if n is not None:
                    root(pool, rstd[:], var_eps[:], B, "ln1_var", "ln1_rstd", n)
                if p is not None:
                    root(pool, rstd2[:], var_eps2[:], B, "ln2_var", "ln2_rstd", p)
                if n is not None:
                    pool.wait_ge(S("ln1"), n + 1)
                    nc.gpsimd.tensor_tensor(z_scaled[:], z[:], spread(const["ln1_g"][:], 1, B), ALU.mult).then_inc(S("z_scaled"), 1)
                    pool.wait_ge(S("z_scaled"), n + 1)
                    nc.gpsimd.tensor_tensor(z_affine[:], z_scaled[:], spread(const["ln1_b"][:], 1, B), ALU.add).then_inc(S("z_affine"), 1)
                    root(pool, rstd[:], var_eps[:], B, "rms_var", "rms_rstd", n)
                if p is not None:
                    nc.gpsimd.tensor_tensor(x_plus[:], x1[:], x_all[:, bass.ds(p * B, B), :], ALU.add).then_inc(S("x_plus"), 1)
                if m is not None:
                    if p is not None:
                        pool.wait_ge(S("x1"), p + 1)
                        wait_apart(pool, S("y0_solved"), m + 1)
                    else:
                        pool.wait_ge(S("y0_solved"), 1)
                    nc.gpsimd.tensor_copy(y0_kept[:], y0_solved[:]).then_inc(S("y0_kept"), 1)
                if n is not None:
                    if m is not None:
                        pool.wait_ge(S("y0_kept"), m + 1)
                    wait_apart(pool, S("ln0"), n + 1)
                    nc.gpsimd.tensor_copy(y0_solved[:], y0[:]).then_inc(S("y0_solved"), 1)
                    wait_apart(pool, S("g"), n + 1)
                    nc.gpsimd.tensor_copy(g_wide[:], spread(sm[:, G], 3, KD)).then_inc(S("g_wide"), 1)
                    if m is not None:
                        pool.wait_ge(S("att_t"), H * (m + 1))
                    for j in range(B):
                        nc.gpsimd.tensor_tensor(g_masked[:, j], spread(const["after"][:], 1, H),
                                                spread(sm[:, G, j, :], 2, P), ALU.mult).then_inc(S("g_masked"), 1)
                    wait_apart(pool, S("conv_done"), n + 1)
                    nc.gpsimd.tensor_copy(conv_in[:, :, :, 0:TAPS - 1], conv_in[:, :, :, P:P + TAPS - 1]).then_inc(S("halo"), 1)
                    root(pool, qk_rn[:].rearrange("p b n -> p (b n)"), qk_var[:].rearrange("p b n -> p (b n)"), 2 * B * H, "qk_var", "qk_rn", n)
                    for j in range(B):
                        wait_apart(pool, S("decay_raw"), B * n + j + 1)
                        nc.gpsimd.affine_select(out=decay[:, j], in_=decay[:, j], compare_op=ALU.is_ge, fill=0.0, base=0,
                                                pattern=[[0, H], [-1, P]], channel_multiplier=1).then_inc(S("decay"), 1)
                if m is not None:
                    pool.wait_ge(S("y0_kept"), m + 1)
                    if n is not None:
                        pool.wait_ge(S("decay"), B * (n + 1))
                    wait_apart(pool, S("delta_ps"), 2 * (m + 1))
                    clear_merged()
                    pool.wait_ge(S("cleared"), m + 2)
                    root(pool, o_rn[:].rearrange("p b n -> p (b n)"), o_var[:].rearrange("p b n -> p (b n)"), B * H, "o_var", "o_rn", m)

            all_steps(pool, body)

        @block.scalar
        def _(act):
            def copy(dst, src, ready, done, t, k=1, i=0, **kw):
                act.wait_ge(S(ready), k * t + i + 1)
                nc.scalar.activation(dst, src, kw.pop("func", ACT.Copy), **kw).then_inc(S(done), 1)

            flat = lambda ap: ap.rearrange("p b n -> p (b n)")

            def blocks_of_one():
                for q in range(4):
                    ins = nc.scalar.activation(inv[quads[q], :, quads[q]], spread(const["eye"][quads[q], quads[q]], 1, PAIRS), ACT.Copy)
                ins.then_inc(S("ones"), 1)

            act.wait_ge(S("zeroed"), 3)
            blocks_of_one()

            def level(m, l):
                for a, half in enumerate(halves):
                    copy(flat(prod_diag[:, half]), bank[a][:, 0:HALF * Q], "prod_ps", "prod", m, 2 * NL, 2 * l + a)

            def body(n, m, p):
                if m is not None:
                    copy(flat(k_t[:]), bank[0][:], "feature_ps", "feature", m, 2, 0)
                    copy(flat(q_t[:]), bank[1][:], "feature_ps", "feature", m, 2, 1)
                    act.wait_ge(S("state"), m + 1)
                    copy(small_exp[:], bank[4][:, 0:2 * B * H + B], "small_ps", "small_exp", m, func=ACT.Exp)
                    for a, half in enumerate(halves):
                        act.wait_ge(S("a_mat"), H * m + (a + 1) * H // 2)
                        for q in range(4):
                            ins = nc.scalar.activation(a_diag[quads[q], half, quads[q]], a_mat[quads[q], half, quads[q]], ACT.Copy)
                        ins.then_inc(S("a_diag"), 1)
                if p is not None:
                    for a in range(2):
                        copy(flat(o_t[:, a]), bank[6 + a][:], "o_t_ps", "o_t", p, 2, a, scale=const["o_norm_w"][:])
                if m is not None:
                    for j in range(B):
                        copy(gate[:, j, :], bank[5 - j % 2][:, 0:VALS], "gates_ps", "gate", m, B, j, func=ACT.Silu)
                    level(m, 0)
                if p is not None:
                    copy(flat(z2_t[:]), bank[7][:], "z2_t_ps", "z2_t", p, func=ACT.Identity, scale=const["ln2_g"][:], bias=const["ln2_b"][:])
                if n is not None:
                    act.wait_ge(S("z_affine"), n + 1)
                    for j in range(B):
                        last = nc.scalar.activation(z_scaled[:, j, :], z_affine[:, j, :], ACT.Square, accum_out=sum_sq[:, j:j + 1])
                    last.then_inc(S("sum_sq"), 1)
                if m is not None:
                    level(m, 1)
                if n is not None:
                    copy(flat(h_t[:]), bank[4][:], "h_t_ps", "h_t", n, scale=const["rms_in_w"][:])
                if p is not None:
                    act.wait_ge(S("pre_gelu"), p + 1)
                    nc.scalar.activation(post_gelu[:], pre_gelu[:], ACT.Gelu).then_inc(S("post_gelu"), 1)
                if n is not None:
                    act.wait_ge(S("halo"), n + 1)
                    for c in range(CHUNKS):
                        copy(conv_in[:, c, :, TAPS - 1:], bank[5 - c % 2][:].rearrange("p (b n) -> p b n", b=B), "proj_ps", "conv_in", n, CHUNKS, c)
                if m is not None:
                    level(m, 2)
                    copy(flat(qd_t[:]), bank[6][:], "decayed_ps", "decayed", m, 2, 0)
                    copy(flat(kd_t[:]), bank[7][:], "decayed_ps", "decayed", m, 2, 1)
                    for hh in range(H):
                        copy(flat(att_t[:, hh]), bank[6 + hh % 2][:], "att_t_ps", "att_t", m, H, hh)
                    level(m, 3)
                if n is not None:
                    act.wait_ge(S("decay_in_mag"), n + 1)
                    nc.scalar.activation(sm[:, U], sm[:, MAG], ACT.Exp, scale=-1.0).then_inc(S("u"), 1)
                    nc.scalar.activation(sm[:, EB], ab[:, :, H:2 * H], ACT.Exp, scale=-1.0).then_inc(S("eb"), 1)
                if m is not None:
                    for a, half in enumerate(halves):
                        copy(flat(prod[:, half]), bank[a][:], "wide_ps", "wide", m, 4, a)
                if n is not None:
                    for c in range(CHUNKS):
                        act.wait_ge(S("conv_acc"), (TAPS - 1) * CHUNKS + TAPS * CHUNKS * n + c + 1)
                        nc.scalar.activation(conv_acc[:, c], conv_acc[:, c], ACT.Silu).then_inc(S("conv_act"), 1)
                    for j in (0, 1):
                        copy(tok[:, j], bank[4 + j % 2][:], "tok_ps", "tok", n, B, j)
                if m is not None:
                    for a, half in enumerate(halves):
                        copy(flat(prod[:, half]), bank[a][:], "wide_ps", "wide", m, 4, 2 + a)
                if n is not None:
                    for j in (2, 3):
                        copy(tok[:, j], bank[4 + j % 2][:], "tok_ps", "tok", n, B, j)
                    act.wait_ge(S("tok"), B * (n + 1))
                    nc.scalar.activation(qk_sq[:], tok[:, :, 0:2 * KEYS], ACT.Square).then_inc(S("qk_sq"), 1)
                    for j in range(B):
                        copy(decay[:, j], bank[4 + j % 2][:].rearrange("p (h n) -> p h n", h=H), "decay_ps", "decay_raw", n, B, j, func=ACT.Exp)
                if m is not None:
                    for a in range(2):
                        copy(delta[:, 2 * a:2 * a + 2].rearrange("p b h n -> p (b h n)"), bank[6 + a][:], "delta_ps", "delta", m, 2, a)
                    blocks_of_one()
                    for a in range(2):
                        copy(o_sq[:, 2 * a:2 * a + 2].rearrange("p b h n -> p (b h n)"), bank[6 + a][:], "o_ps", "o_sq", m, 2, a, func=ACT.Square)

            all_steps(act, body)

        @block.vector
        def _(dve):
            def conv_tap(n, i, chunks=range(CHUNKS)):
                if n is None:
                    return
                for c in chunks:
                    tap = const["conv_w"][:, c, i:i + 1]
                    src = conv_in[:, c, :, i:i + P]
                    if i == 0:
                        dve.wait_ge(S("conv_in"), CHUNKS * n + c + 1)
                        ins = nc.vector.tensor_scalar(conv_acc[:, c], src, tap, None, ALU.mult)
                    else:
                        dve.wait_ge(S("conv_acc"), TAPS * CHUNKS * n + CHUNKS * (i - 1) + c + 1)
                        ins = nc.vector.scalar_tensor_tensor(conv_acc[:, c], src, tap, conv_acc[:, c], ALU.mult, ALU.add)
                    ins.then_inc(S("conv_acc"), 1)

            def decay_inputs(n):
                dve.wait_ge(S("ab_ps"), n + 1)
                nc.vector.tensor_tensor(ab[:], bank[5][:, 0:2 * B * H].rearrange("p (b n) -> p b n", b=B), spread(const["dt_bias"][:], 1, B), ALU.add).then_inc(S("ab"), 1)
                dve.wait_ge(S("ab"), n + 1)
                nc.vector.scalar_tensor_tensor(sm[:, MAG], ab[:, :, 0:H], -1.0, ab[:, :, 0:H], ALU.mult, ALU.max).then_inc(S("decay_in_mag"), 1)
                nc.vector.tensor_scalar(sm[:, RELU], ab[:, :, 0:H], 0.0, None, ALU.max).then_inc(S("relu"), 1)

            def decay_and_beta(n):
                step = [0]
                SMALL = 14

                def chain(ins):
                    step[0] += 1
                    ins.then_inc(S("small_step"), 1)
                    dve.wait_ge(S("small_step"), SMALL * n + step[0])

                dve.wait_ge(S("eb"), n + 1)
                chain(nc.vector.tensor_scalar(sm[:, EB], sm[:, EB], 1.0, None, ALU.add))
                chain(nc.vector.reciprocal(sm[:, BETA], sm[:, EB]))
                chain(nc.vector.tensor_scalar(sm[:, DEN], sm[:, U], 2.0, None, ALU.add))
                chain(nc.vector.reciprocal(sm[:, DEN], sm[:, DEN]))
                chain(nc.vector.tensor_tensor(sm[:, SER], sm[:, U], sm[:, DEN], ALU.mult))
                chain(nc.vector.tensor_tensor(sm[:, SQ], sm[:, SER], sm[:, SER], ALU.mult))
                chain(nc.vector.tensor_scalar(sm[:, Q0], sm[:, SQ], 1.0 / 15, None, ALU.mult))
                for k in (13, 11, 9, 7, 5, 3):
                    chain(nc.vector.scalar_tensor_tensor(sm[:, Q0], sm[:, Q0], 1.0 / k, sm[:, SQ], ALU.add, ALU.mult))
                chain(nc.vector.scalar_tensor_tensor(sm[:, Q0], sm[:, Q0], 1.0, sm[:, SER], ALU.add, ALU.mult))
                assert step[0] == SMALL
                nc.vector.scalar_tensor_tensor(sm[:, Q1], sm[:, Q0], 2.0, sm[:, RELU], ALU.mult, ALU.add).then_inc(S("softplus"), 1)
                dve.wait_ge(S("softplus"), n + 1)
                nc.vector.tensor_tensor(sm[:, Q0], sm[:, Q1], spread(const["neg_exp_a"][:], 1, B), ALU.mult).then_inc(S("g_raw"), 1)
                dve.wait_ge(S("g_raw"), n + 1)
                nc.vector.tensor_scalar(sm[:, G], sm[:, Q0], LOWEST_DECAY, None, ALU.max).then_inc(S("g"), 1)
                nc.vector.tensor_scalar(sm[:, NEG_BETA], sm[:, BETA], -1.0, None, ALU.mult).then_inc(S("neg_beta"), 1)

            def form_a(m, heads):
                for hh in heads:
                    dve.wait_ge(S("kk_ps"), H * m + hh + 1)
                    if hh == 0:
                        dve.wait_ge(S("decay"), B * (m + 1))
                    for j in range(B):
                        ins = nc.vector.scalar_tensor_tensor(a_mat[:, hh * B + j, :], bank[2 + hh % 2][:, j * P:(j + 1) * P], sm[:, NEG_BETA, j, hh:hh + 1],
                                                             decay[:, j, hh, :], ALU.mult, ALU.mult)
                    ins.then_inc(S("a_mat"), 1)

            def mask_attention(m, heads):
                for hh in heads:
                    dve.wait_ge(S("qk_ps"), H * m + hh + 1)
                    nc.vector.tensor_tensor(att[:, hh], bank[hh % 2][:].rearrange("p (b n) -> p b n", b=B), decay[:, :, hh, :], ALU.mult).then_inc(S("att"), 1)

            def turn_diagonal(half, k):
                for q in range(4):
                    last = nc.vector.transpose(inv[quads[q], half, quads[q]], inv_t_diag[quads[q], half, :])
                last.then_inc(S("inv"), 1)

            def level(m, l, between=lambda a: None):
                for a, half in enumerate(halves):
                    wait_apart(dve, S("merged_ps"), 2 * NL * m + 2 * l + a + 1)
                    nc.vector.copy_predicated(inv_t_diag[:, half], spread(const["merge"][:, l, :], 1, HALF),
                                              bank[2 + a][:, 0:HALF * Q].rearrange("p (m n) -> p m n", n=Q)).then_inc(S("inv_t_diag"), 1)
                    dve.wait_ge(S("inv_t_diag"), 2 * NL * m + 2 * l + a + 1)
                    turn_diagonal(half, l)
                    between(a)

            def body(n, m, p):
                if isinstance(n, int) and n == 1:
                    dve.wait_ge(later_x_loaded, 16 * (STEPS - 1))
                if n is not None:
                    norm_stats(dve, lambda j: tile_of(n, j), "ln0", n, stats, mean_var, var_eps)
                if m is not None:
                    form_a(m, (0, 1))
                if p is not None:
                    dve.wait_ge(S("o_rn"), p + 1)
                    for a in range(2):
                        nc.vector.tensor_tensor(o_norm[:, 2 * a:2 * a + 2].rearrange("p b (h v) -> p (b h) v", h=H), bank[6 + a][:].rearrange("p (b v) -> p b v", v=VD),
                                                spread(o_rn[:, 2 * a:2 * a + 2].rearrange("p b h -> p (b h)"), 2, VD), ALU.mult).then_inc(S("o_norm"), 1)
                    dve.wait_ge(S("gate"), B * (p + 1))
                    dve.wait_ge(S("o_norm"), 2 * (p + 1))
                    nc.vector.tensor_tensor(o_gated, o_norm[:], gate[:], ALU.mult).then_inc(S("o_gated"), 1)
                if m is not None:
                    form_a(m, (2, 3))
                    dve.wait_ge(S("small_exp"), m + 1)
                    dve.wait_ge(S("neg_beta"), m + 1)
                    nc.vector.tensor_tensor(sm[:, NBG], sm[:, NEG_BETA], small_exp[:, 0:B * H].rearrange("p (b h) -> p b h", h=H), ALU.mult).then_inc(S("neg_beta_decay"), 1)
                if m is not None:
                    mask_attention(m, (0, 1))
                    dve.wait_ge(S("cleared"), m + 1)
                    dve.wait_ge(S("ones"), m + 1)
                    wait_apart(dve, S("a_mat"), H * (m + 1))
                    for q in range(4):
                        last = nc.vector.copy_predicated(inv[quads[q], :, quads[q]], spread(const["merge_low"][quads[q], quads[q]], 1, PAIRS), a_mat[quads[q], :, quads[q]])
                    last.then_inc(S("inv_first"), 1)
                    dve.wait_ge(S("inv_first"), m + 1)
                    for q in range(4):
                        last = nc.vector.transpose(inv_t_diag[quads[q], :, :], inv[quads[q], :, quads[q]])
                    last.then_inc(S("inv_t_first"), 1)
                    mask_attention(m, (2, 3))
                if n is not None:
                    if m is not None:
                        dve.wait_ge(S("y0_solved"), m + 1)
                    normalise(dve, y0, lambda j: tile_of(n, j), "ln0", n, mean_var, rstd)
                    dve.wait_ge(S("ln0"), n + 1)
                    norm_stats(dve, lambda j: y0[:, j, :], "ln1", n, stats, mean_var, var_eps)
                if p is not None:
                    dve.wait_ge(S("y0_kept"), p + 1)
                    dve.wait_ge(S("x1_ps"), p + 1)
                    nc.vector.tensor_tensor(x1[:].rearrange("p b n -> p (b n)"), bank[6][:], y0_kept[:].rearrange("p b n -> p (b n)"), ALU.add).then_inc(S("x1"), 1)
                    wait_apart(dve, S("x1"), p + 1)
                    norm_stats(dve, lambda j: x1[:, j, :], "ln2", p, stats2, mean_var2, var_eps2)
                if n is not None:
                    normalise(dve, z, lambda j: y0[:, j, :], "ln1", n, mean_var, rstd)
                if p is not None:
                    normalise(dve, z2, lambda j: x1[:, j, :], "ln2", p, mean_var2, rstd2)
                if m is not None:
                    level(m, 0)
                if n is not None:
                    dve.wait_ge(S("sum_sq"), n + 1)
                    nc.vector.tensor_scalar(var_eps[:], sum_sq[:], 1.0 / D, RMS_EPS, ALU.mult, ALU.add).then_inc(S("rms_var"), 1)
                    dve.wait_ge(S("rms_rstd"), n + 1)
                    for j in range(B):
                        last = nc.vector.tensor_scalar(h[:, j, :], z_affine[:, j, :], rstd[:, j:j + 1], None, ALU.mult)
                    last.then_inc(S("h"), 1)
                if m is not None:
                    level(m, 1)
                if p is not None:
                    dve.wait_ge(S("w2_ps"), p + 1)
                    nc.vector.tensor_tensor(pre_gelu[:], bank[6][:].rearrange("p (b n) -> p b n", b=B), spread(const["b2"][:], 1, B), ALU.add).then_inc(S("pre_gelu"), 1)
                if m is not None:
                    level(m, 2, lambda a: conv_tap(n, 0, (2 * a, 2 * a + 1)))
                else:
                    conv_tap(n, 0)
                if n is not None:
                    decay_inputs(n)
                if m is not None:

                    def place_blocks(a):
                        for q in range(4):
                            ins = nc.vector.tensor_copy(inv_t[quads[q], halves[a], quads[q]], inv_t_diag[quads[q], halves[a], :])
                        ins.then_inc(S("inv_t32"), 1)
                        conv_tap(n, 1, (2 * a, 2 * a + 1))

                    level(m, 3, place_blocks)
                else:
                    conv_tap(n, 1)
                if p is not None:
                    dve.wait_ge(S("post_gelu"), p + 1)
                    dve.wait_ge(S("x_plus"), p + 1)
                    nc.vector.tensor_tensor(x_all[:, bass.ds(p * B, B), :], post_gelu[:], x_plus[:], ALU.add).then_inc(S("x_after_delta"), 1)
                conv_tap(n, 2)
                if n is not None:
                    conv_tap(n, 3)
                    dve.wait_ge(S("conv_acc"), TAPS * CHUNKS * (n + 1))
                    dve.sem_inc(S("conv_done"), 1)
                if m is not None:
                    for a, half in enumerate(halves):
                        wait_apart(dve, S("joined_ps"), 4 * m + a + 1)
                        joined = bank[2 + a][:].rearrange("p (m s n) -> p m s n", s=2, n=Q)
                        for s_, q in enumerate((0, 2)):
                            ins = nc.vector.tensor_copy(inv_t[quads[q], half, quads[q + 1]], joined[quads[q], :, s_, :])
                        ins.then_inc(S("inv_t64"), 1)
                        dve.wait_ge(S("inv_t64"), 2 * m + a + 1)
                        for q in (0, 2):
                            ins = nc.vector.transpose(inv[quads[q + 1], half, quads[q]], inv_t[quads[q], half, quads[q + 1]])
                        ins.then_inc(S("inv64"), 1)
                if n is not None:
                    decay_and_beta(n)
                if m is not None:
                    for a, half in enumerate(halves):
                        wait_apart(dve, S("joined_ps"), 4 * m + 2 + a + 1)
                        nc.vector.tensor_copy(inv_t[0:2 * Q, half, 2 * Q:], bank[2 + a][0:2 * Q, :].rearrange("p (m n) -> p m n", n=2 * Q)).then_inc(S("inv_t128"), 1)
                    for a in range(2):
                        dve.wait_ge(S("k_state_ps"), 2 * m + a + 1)
                        nc.vector.tensor_tensor(rhs[:, 2 * a:2 * a + 2].rearrange("p b h n -> p (b h n)"), bank[6 + a][:],
                                                beta_v[:, 2 * a:2 * a + 2].rearrange("p b h n -> p (b h n)"), ALU.add).then_inc(S("rhs"), 1)
                if n is not None:
                    dve.wait_ge(S("qk_sq"), n + 1)
                    nc.vector.tensor_reduce(qk_var[:], qk_sq[:].rearrange("p b (n k) -> p b n k", k=KD), AX.X, ALU.add).then_inc(S("qk_sum"), 1)
                    dve.wait_ge(S("qk_sum"), n + 1)
                    nc.vector.scalar_tensor_tensor(qk_var[:], qk_var[:], RMS_EPS, spread(const["q_scale"][:], 1, B), ALU.add, ALU.mult).then_inc(S("qk_var"), 1)
                    nc.vector.tensor_tensor(beta_v[:].rearrange("p b h v -> p b (h v)").rearrange("p b (h v) -> p b h v", h=H), tok[:, :, 2 * KEYS:].rearrange("p b (h v) -> p b h v", h=H),
                                            spread(sm[:, BETA], 3, VD), ALU.mult).then_inc(S("beta_v"), 1)
                    dve.wait_ge(S("qk_rn"), n + 1)
                    nc.vector.tensor_tensor(qk[:], tok[:, :, 0:2 * KEYS].rearrange("p b (n k) -> p b n k", k=KD), spread(qk_rn[:], 3, KD), ALU.mult).then_inc(S("qk"), 1)
                if m is not None:
                    for a in range(2):
                        dve.wait_ge(S("update_ps"), 2 * m + a + 1)
                        nc.vector.tensor_tensor(update[:, 2 * a:2 * a + 2], bank[6 + a][:].rearrange("p (b n) -> p b n", b=2),
                                                spread(const["own_head"][:], 1, 2), ALU.mult).then_inc(S("update"), 1)
                    dve.wait_ge(S("update"), 2 * (m + 1))
                    dve.wait_ge(S("o_ps"), 2 * (m + 1))
                    for j in range(B):
                        ins = nc.vector.scalar_tensor_tensor(state[:, j], state[:, j], small_exp[:, 2 * B * H + j:2 * B * H + j + 1], update[:, j], ALU.mult, ALU.add)
                    ins.then_inc(S("state"), 1)
                    dve.wait_ge(S("o_sq"), 2 * (m + 1))
                    nc.vector.tensor_reduce(o_var[:], o_sq[:], AX.X, ALU.add).then_inc(S("o_sum"), 1)
                    dve.wait_ge(S("o_sum"), m + 1)
                    nc.vector.tensor_scalar(o_var[:], o_var[:], 1.0 / VD, RMS_EPS, ALU.mult, ALU.add).then_inc(S("o_var"), 1)

            all_steps(dve, body)

        @block.tensor
        def _(pe):
            mm, tr = nc.tensor.matmul, nc.tensor.transpose
            eye = const["eye"]

            def turn(dst, src, done):
                for j in range(B):
                    last = tr(dst[:, j * P:(j + 1) * P], src(j), eye[:])
                last.then_inc(S(done), 1)

            def keep_warm(dst, n=1):
                for _ in range(n):
                    mm(dst[:], eye[:], w["w_qkv"][:, 0:4, :].rearrange("p c n -> p (c n)"), start=True, stop=True)

            def level(m, l, between=None):
                for a, half in enumerate(halves):
                    if l == 0:
                        pe.wait_ge(S("inv_t_first"), m + 1)
                        pe.wait_ge(S("a_diag"), 2 * (m + 1))
                        pe.wait_ge(S("att"), H * (m + 1))
                    else:
                        pe.wait_ge(S("inv"), 2 * NL * m + 2 * (l - 1) + a + 1)
                    keep_warm(bank[a], 1 if l else 2)
                    for k in range(HALF):
                        last = mm(bank[a][:, k * Q:(k + 1) * Q], a_diag[:, half.start + k, :], inv_t_diag[:, half.start + k, :], start=True, stop=True)
                    last.then_inc(S("prod_ps"), 1)
                if between is not None:
                    between()
                for a, half in enumerate(halves):
                    pe.wait_ge(S("prod"), 2 * NL * m + 2 * l + a + 1)
                    keep_warm(bank[2 + a], 1 if l else 2)
                    for k in range(HALF):
                        last = mm(bank[2 + a][:, k * Q:(k + 1) * Q], inv[:, half.start + k, :], prod_diag[:, half.start + k, :], start=True, stop=True)
                    last.then_inc(S("merged_ps"), 1)

            def join(m, l):
                for a, half in enumerate(halves):
                    if l == 0:
                        pe.wait_ge(S("inv_t32"), 2 * m + a + 1)
                        pe.wait_ge(S("inv"), 2 * NL * m + 2 * (NL - 1) + a + 1)
                    else:
                        pe.wait_ge(S("inv64"), 2 * m + a + 1)
                    keep_warm(bank[a])
                    for k in range(HALF):
                        u = inv_t[:, half.start + k, :]
                        u = u.rearrange("p (s r n) -> p s r n", s=2, r=2)[:, :, 1, :] if l == 0 else u[:, 2 * Q:]
                        last = mm(bank[a][:, k * 2 * Q:(k + 1) * 2 * Q], a_mat[:, half.start + k, :], u, start=True, stop=True)
                    last.then_inc(S("wide_ps"), 1)
                for a, half in enumerate(halves):
                    pe.wait_ge(S("wide"), 4 * m + 2 * l + a + 1)
                    keep_warm(bank[2 + a])
                    for k in range(HALF):
                        last = mm(bank[2 + a][:, k * 2 * Q:(k + 1) * 2 * Q], inv[:, half.start + k, :], prod[:, half.start + k, :], start=True, stop=True)
                    last.then_inc(S("joined_ps"), 1)

            def body(n, m, p):
                def project_output():
                    pe.wait_ge(S("o_t"), 2 * (p + 1))
                    for j in range(B):
                        for a in range(2):
                            last = mm(bank[6][:, j * P:(j + 1) * P], o_t[:, a, j, :], w["w_o"][:, a, :], start=a == 0, stop=a == 1)
                    last.then_inc(S("x1_ps"), 1)

                def turn_tokens(js):
                    for j in js:
                        if j >= 2:
                            pe.wait_ge(S("tok"), B * n + j - 1)
                        for c in range(CHUNKS):
                            last = tr(bank[4 + j % 2][:, c * P:(c + 1) * P], conv_acc[:, c, j, :], eye[:])
                        last.then_inc(S("tok_ps"), 1)

                if m is not None:
                    pe.wait_ge(S("qk"), m + 1)
                    turn(bank[0], lambda j: qk[:, j, H:2 * H].rearrange("p h k -> p (h k)"), "feature_ps")
                    turn(bank[1], lambda j: qk[:, j, 0:H].rearrange("p h k -> p (h k)"), "feature_ps")
                    pe.wait_ge(S("feature"), 2 * m + 1)
                    for hh in range(H):
                        rows = slice(hh * KD, (hh + 1) * KD)
                        if hh >= 2:
                            pe.wait_ge(S("a_mat"), H * m + hh - 1)
                        for j in range(B):
                            last = mm(bank[2 + hh % 2][:, j * P:(j + 1) * P], k_t[rows, j, :], k_t[rows, j, :], start=True, stop=True, tile_position=(hh * KD, 0))
                        last.then_inc(S("kk_ps"), 1)
                    pe.wait_ge(S("feature"), 2 * (m + 1))
                    for hh in range(H):
                        rows = slice(hh * KD, (hh + 1) * KD)
                        if hh >= 2:
                            pe.wait_ge(S("att"), H * m + hh - 1)
                        for j in range(B):
                            last = mm(bank[hh % 2][:, j * P:(j + 1) * P], q_t[rows, j, :], k_t[rows, j, :], start=True, stop=True, tile_position=(hh * KD, 0))
                        last.then_inc(S("qk_ps"), 1)
                        if hh == 1 and p is not None:
                            pe.wait_ge(S("o_gated"), p + 1)
                            for a in range(2):
                                turn(bank[6 + a], lambda j: o_gated[:, j, a * P:(a + 1) * P], "o_t_ps")
                        if hh == H - 1:
                            for j in range(B):
                                if j == 0:
                                    pe.wait_ge(S("small_exp"), m + 1)
                                if j >= 2:
                                    pe.wait_ge(S("gate"), B * m + j - 1)
                                mm(bank[5 - j % 2][:, 0:VALS], h_t[:, j, :], w["w_gates"][:, 0:VALS], start=True, stop=True).then_inc(S("gates_ps"), 1)
                            if p is not None:
                                project_output()
                if p is not None and m is None:
                    pe.wait_ge(S("o_gated"), p + 1)
                    for a in range(2):
                        turn(bank[6 + a], lambda j: o_gated[:, j, a * P:(a + 1) * P], "o_t_ps")
                    project_output()
                if m is not None:
                    level(m, 0)
                if p is not None:
                    pe.wait_ge(S("ln2"), p + 1)
                    turn(bank[7], lambda j: z2[:, j, :], "z2_t_ps")

                def turn_h():
                    if n is not None:
                        pe.wait_ge(S("h"), n + 1)
                        if m is not None:
                            pe.wait_ge(S("gate"), B * (m + 1))
                        turn(bank[4], lambda j: h[:, j, :], "h_t_ps")

                if m is not None:
                    level(m, 1, turn_h)
                else:
                    turn_h()
                if p is not None:
                    pe.wait_ge(S("z2_t"), p + 1)
                    pe.wait_ge(S("x1"), p + 1)
                    for j in range(B):
                        last = mm(bank[6][:, j * P:(j + 1) * P], z2_t[:, j, :], w["w_2"][:], start=True, stop=True)
                    last.then_inc(S("w2_ps"), 1)
                if n is not None:
                    pe.wait_ge(S("h_t"), n + 1)
                    h_all = h_t[:].rearrange("p b n -> p (b n)")
                    for c in range(CHUNKS):
                        if c >= 2:
                            pe.wait_ge(S("conv_in"), CHUNKS * n + c - 1)
                        mm(bank[5 - c % 2][:], w["w_qkv"][:, c, :], h_all, start=True, stop=True).then_inc(S("proj_ps"), 1)
                    pe.wait_ge(S("conv_in"), CHUNKS * n + 3)
                    for j in range(B):
                        last = mm(bank[5][:, j * 2 * H:(j + 1) * 2 * H], h_t[:, j, :], w["w_gates"][:, VALS:GATES], start=True, stop=True)
                    last.then_inc(S("ab_ps"), 1)

                def turn_decayed():
                    if p is not None:
                        pe.wait_ge(S("pre_gelu"), p + 1)
                    pe.wait_ge(S("q_dec"), m + 1)
                    turn(bank[6], lambda j: q_dec[:, j].rearrange("p h k -> p (h k)"), "decayed_ps")
                    pe.wait_ge(S("k_dec"), m + 1)
                    turn(bank[7], lambda j: k_dec[:, j].rearrange("p h k -> p (h k)"), "decayed_ps")

                if m is not None:
                    level(m, 2)
                    turn_decayed()
                    pe.wait_ge(S("decayed"), 2 * (m + 1))
                    for hh in range(H):
                        if hh >= 2:
                            pe.wait_ge(S("att_t"), H * m + hh - 1)
                        turn(bank[6 + hh % 2], lambda j: att[:, hh, j, :], "att_t_ps")
                    level(m, 3)
                    pe.wait_ge(S("state"), m + 1)
                    pe.wait_ge(S("att_t"), H * (m + 1))
                    for a in range(2):
                        for jj in range(2):
                            j = 2 * a + jj
                            last = mm(bank[6 + a][:, jj * VALS:(jj + 1) * VALS], kd_t[:, j, :], state[:, j], start=True, stop=True)
                        last.then_inc(S("k_state_ps"), 1)
                    join(m, 0)
                if n is not None:
                    pe.wait_ge(S("conv_act"), CHUNKS * (n + 1))
                    pe.wait_ge(S("ab"), n + 1)
                    pe.wait_ge(S("conv_in"), CHUNKS * (n + 1))
                    turn_tokens((0, 1))
                if m is not None:
                    join(m, 1)
                if n is not None:
                    turn_tokens((2, 3))
                    for j in range(B):
                        pe.wait_ge(S("g_masked"), B * n + j + 1)
                        if j < 2:
                            pe.wait_ge(S("tok"), B * n + j + 3)
                        else:
                            pe.wait_ge(S("decay_raw"), B * n + j - 1)
                        mm(bank[4 + j % 2][:], const["up_to"][:], g_masked[:, j].rearrange("p h n -> p (h n)"), start=True, stop=True).then_inc(S("decay_ps"), 1)
                if m is not None:
                    pe.wait_ge(S("inv_t128"), 2 * (m + 1))
                    for a in range(2):
                        pe.wait_ge(S("rhs"), 2 * m + a + 1)
                        for jj in range(2):
                            for hh in range(H):
                                j = 2 * a + jj
                                c = (jj * H + hh) * VD
                                last = mm(bank[6 + a][:, c:c + VD], inv_t[:, hh * B + j, :], rhs[:, j, hh, :], start=True, stop=True)
                        last.then_inc(S("delta_ps"), 1)
                if n is not None:
                    pe.wait_ge(S("decay_raw"), B * n + 4)
                    pe.wait_ge(S("g_wide"), n + 1)
                    g_all = sm[:, G].rearrange("p b h -> p (b h)")
                    k = B * H
                    mm(bank[4][:, 0:k], const["up_to"][:], g_all, start=True, stop=True)
                    mm(bank[4][:, k:2 * k], const["after"][:], g_all, start=True, stop=True)
                    for j in range(B):
                        last = mm(bank[4][:, 2 * k + j:2 * k + j + 1], g_wide[:, j].rearrange("p h k -> p (h k)"), const["ones"][:, 0:1], start=True, stop=True)
                    last.then_inc(S("small_ps"), 1)
                if m is not None:
                    pe.wait_ge(S("k_end"), m + 1)
                    for a in range(2):
                        pe.wait_ge(S("delta"), 2 * m + a + 1)
                        for jj in range(2):
                            j = 2 * a + jj
                            last = mm(bank[6 + a][:, jj * VALS:(jj + 1) * VALS], k_end[:, j].rearrange("p h k -> p (h k)"),
                                      delta[:, j].rearrange("p h v -> p (h v)"), start=True, stop=True)
                        last.then_inc(S("update_ps"), 1)
                    for a in range(2):
                        pe.wait_ge(S("update"), 2 * m + a + 1)
                        for jj in range(2):
                            j = 2 * a + jj
                            c = jj * VALS
                            mm(bank[6 + a][:, c:c + VALS], qd_t[:, j, :], state[:, j], start=True, stop=False)
                            for hh in range(H):
                                last = mm(bank[6 + a][:, c + hh * VD:c + (hh + 1) * VD], att_t[:, hh, j, :], delta[:, j, hh, :], start=False, stop=hh == H - 1)
                        last.then_inc(S("o_ps"), 1)

            all_steps(pe, body)


def inverse_root(nc, pool, S, const, dst, src, n, ready, done, t):
    pool.wait_ge(S(ready), t + 1)
    nc.gpsimd.tensor_tensor(dst, src, const["minus_half"][:, 0:n], ALU.pow).then_inc(S(done), 1)


def token_layers(nc, x_all, y_all, over_all, onehot_all, expert_all, const, w, psum, nets_loaded, net_loads):
    with ExitStack() as ctx:
        def sb(name, shape, dt=F32):
            return ctx.enter_context(nc.sbuf_tensor(name, shape, dt))

        S = named_signals(nc, ctx, "tokens_")
        bank = psum
        y = sb("m_y", [P, B, D])
        y_t = sb("m_y_t", [P, B, P])
        stats = sb("m_stats", [P, B, 6])
        mean_var = sb("m_mean_var", [P, B, 2])
        var_eps = sb("m_var_eps", [P, B])
        rstd = sb("m_rstd", [P, B])
        logits = sb("m_logits", [P, B, E])
        top = sb("m_top", [P, B, E])
        top_at = sb("m_top_at", [P, B, E], U32)
        top_at_f = sb("m_top_at_f", [P, B, E])
        pick = sb("m_pick", [P, 3, B, E])
        shifted = sb("m_shifted", [P, B, E])
        exp_l = sb("m_exp_l", [P, B, E])
        kept = sb("m_kept", [P, B, E])
        kept_sum = sb("m_kept_sum", [P, B])
        kept_inv = sb("m_kept_inv", [P, B])
        weight = sb("m_weight", [P, B, E])
        act_gate = sb("m_act_gate", [P, NETBANKS, F])
        hidden = sb("m_hidden", [P, 2, NETS * F])
        hidden_t = sb("m_hidden_t", [P, 2, 4, P])
        z = sb("m_z", [P, B, D])
        z_t = sb("m_z_t", [P, B, P])
        latent = sb("m_latent", [LATENT, B * P])
        qk = sb("m_qk", [P, B, 2, 2, D // 2])
        v_new = sb("m_v_new", [P, B, HD, HEADS])
        v = sb("m_v", [P, B, HD, HEADS])
        by_cos = sb("m_by_cos", [P, B * 2, 2, D // 2])
        by_sin = sb("m_by_sin", [P, B * 2, 2, D // 2])
        turned = sb("m_turned", [P, B * 2, HEADS, HD])
        qk_prod = sb("m_qk_prod", [P, 2, HEADS, HEADS, HD])
        pv_prod = sb("m_pv_prod", [P, HEADS, HD, HEADS])
        score = sb("m_score", [P, B, HEADS, HEADS])
        score_max = sb("m_score_max", [P, B, HEADS])
        probs = sb("m_probs", [P, B, HEADS, HEADS])
        prob_sum = sb("m_prob_sum", [P, B, HEADS])
        prob_inv = sb("m_prob_inv", [P, B, HEADS])
        mixed = sb("m_mixed", [P, B, HEADS, HD])
        att_out = sb("m_att_out", [P, B, D])
        att_out_t = sb("m_att_out_t", [P, B, P])
        y3 = sb("m_y3", [P, B, D])
        y3_t = sb("m_y3_t", [P, B, P])
        over_h = sb("m_over_h", [P, 4, B * P])
        r_logits = sb("m_r_logits", [P, B, E])
        r_top = sb("m_r_top", [P, B, E])
        r_at = sb("m_r_at", [P, B, E], U32)

        block = ctx.enter_context(nc.Block())
        flat = lambda ap: ap.rearrange("p b n -> p (b n)")
        tiles = lambda t: bass.ds(t * B, B)
        tile_of = lambda t, j: x_all[:, bass.ds(t * B + j, 1), :].rearrange("p a d -> p (a d)")
        net_bank = lambda n: bank[1 + n % NETBANKS]

        def wait_apart(engine, semaphore, value):
            engine.wait_ge(semaphore, value)
            engine.sem_inc(S("waited_apart"), 1)

        def all_steps(engine, body):
            body(0, None, None, None)
            body(1, 0, None, None)
            body(2, 1, 0, None)
            with engine.Fori(2, STEPS - 1) as t:
                body(t + 1, t, t - 1, t - 2)
            body(None, STEPS - 1, STEPS - 2, STEPS - 3)
            body(None, None, STEPS - 1, STEPS - 2)
            body(None, None, None, STEPS - 1)

        def layernorm(dve, dst, src, tag, t):
            for j in range(B):
                last = nc.vector.bn_stats(stats[:, j, :], src(j))
            last.then_inc(S(tag + "_stats"), 1)
            wait_apart(dve, S(tag + "_stats"), t + 1)
            for j in range(B):
                last = nc.vector.bn_aggr(mean_var[:, j, :], stats[:, j, :])
            last.then_inc(S(tag + "_aggr"), 1)
            dve.wait_ge(S(tag + "_aggr"), t + 1)
            nc.vector.tensor_scalar(var_eps[:], mean_var[:, :, 1], LN_EPS, None, ALU.add).then_inc(S(tag + "_var"), 1)
            dve.wait_ge(S(tag + "_rstd"), t + 1)
            for j in range(B):
                last = nc.vector.tensor_scalar(dst[:, j, :], src(j), mean_var[:, j, 0:1], rstd[:, j:j + 1],
                                               ALU.subtract, ALU.mult)
            last.then_inc(S(tag), 1)

        @block.gpsimd
        def _(pool):
            def body(head, nets, scores, output):
                if scores is not None:
                    t = scores
                    inverse_root(nc, pool, S, const, rstd[:], var_eps[:], B, "ln4_var", "ln4_rstd", t)
                    pool.wait_ge(S("ln4"), t + 1)
                    nc.gpsimd.tensor_tensor(x_all[:, tiles(t), :], x_all[:, tiles(t), :], spread(const["bout"][:], 1, B), ALU.add).then_inc(S("x2_bias"), 1)
                if head is not None:
                    inverse_root(nc, pool, S, const, rstd[:], var_eps[:], B, "ln3_var", "ln3_rstd", head)
                if scores is not None:
                    pool.wait_ge(S("qkv"), 3 * (t + 1))
                    parts = qk[:].rearrange("p b q s n -> p (b q s) n")
                    nc.gpsimd.tensor_tensor(by_cos[:].rearrange("p b s n -> p (b s) n"), parts,
                                            const["cos"][:, bass.ds(t, 1), :].to_broadcast([P, B * 4, D // 2]), ALU.mult).then_inc(S("by_cos"), 1)
                    nc.gpsimd.tensor_tensor(by_sin[:].rearrange("p b s n -> p (b s) n"), parts,
                                            const["sin"][:, bass.ds(t, 1), :].to_broadcast([P, B * 4, D // 2]), ALU.mult).then_inc(S("by_sin"), 1)
                    pool.wait_ge(S("by_cos"), t + 1)
                    pool.wait_ge(S("by_sin"), t + 1)
                    quads = lambda ap: ap.rearrange("p b (h d) -> p b h d", h=HEADS)
                    nc.gpsimd.tensor_tensor(turned[:, :, :, 0:HD // 2], quads(by_cos[:, :, 0, :]), quads(by_sin[:, :, 1, :]), ALU.subtract).then_inc(S("turned"), 1)
                    nc.gpsimd.tensor_tensor(turned[:, :, :, HD // 2:], quads(by_sin[:, :, 0, :]), quads(by_cos[:, :, 1, :]), ALU.add).then_inc(S("turned"), 1)
                    pool.wait_ge(S("turned"), 2 * (t + 1))
                for j in range(B):
                    if scores is not None:
                        pool.wait_ge(S("score"), B * t + j + 1)
                        nc.gpsimd.tensor_tensor(qk_prod[:, j % 2], spread(turned[:, 2 * j], 2, HEADS), spread(turned[:, 2 * j + 1], 1, HEADS), ALU.mult).then_inc(S("qk_prod"), 1)
                    if j == 1 and output is not None:
                        inverse_root(nc, pool, S, const, rstd[:], var_eps[:], B, "ln5_var", "ln5_rstd", output)
                        wait_apart(pool, S("ln5"), output + 1)
                        nc.gpsimd.tensor_copy(y_all[:, tiles(output), :], y3[:]).then_inc(S("y_kept"), 1)
                if scores is not None:
                    if output is not None:
                        wait_apart(pool, S("mixed"), B * (output + 1))
                    nc.gpsimd.tensor_copy(v[:], v_new[:]).then_inc(S("v"), 1)

            all_steps(pool, body)

        @block.scalar
        def _(act):
            def turned_copy(dst, src, ready, done, t):
                act.wait_ge(S(ready), t + 1)
                nc.scalar.activation(flat(dst[:]), src[:], ACT.Copy).then_inc(S(done), 1)

            def body(head, nets, scores, output):
                for j in range(B + 1):
                    for e in range(NETS):
                        if j < B and nets is not None:
                            n = j * NETS + e
                            act.wait_ge(S("gate_up_ps"), B * NETS * nets + n + 1)
                            nc.scalar.activation(act_gate[:, n % NETBANKS], net_bank(n)[:, 0:F], ACT.Silu).then_inc(S("act_gate"), 1)
                        if scores is not None and (j, e) == (0, 3):
                            turned_copy(z_t, bank[0], "z_t_ps", "z_t", scores)
                        if scores is not None and (j, e) == (0, 7):
                            act.wait_ge(S("latent_ps"), scores + 1)
                            nc.scalar.activation(latent[:], bank[7][0:LATENT, :], ACT.Identity, bias=const["bdown"][:]).then_inc(S("latent"), 1)
                        if output is not None and (j, e) == (2, 2):
                            turned_copy(att_out_t, bank[7], "att_out_t_ps", "att_out_t", output)
                        if output is not None and (j, e) == (3, 3):
                            turned_copy(y3_t, bank[0], "y3_t_ps", "y3_t", output)
                    if j == B and head is not None:
                        turned_copy(y_t, bank[7], "y_t_ps", "y_t", head)
                    for g in range(GROUPS):
                        if j and nets is not None:
                            act.wait_ge(S("hidden_t_ps"), GROUPS * (B * nets + j - 1) + g + 1)
                            n_chunks = min(4, CHUNKS_F - 4 * g)
                            nc.scalar.activation(flat(hidden_t[:, g % 2, 0:n_chunks, :]), bank[4 + g % 2][:, 0:n_chunks * P], ACT.Copy).then_inc(S("hidden_t"), 1)
                        if j == B and output is not None:
                            act.wait_ge(S("over_h_ps"), 4 * output + g + 1)
                            nc.scalar.activation(over_h[:, g, :], bank[7 if g == 3 else 0][:], ACT.Relu, bias=const["ob1"][:, g:g + 1]).then_inc(S("over_h"), 1)
                if head is not None:
                    act.wait_ge(S("shifted"), head + 1)
                    nc.scalar.activation(exp_l[:], shifted[:], ACT.Exp).then_inc(S("exp_l"), 1)
                if scores is not None:
                    act.wait_ge(S("centred"), scores + 1)
                    nc.scalar.activation(probs[:], score[:], ACT.Exp, scale=float(HD) ** -0.5).then_inc(S("probs"), 1)

            all_steps(act, body)

        @block.vector
        def _(dve):
            def route(t):
                dve.wait_ge(S("logits_ps"), t + 1)
                nc.vector.tensor_copy(logits[:].rearrange("p b e -> p (b e)"), bank[7][:, 0:B * E]).then_inc(S("logits"), 1)
                wait_apart(dve, S("logits"), t + 1)
                for j in range(B):
                    last = nc.vector.max(top[:, j, :], logits[:, j, :])
                last.then_inc(S("top"), 1)
                wait_apart(dve, S("top"), t + 1)
                nc.vector.tensor_tensor(shifted[:], logits[:], spread(top[:, :, 0], 2, E), ALU.subtract).then_inc(S("shifted"), 1)
                for j in range(B):
                    last = nc.vector.max_index(top_at[:, j, :], top[:, j, :], logits[:, j, :])
                last.then_inc(S("top_at"), 1)
                dve.wait_ge(S("top_at"), t + 1)
                nc.vector.tensor_copy(top_at_f[:], top_at[:]).then_inc(S("top_at_f"), 1)
                dve.wait_ge(S("top_at_f"), t + 1)
                for k in range(2):
                    last = nc.vector.tensor_tensor(pick[:, k], spread(const["expert_ids"][:], 1, B), spread(top_at_f[:, :, k], 2, E), ALU.is_equal)
                last.then_inc(S("pick"), 1)
                dve.wait_ge(S("pick"), t + 1)
                nc.vector.tensor_tensor(pick[:, 2], pick[:, 0], pick[:, 1], ALU.add).then_inc(S("picked"), 1)
                dve.wait_ge(S("picked"), t + 1)
                dve.wait_ge(S("exp_l"), t + 1)
                nc.vector.tensor_tensor(kept[:], pick[:, 2], exp_l[:], ALU.mult).then_inc(S("kept"), 1)
                dve.wait_ge(S("kept"), t + 1)
                nc.vector.tensor_reduce(kept_sum[:], kept[:], AX.X, ALU.add).then_inc(S("kept_sum"), 1)
                dve.wait_ge(S("kept_sum"), t + 1)
                nc.vector.reciprocal(kept_inv[:], kept_sum[:]).then_inc(S("kept_inv"), 1)
                dve.wait_ge(S("kept_inv"), t + 1)
                nc.vector.tensor_tensor(weight[:], kept[:], spread(kept_inv[:], 2, E), ALU.mult).then_inc(S("weight"), 1)
                dve.wait_ge(S("weight"), t + 1)

            def values_times_probs(t, j):
                if j == 0:
                    dve.wait_ge(S("probs"), t + 1)
                    dve.wait_ge(S("v"), t + 1)
                    nc.vector.tensor_reduce(prob_sum[:], probs[:], AX.X, ALU.add).then_inc(S("prob_sum"), 1)
                else:
                    dve.wait_ge(S("mixed"), B * t + j)
                nc.vector.tensor_tensor(pv_prod[:], spread(probs[:, j], 2, HD), spread(v[:, j], 1, HEADS), ALU.mult).then_inc(S("pv_prod"), 1)

            def mix(t, j):
                dve.wait_ge(S("pv_prod"), B * t + j + 1)
                nc.vector.tensor_reduce(mixed[:, j], pv_prod[:], AX.X, ALU.add).then_inc(S("mixed"), 1)
                if j == B - 1:
                    dve.wait_ge(S("prob_sum"), t + 1)
                    nc.vector.reciprocal(prob_inv[:], prob_sum[:]).then_inc(S("prob_inv"), 1)
                    dve.wait_ge(S("prob_inv"), t + 1)
                    dve.wait_ge(S("mixed"), B * (t + 1))
                    nc.vector.tensor_tensor(att_out[:].rearrange("p b (h d) -> p (b h) d", h=HEADS), mixed[:].rearrange("p b h d -> p (b h) d"),
                                            spread(prob_inv[:].rearrange("p b h -> p (b h)"), 2, HD), ALU.mult).then_inc(S("att_out"), 1)

            def add_q_bias(t):
                dve.wait_ge(S("q_ps"), t + 1)
                nc.vector.tensor_tensor(qk[:, :, 0].rearrange("p b s n -> p b (s n)"), bank[0][:].rearrange("p (b n) -> p b n", b=B),
                                        spread(const["bq"][:], 1, B), ALU.add).then_inc(S("qkv"), 1)

            def add_kv_bias(t):
                for n in range(2):
                    dve.wait_ge(S("kv_ps"), 2 * t + n + 1)
                    src = bank[0 if n else 7][:].rearrange("p (b n) -> p b n", b=2)
                    nc.vector.tensor_tensor(qk[:, 2 * n:2 * n + 2, 1].rearrange("p b s n -> p b (s n)"), src[:, :, 0:D], spread(const["bup"][:, 0:D], 1, 2), ALU.add)
                    nc.vector.tensor_tensor(v_new[:, 2 * n:2 * n + 2].rearrange("p b d h -> p b (d h)"), src[:, :, D:2 * D], spread(const["bup"][:, D:2 * D], 1, 2), ALU.add).then_inc(S("qkv"), 1)

            def sum_score(t, j):
                dve.wait_ge(S("qk_prod"), B * t + j + 1)
                nc.vector.tensor_reduce(score[:, j], qk_prod[:, j % 2], AX.X, ALU.add).then_inc(S("score"), 1)

            def centre(t):
                dve.wait_ge(S("score"), B * (t + 1) + 2)
                nc.vector.tensor_reduce(score_max[:], score[:], AX.X, ALU.max).then_inc(S("score_max"), 1)
                dve.wait_ge(S("score_max"), t + 1)
                merged = lambda ap: ap.rearrange("p b h g -> p (b h) g")
                nc.vector.tensor_tensor(merged(score[:]), merged(score[:]), spread(score_max[:].rearrange("p b h -> p (b h)"), 2, HEADS), ALU.subtract).then_inc(S("centred"), 1)

            def third_norm(t):
                dve.wait_ge(S("x2_bias"), t + 1)
                dve.wait_ge(S("wout_ps"), t + 1)
                nc.vector.tensor_tensor(x_all[:, tiles(t), :], bank[0][:].rearrange("p (b n) -> p b n", b=B), x_all[:, tiles(t), :], ALU.add).then_inc(S("x3"), 1)
                wait_apart(dve, S("x3"), t + 1)
                layernorm(dve, y3, lambda j: tile_of(t, j), "ln5", t)

            def choose(t):
                dve.wait_ge(S("r_logits_ps"), t + 1)
                nc.vector.tensor_tensor(r_logits[:], bank[7][:, 0:B * E].rearrange("p (b e) -> p b e", b=B), spread(const["router_b"][:], 1, B), ALU.add).then_inc(S("r_logits"), 1)
                wait_apart(dve, S("r_logits"), t + 1)
                for j in range(B):
                    last = nc.vector.max(r_top[:, j, :], r_logits[:, j, :])
                last.then_inc(S("r_top"), 1)
                wait_apart(dve, S("r_top"), t + 1)
                for j in range(B):
                    last = nc.vector.max_index(r_at[:, j, :], r_top[:, j, :], r_logits[:, j, :])
                last.then_inc(S("r_at"), 1)
                wait_apart(dve, S("r_at"), t + 1)
                nc.vector.tensor_copy(expert_all[:, tiles(t)], r_at[:, :, 0]).then_inc(S("expert"), 1)
                dve.wait_ge(S("expert"), t + 1)
                nc.vector.tensor_tensor(onehot_all[:, tiles(t), :], spread(const["expert_ids"][:], 1, B), spread(expert_all[:, tiles(t)], 2, E), ALU.is_equal).then_inc(S("onehot"), 1)

            def body(head, nets, scores, output):
                if scores is not None:
                    wait_apart(dve, S("x2"), scores + 1)
                    layernorm(dve, z, lambda j: tile_of(scores, j), "ln4", scores)
                for j in range(B + 1):
                    for e in range(NETS):
                        if nets is not None and j < B:
                            n = j * NETS + e
                            dve.wait_ge(S("act_gate"), B * NETS * nets + n + 1)
                            out = hidden[:, j % 2, e * F:(e + 1) * F]
                            up = net_bank(n)[:, F:2 * F]
                            if e < E:
                                ins = nc.vector.scalar_tensor_tensor(out, up, weight[:, j, e:e + 1], act_gate[:, n % NETBANKS], ALU.mult, ALU.mult)
                            else:
                                ins = nc.vector.tensor_tensor(out, up, act_gate[:, n % NETBANKS], ALU.mult)
                            ins.then_inc(S("hidden"), 1)
                        if output is not None and j < 2 and e in (1, 6):
                            values_times_probs(output, 2 * j + e // 5)
                        if output is not None and j < 2 and e in (3, 9):
                            mix(output, 2 * j + e // 5)
                        if scores is not None and (j, e) == (0, 8):
                            add_q_bias(scores)
                        if scores is not None and (j, e) == (1, 4):
                            add_kv_bias(scores)
                        if output is not None and (j, e) == (2, 5):
                            third_norm(output)
                        if scores is not None and (j, e) in ((2, 8), (3, 2), (3, 6)):
                            sum_score(scores, {8: 0, 2: 1, 6: 2}[e])
                        if output is not None and (j, e) == (3, 8):
                            choose(output)
                        if head is not None and (j, e) == (2, 1):
                            layernorm(dve, y, lambda j: tile_of(head, j), "ln3", head)
                if head is not None:
                    route(head)
                if nets is not None:
                    dve.wait_ge(S("mixture_ps"), B * (nets + 1))
                    nc.vector.tensor_tensor(x_all[:, tiles(nets), :], bank[6][:].rearrange("p (b n) -> p b n", b=B), x_all[:, tiles(nets), :], ALU.add).then_inc(S("x2"), 1)
                if scores is not None:
                    sum_score(scores, 3)
                    centre(scores)
                if output is not None:
                    dve.wait_ge(S("over_ps"), output + 1)
                    nc.vector.tensor_tensor(over_all[:, tiles(output), :], bank[0][:].rearrange("p (b n) -> p b n", b=B), spread(const["ob2"][:], 1, B), ALU.add).then_inc(S("over"), 1)

            dve.sem_inc(S("hidden"), NETBANKS)
            dve.sem_inc(S("score"), 2)
            all_steps(dve, body)

        @block.tensor
        def _(pe):
            mm, tr = nc.tensor.matmul, nc.tensor.transpose
            eye = const["eye"]

            def turn(dst, src, ready, done, t):
                pe.wait_ge(S(ready), t + 1)
                for j in range(B):
                    last = tr(dst[:, j * P:(j + 1) * P], src[:, j, :], eye[:])
                last.then_inc(S(done), 1)

            def times(dst, src_t, weights, width, ready, done, t):
                pe.wait_ge(S(ready), t + 1)
                for j in range(B):
                    last = mm(dst[:, j * width:(j + 1) * width], src_t[:, j, :], weights[:], start=True, stop=True)
                last.then_inc(S(done), 1)

            def keys_and_values(t):
                pe.wait_ge(S("latent"), t + 1)
                for n in range(2):
                    if n:
                        pe.wait_ge(S("qkv"), 3 * t + 1)
                    for jj in range(2):
                        j = 2 * n + jj
                        last = mm(bank[0 if n else 7][:, jj * 2 * D:(jj + 1) * 2 * D], latent[:, j * P:(j + 1) * P], w["wup"][:], start=True, stop=True)
                    last.then_inc(S("kv_ps"), 1)

            def overflow_hidden(t, c):
                mm(bank[7 if c == 3 else 0][:], w["ow1"][:, c * P:(c + 1) * P], flat(y3_t[:]), start=True, stop=True).then_inc(S("over_h_ps"), 1)

            def down(nets, i, g):
                pe.wait_ge(S("hidden_t"), GROUPS * (B * nets + i) + g + 1)
                for c in range(4 * g, min(4 * g + 4, CHUNKS_F)):
                    rows = min(P, NETS * F - c * P)
                    last = mm(bank[6][:, i * P:(i + 1) * P], hidden_t[0:rows, g % 2, c % 4, :], w["down"][0:rows, c, :], start=c == 0, stop=c == CHUNKS_F - 1)
                return last

            def body(head, nets, scores, output):
                if isinstance(nets, int) and nets == 0:
                    pe.wait_ge(nets_loaded, 16 * net_loads)
                for j in range(B + 1):
                    for e in range(NETS):
                        if nets is not None and j < B:
                            n = j * NETS + e
                            pe.wait_ge(S("hidden"), B * NETS * nets + n + 1)
                            mm(net_bank(n)[:, 0:2 * F], y_t[:, j, :], w["gate_up"][:, e, :], start=True, stop=True).then_inc(S("gate_up_ps"), 1)
                        if scores is not None and (j, e) == (0, 3):
                            turn(bank[0], z, "ln4", "z_t_ps", scores)
                        if scores is not None and (j, e) == (0, 6):
                            pe.wait_ge(S("z_t"), scores + 1)
                            mm(bank[7][0:LATENT, :], w["wdown"][:], flat(z_t[:]), start=True, stop=True).then_inc(S("latent_ps"), 1)
                            times(bank[0], z_t, w["wq"], D, "z_t", "q_ps", scores)
                        if scores is not None and (j, e) == (1, 2):
                            keys_and_values(scores)
                        if output is not None and (j, e) == (2, 1):
                            if scores is not None:
                                pe.wait_ge(S("qkv"), 3 * (scores + 1))
                            turn(bank[7], att_out, "att_out", "att_out_t_ps", output)
                        if output is not None and (j, e) == (2, 4):
                            times(bank[0], att_out_t, w["wout"], D, "att_out_t", "wout_ps", output)
                        if output is not None and (j, e) == (3, 2):
                            turn(bank[0], y3, "ln5", "y3_t_ps", output)
                        if output is not None and (j, e) == (3, 6):
                            times(bank[7], y3_t, w["router_w"], E, "y3_t", "r_logits_ps", output)
                        if output is not None and (j, e) == (3, 9):
                            overflow_hidden(output, 0)
                    if j == B and head is not None:
                        if output is not None:
                            pe.wait_ge(S("r_logits"), output + 1)
                        turn(bank[7], y, "ln3", "y_t_ps", head)
                    for g in range(GROUPS + 1):
                        if nets is not None and j:
                            if g == 0:
                                pe.wait_ge(S("hidden"), B * NETS * nets + NETS * j + NETBANKS)
                            if g < GROUPS:
                                for c in range(4 * g, min(4 * g + 4, CHUNKS_F)):
                                    cols = min(P, NETS * F - c * P)
                                    last = tr(bank[4 + g % 2][0:cols, c % 4 * P:(c % 4 + 1) * P], hidden[:, (j - 1) % 2, c * P:c * P + cols], eye[:])
                                last.then_inc(S("hidden_t_ps"), 1)
                            if g > 0:
                                last = down(nets, j - 1, g - 1)
                                if g == GROUPS:
                                    last.then_inc(S("mixture_ps"), 1)
                        if j == B and g == 1 and head is not None:
                            times(bank[7], y_t, w["gate_w"], E, "y_t", "logits_ps", head)
                        if j == B and output is not None and 1 <= g <= 3:
                            pe.wait_ge(S("over_h"), 4 * output + g - (g == 3))
                            if g == 3:
                                if head is not None:
                                    pe.wait_ge(S("logits"), head + 1)
                                else:
                                    pe.wait_ge(S("r_logits"), output + 1)
                            overflow_hidden(output, g)
                if output is not None:
                    pe.wait_ge(S("over_h"), 4 * (output + 1))
                    for j in range(B):
                        for c in range(4):
                            last = mm(bank[0][:, j * P:(j + 1) * P], over_h[:, c, j * P:(j + 1) * P], w["ow2"][:, c, :], start=c == 0, stop=c == 3)
                    last.then_inc(S("over_ps"), 1)

            all_steps(pe, body)


def capacity_layer(nc, x_all, y_all, over_all, onehot_all, expert_all, const, w, psum, slots_in, slots_out, out_dram, experts_loaded, expert_loads):
    with ExitStack() as ctx:
        def sb(name, shape, dt=F32):
            return ctx.enter_context(nc.sbuf_tensor(name, shape, dt))

        S = named_signals(nc, ctx, "capacity_")
        bank = psum
        n_slots = E * CAP
        blocks = n_slots // P
        zeros = sb("c_zeros", [P, n_slots // P, D])
        totals = sb("c_totals", [P, E, B, STEPS])
        running = sb("c_running", [P, E, B * STEPS])
        before = sb("c_before", [P, E, B, STEPS])
        place = sb("c_place", [P, STEPS, B, E])
        own = sb("c_own", [P, TILES, E])
        rank = sb("c_rank", [P, TILES])
        late = sb("c_late", [P, TILES])
        slot_f = sb("c_slot_f", [P, 2, TILES])
        slot = sb("c_slot", [P, TILES], U32)
        rows = sb("c_rows", [P, blocks, D])
        rows_t = sb("c_rows_t", [P, n_slots])
        hidden = sb("c_hidden", [P, 2, 4, CAP])
        y_t = sb("c_y_t", [P, n_slots])
        y_rows = sb("c_y_rows", [P, blocks, D])
        taken = sb("c_taken", [P, TILES, D])
        late_sum = sb("c_late_sum", [P, TILES, D])
        result = y_all
        block = ctx.enter_context(nc.Block())

        @block.sync
        def _(sp):
            sp.wait_ge(S("zeros"), 1)
            sp.dma_start(slots_in.rearrange("(c p) d -> p c d", p=P), zeros[:]).then_inc(S("slots_zeroed"), 16)
            sp.wait_ge(S("scattered"), 16 * TILES)
            sp.dma_start(rows[:], slots_in.rearrange("(c p) d -> p c d", p=P)).then_inc(S("rows"), 16)
            sp.wait_ge(S("y_rows"), 3)
            sp.dma_start(slots_out.rearrange("(c p) d -> p c d", p=P), y_rows[:]).then_inc(S("slots_done"), 16)
            for t in range(STEPS):
                sp.wait_ge(S("result"), t + 1)
                sp.dma_start(out_dram[t], result[:, t * B:(t + 1) * B, :]).then_inc(S("stored"), 16)
            sp.wait_ge(S("stored"), 16 * STEPS)

        @block.gpsimd
        def _(pool):
            nc.gpsimd.memset(zeros[:], 0.0).then_inc(S("zeros"), 1)
            nc.gpsimd.memset(taken[:], 0.0).then_inc(S("taken_zeroed"), 1)
            pool.wait_ge(S("slots_zeroed"), 16)
            pool.wait_ge(S("slot"), 1)
            for n in range(TILES):
                pool.indirect_dma_start(out=slots_in, out_offset=bass.IndirectOffsetOnAxis(slot[:, n:n + 1], 0), in_=y_all[:, n, :], in_offset=None,
                                        bounds_check=n_slots - 1, oob_is_err=False).then_inc(S("scattered"), 16)
            pool.wait_ge(S("slots_done"), 16)
            pool.wait_ge(S("taken_zeroed"), 1)
            for n in range(TILES):
                pool.indirect_dma_start(out=taken[:, n, :], out_offset=None, in_=slots_out, in_offset=bass.IndirectOffsetOnAxis(slot[:, n:n + 1], 0),
                                        bounds_check=n_slots - 1, oob_is_err=False).then_inc(S("taken"), 16)

        @block.vector
        def _(dve):
            counts = lambda ap: ap.rearrange("p (t b e) -> p t b e", t=STEPS, b=B)
            in_order = lambda ap: ap.rearrange("p e b t -> p t b e")
            dve.wait_ge(S("count_ps"), 2)
            for b in range(B):
                last = nc.vector.tensor_copy(totals[:, :, b, :].rearrange("p e t -> p t e"), counts(bank[1][:, 0:TILES * E])[:, :, b, :])
            last.then_inc(S("totals"), 1)
            dve.wait_ge(S("totals"), 1)
            for e in range(E):
                flat_e = totals[:, e].rearrange("p b t -> p (b t)")
                last = nc.vector.tensor_tensor_scan(running[:, e, :], const["ones"][:, 0:TILES], flat_e, 0.0, ALU.mult, ALU.add)
            last.then_inc(S("running"), 1)
            dve.wait_ge(S("running"), 1)
            nc.vector.tensor_tensor(before[:].rearrange("p e b t -> p (e b t)"), running[:].rearrange("p e n -> p (e n)"),
                                    totals[:].rearrange("p e b t -> p (e b t)"), ALU.subtract).then_inc(S("before"), 1)
            dve.wait_ge(S("before"), 1)
            nc.vector.tensor_tensor(place[:], counts(bank[0][:, 0:TILES * E]), in_order(before[:]), ALU.add).then_inc(S("place"), 1)
            dve.wait_ge(S("place"), 1)
            nc.vector.tensor_tensor(own[:], place[:].rearrange("p t b e -> p (t b) e"), onehot_all[:], ALU.mult).then_inc(S("own"), 1)
            dve.wait_ge(S("own"), 1)
            nc.vector.tensor_reduce(rank[:], own[:], AX.X, ALU.add).then_inc(S("rank"), 1)
            dve.wait_ge(S("rank"), 1)
            nc.vector.tensor_scalar(late[:], rank[:], float(CAP), None, ALU.is_gt).then_inc(S("late"), 1)
            nc.vector.scalar_tensor_tensor(slot_f[:, 0], expert_all[:], float(CAP), rank[:], ALU.mult, ALU.add).then_inc(S("slot_raw"), 1)
            dve.wait_ge(S("late"), 1)
            dve.wait_ge(S("slot_raw"), 1)
            nc.vector.scalar_tensor_tensor(slot_f[:, 1], late[:], float(4 * E * T), slot_f[:, 0], ALU.mult, ALU.add).then_inc(S("slot_f"), 1)
            dve.wait_ge(S("slot_f"), 1)
            nc.vector.tensor_scalar(slot[:], slot_f[:, 1], -1.0, None, ALU.add).then_inc(S("slot"), 1)
            for n in range(TILES):
                last = nc.vector.scalar_tensor_tensor(late_sum[:, n, :], over_all[:, n, :], late[:, n:n + 1], x_all[:, n, :], ALU.mult, ALU.add)
            last.then_inc(S("late_sum"), 1)
            for n in range(3):
                cols = min(4, blocks - 4 * n) * P
                dve.wait_ge(S("rows_t_ps"), n + 1)
                nc.vector.tensor_copy(rows_t[:, 512 * n:512 * n + cols], bank[5 + n][:, 0:cols]).then_inc(S("rows_t"), 1)
            for n in range(3):
                k = min(4, blocks - 4 * n)
                dve.wait_ge(S("y_rows_ps"), n + 1)
                nc.vector.tensor_copy(y_rows[:, 4 * n:4 * n + k, :].rearrange("p c d -> p (c d)"), bank[1 + n][:, 0:k * P]).then_inc(S("y_rows"), 1)
            dve.wait_ge(S("late_sum"), 1)
            dve.wait_ge(S("taken"), 16 * TILES)
            for t in range(STEPS):
                nc.vector.tensor_tensor(result[:, t * B:(t + 1) * B, :], late_sum[:, t * B:(t + 1) * B, :], taken[:, t * B:(t + 1) * B, :], ALU.add).then_inc(S("result"), 1)

        @block.scalar
        def _(act):
            for e in range(E):
                for c in range(4):
                    act.wait_ge(S("c_hidden_ps"), 4 * e + c + 1)
                    if e >= 2:
                        act.wait_ge(S("c_y_ps"), e - 1)
                    nc.scalar.activation(hidden[:, e % 2, c, :], bank[1 + c][:, 0:CAP], ACT.Relu, bias=const["b1"][:, e, c:c + 1]).then_inc(S("c_hidden"), 1)
                act.wait_ge(S("c_y_ps"), e + 1)
                nc.scalar.activation(y_t[:, e * CAP:(e + 1) * CAP], bank[5 + e % 2][:, 0:CAP], ACT.Identity, bias=const["e_b2"][:, e:e + 1]).then_inc(S("c_y"), 1)

        @block.tensor
        def _(pe):
            mm, tr = nc.tensor.matmul, nc.tensor.transpose
            eye = const["eye"]
            seen = onehot_all[:].rearrange("p n e -> p (n e)")
            mm(bank[0][:, 0:TILES * E], const["up_to"][:], seen, start=True, stop=True).then_inc(S("count_ps"), 1)
            mm(bank[1][:, 0:TILES * E], const["ones"][:], seen, start=True, stop=True).then_inc(S("count_ps"), 1)
            pe.wait_ge(S("rows"), 16)
            for c in range(blocks):
                last = tr(bank[5 + c // 4][:, c % 4 * P:(c % 4 + 1) * P], rows[:, c, :], eye[:])
                if c % 4 == 3 or c == blocks - 1:
                    last.then_inc(S("rows_t_ps"), 1)
            pe.wait_ge(S("rows_t"), 3)
            pe.wait_ge(S("place"), 1)
            pe.wait_ge(experts_loaded, 16 * expert_loads)
            for e in range(E):
                for c in range(4):
                    if e >= 1:
                        pe.wait_ge(S("c_hidden"), 4 * (e - 1) + c + 1)
                    mm(bank[1 + c][:, 0:CAP], w["w1"][:, e, c * P:(c + 1) * P], rows_t[:, e * CAP:(e + 1) * CAP], start=True, stop=True).then_inc(S("c_hidden_ps"), 1)
                if e >= 2:
                    pe.wait_ge(S("c_y"), e - 1)
                for c in range(4):
                    pe.wait_ge(S("c_hidden"), 4 * e + c + 1)
                    last = mm(bank[5 + e % 2][:, 0:CAP], w["w2"][:, e, c, :], hidden[:, e % 2, c, :], start=c == 0, stop=c == 3)
                last.then_inc(S("c_y_ps"), 1)
            pe.wait_ge(S("c_y"), E)
            for c in range(blocks):
                last = tr(bank[1 + c // 4][:, c % 4 * P:(c % 4 + 1) * P], y_t[:, c * P:(c + 1) * P], eye[:])
                if c % 4 == 3 or c == blocks - 1:
                    last.then_inc(S("y_rows_ps"), 1)


def build(nc, a, out):
    with ExitStack() as ctx:
        def sb(name, shape, dt=F32):
            return ctx.enter_context(nc.sbuf_tensor(name, shape, dt))

        signal = named_signals(nc, ctx)
        psum = [ctx.enter_context(nc.psum_tensor(f"bank{i}", [P, 512], F32)) for i in range(8)]
        x_all = sb("x_all", [P, TILES, D])
        loads = []
        const, w = {}, {}

        first_ctx = ctx.enter_context(ExitStack())

        def load(where, name, shape, src, dt=F32, within=ctx):
            where[name] = within.enter_context(nc.sbuf_tensor(name + "_sb", shape, dt))
            loads.append((where[name][:], src))

        def row(ap, n):
            return ap.partition_broadcast(P)

        for name in ("eye", "after", "up_to", "own_head", "q_scale", "ones", "minus_half"):
            load(const, name, list(a[name].shape), a[name])
        load(const, "merge_low", [P, P], a["merge_low"], I32)
        load(const, "merge", [P, len(LEVELS), Q], a["merge"], I32)
        for name, src in (("ln1_g", "L0_attn_ln1_g"), ("ln1_b", "L0_attn_ln1_b"), ("b2", "L0_attn_b2")):
            load(const, name, [P, D], row(a[src], D))
        for name, src in (("rms_in_w", "L0_attn_rms_in_w"), ("ln2_g", "L0_attn_ln2_g"), ("ln2_b", "L0_attn_ln2_b"), ("o_norm_w", "o_norm_w2")):
            load(const, name, [P, 1], a[src].rearrange("(p a) -> p a", a=1))
        load(const, "dt_bias", [P, 2 * H], row(a["dt_bias8"], 2 * H))
        load(const, "a_log", [P, H], row(a["L0_attn_A_log"], H))
        load(const, "conv_w", [P, CHUNKS, TAPS], a["conv_w"].rearrange("(c p) i -> p c i", p=P))
        load(w, "w_qkv", [P, CHUNKS, P], a["w_qkv"].rearrange("d (c n) -> d c n", n=P))
        load(w, "w_gates", [P, GATES], a["w_gates"])
        load(w, "w_o", [P, 2, D], a["L0_attn_Wo"].rearrange("(c p) n -> p c n", p=P))
        load(w, "w_2", [P, D], a["L0_attn_W2"])
        const["neg_exp_a"] = sb("neg_exp_a", [P, H])
        exp_a = sb("exp_a", [P, H])
        x_loaded = signal("x_loaded")
        later_x_loaded = signal("later_x_loaded")
        x_dram = a["L0_attn_x"].rearrange("b (t p) d -> t p b d", p=P)
        out_dram = out.rearrange("b (t p) d -> t p b d", p=P)
        with nc.Block() as block:
            @block.sync
            def _(sp):
                for n, (dst, src) in enumerate(loads):
                    sp.dma_start(dst, src).then_inc(x_loaded, 16)
                for t in range(STEPS):
                    sp.dma_start(x_all[:, t * B:(t + 1) * B, :], x_dram[t]).then_inc(later_x_loaded if t else x_loaded, 16)
                sp.wait_ge(x_loaded, 16 * (len(loads) + 1))

            @block.scalar
            def _(act):
                act.wait_ge(x_loaded, 16 * (len(loads) + 1))
                nc.scalar.activation(exp_a[:], const["a_log"][:], ACT.Exp).then_inc(signal("exp_a"), 1)

            @block.vector
            def _(dve):
                dve.wait_ge(signal("exp_a"), 1)
                nc.vector.tensor_scalar(const["neg_exp_a"][:], exp_a[:], -1.0, None, ALU.mult).then_inc(signal("neg_exp_a"), 1)
                dve.wait_ge(signal("neg_exp_a"), 1)

        delta_rule_layer(nc, x_all, const, w, later_x_loaded, psum)
        loads.clear()
        load(w, "gate_w", [P, E], a["L0_ffn_gate_w"])
        w["gate_up"] = sb("gate_up_sb", [P, NETS, 2 * F])
        w["down"] = sb("down_sb", [P, CHUNKS_F, D])
        whole = (CHUNKS_F - 1) * P
        nets_loaded = signal("nets_loaded")
        net_loads = [(w["gate_up"][:], a["gate_up"].rearrange("e d n -> d e n"))]
        net_loads.append((w["down"][:, 0:CHUNKS_F - 1, :], a["down"][0:whole, :].rearrange("(c p) n -> p c n", p=P)))
        net_loads.append((w["down"][0:NETS * F - whole, CHUNKS_F - 1, :], a["down"][whole:, :]))
        load(w, "wq", [P, D], a["wq"])
        load(w, "wdown", [P, LATENT], a["L1_attn_Wdown"])
        load(w, "wup", [LATENT, 2 * D], a["wup"])
        load(w, "wout", [P, D], a["L1_attn_Wout"])
        load(w, "router_w", [P, E], a["L1_ffn_router_w"])
        load(w, "ow1", [P, FF], a["L1_ffn_ow1"])
        load(w, "ow2", [P, 4, D], a["L1_ffn_ow2"].rearrange("(c p) n -> p c n", p=P))
        for name, src, n in (("bq", "bq", D), ("bup", "bup", 2 * D), ("bout", "L1_attn_bout", D), ("router_b", "L1_ffn_router_b", E), ("ob2", "L1_ffn_ob2", D)):
            load(const, name, [P, n], row(a[src], n))
        load(const, "bdown", [LATENT, 1], a["L1_attn_bdown"].rearrange("(p a) -> p a", a=1))
        for name in ("cos", "sin", "expert_ids", "ob1", "b1", "e_b2"):
            load(const, name, list(a[name].shape), a[name])
        y_all = sb("y_all", [P, TILES, D])
        over_all = sb("over_all", [P, TILES, D])
        onehot_all = sb("onehot_all", [P, TILES, E])
        expert_all = sb("expert_all", [P, TILES])
        with nc.Block() as block:
            @block.sync
            def _(sp):
                for dst, src in loads:
                    sp.dma_start(dst, src).then_inc(signal("token_layers_loaded"), 16)
                for dst, src in net_loads:
                    sp.dma_start(dst, src).then_inc(nets_loaded, 16)
                sp.wait_ge(signal("token_layers_loaded"), 16 * len(loads))
        token_layers(nc, x_all, y_all, over_all, onehot_all, expert_all, const, w, psum, nets_loaded, len(net_loads))
        slots_in = nc.dram_tensor("slots_in", (E * CAP, D), F32, kind="Internal").ap()
        slots_out = nc.dram_tensor("slots_out", (E * CAP, D), F32, kind="Internal").ap()
        loads.clear()
        w["w1"] = sb("w1_sb", [P, E, FF])
        w["w2"] = sb("w2_sb", [P, E, 4, D])
        loads.append((w["w1"][:], a["L1_ffn_w1"].rearrange("e d n -> d e n")))
        for e in range(E):
            loads.append((w["w2"][:, e], a["L1_ffn_w2"][e].rearrange("(c p) n -> p c n", p=P)))
        with nc.Block() as block:
            @block.sync
            def _(sp):
                for dst, src in loads:
                    sp.dma_start(dst, src).then_inc(signal("experts_loaded"), 16)
        capacity_layer(nc, x_all, y_all, over_all, onehot_all, expert_all, const, w, psum, slots_in, slots_out, out_dram, signal("experts_loaded"), len(loads))


def constants():
    i = np.arange(P)
    r, c = i[:, None], i[None, :]
    f = lambda m: np.ascontiguousarray(m.astype(np.float32))
    out = {
        "eye": f(r == c),
        "after": f(r > c),
        "up_to": f(r <= c),
        "own_head": f((i // KD)[:, None] == (np.arange(VALS) // VD)[None, :]),
        "q_scale": np.tile(np.repeat(np.float32([KD, 1]), H)[None], (P, 1)),
        "ones": np.ones((P, P), np.float32),
        "minus_half": np.full((P, 32), -0.5, np.float32),
    }

    inv_freq = (1.0 / 10000.0 ** (np.arange(0, HD, 2, dtype=np.float32) / np.float32(HD))).astype(np.float32)
    angle = np.arange(T, dtype=np.float32)[:, None] * inv_freq[None, :]
    for name, fn in (("cos", np.cos), ("sin", np.sin)):
        table = np.tile(fn(angle.astype(np.float64)).astype(np.float32), (1, HEADS))
        out[name] = np.ascontiguousarray(table.reshape(STEPS, P, D // 2).transpose(1, 0, 2))
    out["expert_ids"] = np.tile(np.arange(E, dtype=np.float32)[None], (P, 1))

    def merge(s):
        return ((r // (2 * s) == c // (2 * s)) & (r // s % 2 == 1) & (c // s % 2 == 0)).astype(np.int32)

    out["merge_low"] = merge(1)
    out["merge"] = np.ascontiguousarray(np.tile(np.stack([merge(s).T[:Q, :Q] for s in LEVELS], 1), (P // Q, 1, 1)))
    return out


def kernel(**inputs):
    import concourse.bacc as bacc
    from concourse.bass_utils import run_bass_kernel_spmd

    arrays = {k: np.ascontiguousarray(v) for k, v in inputs.items()}
    arrays["w_qkv"] = np.concatenate([arrays.pop("L0_attn_Wq"), arrays.pop("L0_attn_Wk"), arrays.pop("L0_attn_Wv")], 1)
    arrays["w_gates"] = np.concatenate([arrays.pop("L0_attn_Wg"), arrays.pop("L0_attn_Wa"), arrays.pop("L0_attn_Wb")], 1)
    arrays["conv_w"] = np.concatenate([arrays.pop("L0_attn_conv_q_w"), arrays.pop("L0_attn_conv_k_w"), arrays.pop("L0_attn_conv_v_w")], 0)
    arrays["dt_bias8"] = np.concatenate([arrays.pop("L0_attn_dt_bias"), np.zeros(H, np.float32)])
    arrays["o_norm_w2"] = np.tile(arrays.pop("L0_attn_o_norm_w"), 2)
    pop = arrays.pop
    arrays["gate_up"] = np.concatenate([np.concatenate([pop("L0_ffn_exp_gate"), pop("L0_ffn_exp_up")], 2),
                                        np.concatenate([pop("L0_ffn_sh_gate"), pop("L0_ffn_sh_up")], 2)], 0)
    arrays["down"] = np.concatenate([pop("L0_ffn_exp_down").reshape(-1, D), pop("L0_ffn_sh_down").reshape(-1, D)], 0)
    halves = np.arange(D).reshape(HEADS, 2, HD // 2).transpose(1, 0, 2).ravel()
    of_kv = np.arange(2 * D).reshape(HEADS, 2, HD)
    k_order = of_kv[:, 0].ravel()[halves]
    v_order = of_kv[:, 1].T.ravel()
    kv_order = np.concatenate([k_order, v_order])
    arrays["wq"] = np.ascontiguousarray(pop("L1_attn_Wq")[:, halves])
    arrays["bq"] = pop("L1_attn_bq")[halves]
    arrays["wup"] = np.ascontiguousarray(pop("L1_attn_Wup")[:, kv_order])
    arrays["bup"] = pop("L1_attn_bup")[kv_order]
    arrays["ob1"] = np.ascontiguousarray(pop("L1_ffn_ob1").reshape(4, P).T)
    arrays["b1"] = np.ascontiguousarray(pop("L1_ffn_b1").reshape(E, 4, P).transpose(2, 0, 1))
    arrays["e_b2"] = np.ascontiguousarray(pop("L1_ffn_b2").T)
    arrays.update(constants())
    nc = bacc.Bacc("TRN2", target_bir_lowering=False, num_devices=1)
    aps = {k: nc.dram_tensor("in_" + k, v.shape, mybir.dt.from_np(v.dtype), kind="ExternalInput").ap() for k, v in arrays.items()}
    out = nc.dram_tensor("out_0", (B, T, D), F32, kind="ExternalOutput").ap()
    build(nc, aps, out)
    r = run_bass_kernel_spmd(nc, [{"in_" + k: v for k, v in arrays.items()}], core_ids=[0])
    return r.results[0]["out_0"]
```
